# Optimizing a Trainium2 kernel written in Bass

```python
import numpy as np
import jax
import jax.numpy as jnp

def _softmax(x, axis=-1):
    return jax.nn.softmax(x, axis=axis)

def _gelu(x):
    return jax.nn.gelu(x, approximate=True)

def _silu(x):
    return jax.nn.silu(x)

def _sigmoid(x):
    return jax.nn.sigmoid(x)

def _layernorm(x, axis=-1, eps=1e-05):
    m = jnp.mean(x, axis=axis, keepdims=True)
    v = jnp.var(x, axis=axis, keepdims=True)
    return (x - m) / jnp.sqrt(v + eps)

def _scatter_add(tgt, idx, src, axis=0):
    return tgt.at[idx].add(src)

def _segment_sum(src, seg, n):
    return jax.ops.segment_sum(src, seg, n)
kernel_name = 'mk_gnn_preln_d4_gnn_r8_325fd7'

def setup_inputs(seed: int=0):
    np.random.seed(seed)
    _w = jnp.asarray

    def _rec_inputs():
        import jax
        import jax.numpy as jnp
        _gk = jax.random.key(seed)
        x = -0.0002928 + 1 * jax.random.normal(jax.random.fold_in(_gk, 1), (1024, 512), jnp.float32)
        _s = jax.random.randint(jax.random.fold_in(_gk, 2), (8192,), 0, 1024, jnp.int32)
        _d = jax.random.randint(jax.random.fold_in(_gk, 3), (8192,), 0, 1024, jnp.int32)
        _loop = jnp.arange(1024, dtype=jnp.int32)
        src = jnp.concatenate([_s, _d, _loop])
        dst = jnp.concatenate([_d, _s, _loop])
        _o = jnp.argsort(dst, stable=True)
        src = src[_o]
        dst = dst[_o]
        edge_attr_4 = 0.00171547 + 0.999346 * jax.random.normal(jax.random.fold_in(_gk, 12), (17408, 4), jnp.float32)
        edge_attr_8 = 0.000126197 + 0.999763 * jax.random.normal(jax.random.fold_in(_gk, 13), (17408, 8), jnp.float32)
        edge_type_8 = jax.random.randint(jax.random.fold_in(_gk, 15), (17408,), 0, 8, jnp.int32)
        edge_weight = jax.random.uniform(jax.random.fold_in(_gk, 16), (17408,), jnp.float32, 0.0, 0.999998)
        return (x, src, dst, edge_attr_4, edge_attr_8, edge_type_8, edge_weight)
    x, src, dst, edge_attr_4, edge_attr_8, edge_type_8, edge_weight = _rec_inputs()

    def _L0_gnn_setup():
        import jax, jax.numpy as jnp
        import numpy as np
        N_NODES = 1024
        N_EDGES = 32768
        D_IN = 512
        D_OUT = 512
        key = jax.random.key(seed)
        k1, k2, k3 = jax.random.split(key, 3)
        x = jax.random.normal(k1, (N_NODES, D_IN), dtype=jnp.float32)
        edge_index = jax.random.randint(k2, (2, N_EDGES), 0, N_NODES, dtype=jnp.int64)
        weight = jax.random.normal(k3, (D_IN, D_OUT), dtype=jnp.float32)
        bias = jnp.zeros((D_OUT,), dtype=jnp.float32)
        return {'x': x, 'edge_index': edge_index, 'weight': weight, 'bias': bias}
    _L0_gnn_all = _L0_gnn_setup()
    _L0_gnn_in = {k: v for k, v in _L0_gnn_all.items() if k in ('weight', 'bias')}
    del _L0_gnn_all

    def _L1_gnn_setup():
        import jax, jax.numpy as jnp
        import numpy as np
        MUL = 128
        N_NODES = 1250
        N_EDGES = 20000
        R_BASIS = 8
        HIDDEN = 64
        W_NUMEL = 4 * MUL
        SQRT3 = 3.0 ** 0.5
        SILU_2MOM = 1.679177
        AVG_NUM_NEIGHBORS = 10.0

        def _lin_irreps(x0, x1, W0, W1):
            y0 = x0 @ W0 / jnp.sqrt(jnp.float32(W0.shape[0]))
            y1 = jnp.einsum('num,uv->nvm', x1, W1) / jnp.sqrt(jnp.float32(W1.shape[0]))
            return (y0, y1)

        def _forward(node_feats, edge_attrs, edge_feats, edge_index, W_up0, W_up1, W_mlp1, W_mlp2, W_mlp3, W_mlp4, W_out0, W_out1):
            num_nodes = node_feats.shape[0]
            sender, receiver = (edge_index[0], edge_index[1])
            x0 = node_feats[:, :MUL]
            x1 = node_feats[:, MUL:].reshape(num_nodes, MUL, 3)
            x0, x1 = _lin_irreps(x0, x1, W_up0, W_up1)
            h = edge_feats
            for W in (W_mlp1, W_mlp2, W_mlp3):
                h = SILU_2MOM * jax.nn.silu(h @ W / jnp.sqrt(jnp.float32(W.shape[0])))
            tpw = h @ W_mlp4 / jnp.sqrt(jnp.float32(W_mlp4.shape[0]))
            w1, w2, w3, w4 = jnp.split(tpw, 4, axis=-1)
            s0 = x0[sender]
            s1 = x1[sender]
            y0 = edge_attrs[:, 0:1]
            y1 = edge_attrs[:, 1:4]
            p1 = w1 * s0 * y0
            p2 = (w2 * s0)[:, :, None] * y1[:, None, :]
            p3 = w3[:, :, None] * s1 * y0[:, None, :]
            p4 = w4 * jnp.einsum('eum,em->eu', s1, y1) / SQRT3
            m0 = jnp.concatenate([p1, p4], axis=-1)
            m1 = jnp.concatenate([p2, p3], axis=1)
            msg0 = jax.ops.segment_sum(m0, receiver, num_segments=num_nodes)
            msg1 = jax.ops.segment_sum(m1, receiver, num_segments=num_nodes)
            o0, o1 = _lin_irreps(msg0, msg1, W_out0, W_out1)
            out = jnp.concatenate([o0, o1.reshape(num_nodes, 3 * MUL)], axis=-1)
            return out / AVG_NUM_NEIGHBORS
        key = jax.random.key(seed)
        ks = jax.random.split(key, 12)
        rn = lambda k, s: jax.random.normal(k, s, dtype=jnp.float32)
        return {'node_feats': rn(ks[0], (N_NODES, 4 * MUL)), 'edge_attrs': rn(ks[1], (N_EDGES, 4)), 'edge_feats': rn(ks[2], (N_EDGES, R_BASIS)), 'edge_index': jax.random.randint(ks[3], (2, N_EDGES), 0, N_NODES), 'W_up0': rn(ks[4], (MUL, MUL)), 'W_up1': rn(ks[5], (MUL, MUL)), 'W_mlp1': rn(ks[6], (R_BASIS, HIDDEN)), 'W_mlp2': rn(ks[7], (HIDDEN, HIDDEN)), 'W_mlp3': rn(ks[8], (HIDDEN, HIDDEN)), 'W_mlp4': rn(ks[9], (HIDDEN, W_NUMEL)), 'W_out0': rn(ks[10], (2 * MUL, MUL)), 'W_out1': rn(ks[11], (2 * MUL, MUL))}
    _L1_gnn_all = _L1_gnn_setup()
    _L1_gnn_in = {k: v for k, v in _L1_gnn_all.items() if k in ('W_up0', 'W_up1', 'W_mlp1', 'W_mlp2', 'W_mlp3', 'W_mlp4', 'W_out0', 'W_out1')}
    del _L1_gnn_all

    def _L2_gnn_setup():
        import jax, jax.numpy as jnp
        import numpy as np
        N = 6250
        E = 20000
        D = 512
        H = 512
        NEG_SLOPE = 0.01

        def _cheb_norm(src, dst, n):
            deg = jax.ops.segment_sum(jnp.ones((src.shape[0],), jnp.float32), src, num_segments=n)
            dinv = jnp.where(deg > 0, jax.lax.rsqrt(jnp.maximum(deg, 1.0)), 0.0)
            return -dinv[src] * dinv[dst]

        def _cheb_conv(x, src, dst, norm, W0, W1, b):

            def prop(h):
                return jax.ops.segment_sum(h[src] * norm[:, None], dst, num_segments=x.shape[0])
            out = x @ W0
            tx1 = prop(x)
            out = out + tx1 @ W1
            return out + b

        def _layer_norm(x, gamma, beta, eps=1e-05):
            mu = jnp.mean(x, axis=-1, keepdims=True)
            var = jnp.mean(jnp.square(x - mu), axis=-1, keepdims=True)
            return (x - mu) * jax.lax.rsqrt(var + eps) * gamma + beta
        key = jax.random.key(seed)
        ks = jax.random.split(key, 8)
        s_in = 1.0 / np.sqrt(D)
        s_h = 1.0 / np.sqrt(H)
        x = jax.random.normal(ks[0], (N, D), jnp.float32)
        edge_index = jax.random.randint(ks[1], (2, E), 0, N, dtype=jnp.int64)
        return {'x': x, 'W1_0': jax.random.normal(ks[2], (D, H), jnp.float32) * s_in, 'W1_1': jax.random.normal(ks[3], (D, H), jnp.float32) * s_in, 'b1': jnp.zeros((H,), jnp.float32), 'gamma': jnp.ones((H,), jnp.float32), 'beta': jnp.zeros((H,), jnp.float32), 'W2_0': jax.random.normal(ks[4], (H, H), jnp.float32) * s_h, 'W2_1': jax.random.normal(ks[5], (H, H), jnp.float32) * s_h, 'b2': jnp.zeros((H,), jnp.float32), 'edge_index': edge_index}
    _L2_gnn_all = _L2_gnn_setup()
    _L2_gnn_in = {k: v for k, v in _L2_gnn_all.items() if k in ('W1_0', 'W1_1', 'b1', 'gamma', 'beta', 'W2_0', 'W2_1', 'b2')}
    del _L2_gnn_all

    def _L3_gnn_setup():
        import jax, jax.numpy as jnp
        import numpy as np
        N_NODES = 2500
        N_EDGES = 40000
        D = 512
        NUM_RELS = 8
        NUM_BASES = 4

        def _rel_graph_conv(h, src, dst, etypes, norm, basis, comp, bias, loop_w, apply_relu):
            n = h.shape[0]
            hb = jnp.einsum('nd,bdo->bno', h, basis)
            coef = comp[etypes]
            m = coef[:, 0, None] * hb[0][src]
            for b in range(1, basis.shape[0]):
                m = m + coef[:, b, None] * hb[b][src]
            m = m * norm[:, None]
            agg = jax.ops.segment_sum(m, dst, num_segments=n)
            out = agg + bias + h @ loop_w
            if apply_relu:
                out = jax.nn.relu(out)
            return out
        key = jax.random.key(seed)
        ks = jax.random.split(key, 16)
        inp = {'emb': jax.random.normal(ks[0], (N_NODES, D), dtype=jnp.float32), 'src': jax.random.randint(ks[1], (N_EDGES,), 0, N_NODES), 'dst': jax.random.randint(ks[2], (N_EDGES,), 0, N_NODES), 'etypes': jax.random.randint(ks[3], (N_EDGES,), 0, NUM_RELS), 'edge_norm': jax.random.uniform(ks[4], (N_EDGES,), dtype=jnp.float32)}
        s = 1.0 / np.sqrt(D)
        inp['basis0'] = jax.random.normal(ks[5], (NUM_BASES, D, D), dtype=jnp.float32) * s
        inp['comp0'] = jax.random.normal(ks[6], (NUM_RELS, NUM_BASES), dtype=jnp.float32)
        inp['bias0'] = jnp.zeros((D,), dtype=jnp.float32)
        inp['loop0'] = jax.random.normal(ks[7], (D, D), dtype=jnp.float32) * s
        inp['basis1'] = jax.random.normal(ks[8], (NUM_BASES, D, D), dtype=jnp.float32) * s
        inp['comp1'] = jax.random.normal(ks[9], (NUM_RELS, NUM_BASES), dtype=jnp.float32)
        inp['bias1'] = jnp.zeros((D,), dtype=jnp.float32)
        inp['loop1'] = jax.random.normal(ks[10], (D, D), dtype=jnp.float32) * s
        return inp
    _L3_gnn_all = _L3_gnn_setup()
    _L3_gnn_in = {k: v for k, v in _L3_gnn_all.items() if k in ('basis0', 'comp0', 'bias0', 'loop0', 'basis1', 'comp1', 'bias1', 'loop1')}
    del _L3_gnn_all
    return {'x': x, 'src': src, 'dst': dst, 'edge_attr_4': edge_attr_4, 'edge_attr_8': edge_attr_8, 'edge_type_8': edge_type_8, 'edge_weight': edge_weight, 'L0_gnn_weight': _L0_gnn_in['weight'], 'L0_gnn_bias': _L0_gnn_in['bias'], 'L1_gnn_W_up0': _L1_gnn_in['W_up0'], 'L1_gnn_W_up1': _L1_gnn_in['W_up1'], 'L1_gnn_W_mlp1': _L1_gnn_in['W_mlp1'], 'L1_gnn_W_mlp2': _L1_gnn_in['W_mlp2'], 'L1_gnn_W_mlp3': _L1_gnn_in['W_mlp3'], 'L1_gnn_W_mlp4': _L1_gnn_in['W_mlp4'], 'L1_gnn_W_out0': _L1_gnn_in['W_out0'], 'L1_gnn_W_out1': _L1_gnn_in['W_out1'], 'L2_gnn_W1_0': _L2_gnn_in['W1_0'], 'L2_gnn_W1_1': _L2_gnn_in['W1_1'], 'L2_gnn_b1': _L2_gnn_in['b1'], 'L2_gnn_gamma': _L2_gnn_in['gamma'], 'L2_gnn_beta': _L2_gnn_in['beta'], 'L2_gnn_W2_0': _L2_gnn_in['W2_0'], 'L2_gnn_W2_1': _L2_gnn_in['W2_1'], 'L2_gnn_b2': _L2_gnn_in['b2'], 'L3_gnn_basis0': _L3_gnn_in['basis0'], 'L3_gnn_comp0': _L3_gnn_in['comp0'], 'L3_gnn_bias0': _L3_gnn_in['bias0'], 'L3_gnn_loop0': _L3_gnn_in['loop0'], 'L3_gnn_basis1': _L3_gnn_in['basis1'], 'L3_gnn_comp1': _L3_gnn_in['comp1'], 'L3_gnn_bias1': _L3_gnn_in['bias1'], 'L3_gnn_loop1': _L3_gnn_in['loop1']}

def reference(x, src, dst, edge_attr_4, edge_attr_8, edge_type_8, edge_weight, L0_gnn_weight, L0_gnn_bias, L1_gnn_W_up0, L1_gnn_W_up1, L1_gnn_W_mlp1, L1_gnn_W_mlp2, L1_gnn_W_mlp3, L1_gnn_W_mlp4, L1_gnn_W_out0, L1_gnn_W_out1, L2_gnn_W1_0, L2_gnn_W1_1, L2_gnn_b1, L2_gnn_gamma, L2_gnn_beta, L2_gnn_W2_0, L2_gnn_W2_1, L2_gnn_b2, L3_gnn_basis0, L3_gnn_comp0, L3_gnn_bias0, L3_gnn_loop0, L3_gnn_basis1, L3_gnn_comp1, L3_gnn_bias1, L3_gnn_loop1):
    import jax
    import jax.numpy as jnp

    def _L0_gnn_ref(x, edge_index, weight, bias):
        import jax, jax.numpy as jnp
        import numpy as np
        N_NODES = 1024
        N_EDGES = 32768
        D_IN = 512
        D_OUT = 512
        n = x.shape[0]
        adj = jnp.zeros((n, n), dtype=x.dtype)
        adj = adj.at[edge_index[0], edge_index[1]].set(1.0)
        adj = adj.at[edge_index[1], edge_index[0]].set(1.0)
        adj = adj + jnp.eye(n, dtype=x.dtype)
        deg = jnp.sum(adj, axis=1)
        dinv = 1.0 / jnp.sqrt(deg)
        adj = adj * dinv[:, None] * dinv[None, :]
        return adj @ (x @ weight) + bias

    def _L1_gnn_ref(node_feats, edge_attrs, edge_feats, edge_index, W_up0, W_up1, W_mlp1, W_mlp2, W_mlp3, W_mlp4, W_out0, W_out1):
        import jax, jax.numpy as jnp
        import numpy as np
        MUL = 128
        N_NODES = 1250
        N_EDGES = 20000
        R_BASIS = 8
        HIDDEN = 64
        W_NUMEL = 4 * MUL
        SQRT3 = 3.0 ** 0.5
        SILU_2MOM = 1.679177
        AVG_NUM_NEIGHBORS = 10.0

        def _lin_irreps(x0, x1, W0, W1):
            y0 = x0 @ W0 / jnp.sqrt(jnp.float32(W0.shape[0]))
            y1 = jnp.einsum('num,uv->nvm', x1, W1) / jnp.sqrt(jnp.float32(W1.shape[0]))
            return (y0, y1)

        def _forward(node_feats, edge_attrs, edge_feats, edge_index, W_up0, W_up1, W_mlp1, W_mlp2, W_mlp3, W_mlp4, W_out0, W_out1):
            num_nodes = node_feats.shape[0]
            sender, receiver = (edge_index[0], edge_index[1])
            x0 = node_feats[:, :MUL]
            x1 = node_feats[:, MUL:].reshape(num_nodes, MUL, 3)
            x0, x1 = _lin_irreps(x0, x1, W_up0, W_up1)
            h = edge_feats
            for W in (W_mlp1, W_mlp2, W_mlp3):
                h = SILU_2MOM * jax.nn.silu(h @ W / jnp.sqrt(jnp.float32(W.shape[0])))
            tpw = h @ W_mlp4 / jnp.sqrt(jnp.float32(W_mlp4.shape[0]))
            w1, w2, w3, w4 = jnp.split(tpw, 4, axis=-1)
            s0 = x0[sender]
            s1 = x1[sender]
            y0 = edge_attrs[:, 0:1]
            y1 = edge_attrs[:, 1:4]
            p1 = w1 * s0 * y0
            p2 = (w2 * s0)[:, :, None] * y1[:, None, :]
            p3 = w3[:, :, None] * s1 * y0[:, None, :]
            p4 = w4 * jnp.einsum('eum,em->eu', s1, y1) / SQRT3
            m0 = jnp.concatenate([p1, p4], axis=-1)
            m1 = jnp.concatenate([p2, p3], axis=1)
            msg0 = jax.ops.segment_sum(m0, receiver, num_segments=num_nodes)
            msg1 = jax.ops.segment_sum(m1, receiver, num_segments=num_nodes)
            o0, o1 = _lin_irreps(msg0, msg1, W_out0, W_out1)
            out = jnp.concatenate([o0, o1.reshape(num_nodes, 3 * MUL)], axis=-1)
            return out / AVG_NUM_NEIGHBORS
        return _forward(node_feats, edge_attrs, edge_feats, edge_index, W_up0, W_up1, W_mlp1, W_mlp2, W_mlp3, W_mlp4, W_out0, W_out1)

    def _L2_gnn_ref(x, W1_0, W1_1, b1, gamma, beta, W2_0, W2_1, b2, edge_index):
        import jax, jax.numpy as jnp
        import numpy as np
        N = 6250
        E = 20000
        D = 512
        H = 512
        NEG_SLOPE = 0.01

        def _cheb_norm(src, dst, n):
            deg = jax.ops.segment_sum(jnp.ones((src.shape[0],), jnp.float32), src, num_segments=n)
            dinv = jnp.where(deg > 0, jax.lax.rsqrt(jnp.maximum(deg, 1.0)), 0.0)
            return -dinv[src] * dinv[dst]

        def _cheb_conv(x, src, dst, norm, W0, W1, b):

            def prop(h):
                return jax.ops.segment_sum(h[src] * norm[:, None], dst, num_segments=x.shape[0])
            out = x @ W0
            tx1 = prop(x)
            out = out + tx1 @ W1
            return out + b

        def _layer_norm(x, gamma, beta, eps=1e-05):
            mu = jnp.mean(x, axis=-1, keepdims=True)
            var = jnp.mean(jnp.square(x - mu), axis=-1, keepdims=True)
            return (x - mu) * jax.lax.rsqrt(var + eps) * gamma + beta
        src, dst = (edge_index[0], edge_index[1])
        norm = _cheb_norm(src, dst, x.shape[0])
        h = _cheb_conv(x, src, dst, norm, W1_0, W1_1, b1)
        h = _layer_norm(h, gamma, beta)
        h = jnp.where(h >= 0, h, NEG_SLOPE * h)
        out = _cheb_conv(h, src, dst, norm, W2_0, W2_1, b2)
        return out

    def _L3_gnn_ref(emb, src, dst, etypes, edge_norm, basis0, comp0, bias0, loop0, basis1, comp1, bias1, loop1):
        import jax, jax.numpy as jnp
        import numpy as np
        N_NODES = 2500
        N_EDGES = 40000
        D = 512
        NUM_RELS = 8
        NUM_BASES = 4

        def _rel_graph_conv(h, src, dst, etypes, norm, basis, comp, bias, loop_w, apply_relu):
            n = h.shape[0]
            hb = jnp.einsum('nd,bdo->bno', h, basis)
            coef = comp[etypes]
            m = coef[:, 0, None] * hb[0][src]
            for b in range(1, basis.shape[0]):
                m = m + coef[:, b, None] * hb[b][src]
            m = m * norm[:, None]
            agg = jax.ops.segment_sum(m, dst, num_segments=n)
            out = agg + bias + h @ loop_w
            if apply_relu:
                out = jax.nn.relu(out)
            return out
        h = _rel_graph_conv(emb, src, dst, etypes, edge_norm, basis0, comp0, bias0, loop0, True)
        h = _rel_graph_conv(h, src, dst, etypes, edge_norm, basis1, comp1, bias1, loop1, False)
        return h
    edge_index = jnp.stack([src, dst])
    h = jnp.maximum(_layernorm(x, axis=-1), 0.0)
    x = x + _L0_gnn_ref(h, edge_index, L0_gnn_weight, L0_gnn_bias)
    h = jnp.maximum(_layernorm(x, axis=-1), 0.0)
    x = x + _L1_gnn_ref(h, edge_attr_4, edge_attr_8, edge_index, L1_gnn_W_up0, L1_gnn_W_up1, L1_gnn_W_mlp1, L1_gnn_W_mlp2, L1_gnn_W_mlp3, L1_gnn_W_mlp4, L1_gnn_W_out0, L1_gnn_W_out1)
    h = jnp.maximum(_layernorm(x, axis=-1), 0.0)
    x = x + _L2_gnn_ref(h, L2_gnn_W1_0, L2_gnn_W1_1, L2_gnn_b1, L2_gnn_gamma, L2_gnn_beta, L2_gnn_W2_0, L2_gnn_W2_1, L2_gnn_b2, edge_index)
    h = jnp.maximum(_layernorm(x, axis=-1), 0.0)
    x = x + _L3_gnn_ref(h, src, dst, edge_type_8, edge_weight, L3_gnn_basis0, L3_gnn_comp0, L3_gnn_bias0, L3_gnn_loop0, L3_gnn_basis1, L3_gnn_comp1, L3_gnn_bias1, L3_gnn_loop1)
    return x

_drawn_inputs = setup_inputs


def setup_inputs(seed=0):
    import zlib

    import numpy as np

    out = dict(_drawn_inputs(seed))
    spreads = {'L0_gnn_bias': (0.0, 0.8),
     'L2_gnn_b1': (0.0, 0.8),
     'L2_gnn_gamma': (1.0, 0.6),
     'L2_gnn_beta': (0.0, 0.8),
     'L2_gnn_b2': (0.0, 0.8),
     'L3_gnn_bias0': (0.0, 0.334),
     'L3_gnn_bias1': (0.0, 0.8)}
    factors = {'L1_gnn_W_up0': 3.116,
     'L1_gnn_W_up1': 3.002,
     'L1_gnn_W_mlp1': 2.888,
     'L1_gnn_W_out0': 4.334}
    for name, (base, spread) in spreads.items():
        noise = np.random.default_rng([zlib.crc32(name.encode()), seed]).standard_normal(out[name].shape)
        drawn = base * np.exp(spread * noise) if base else spread * noise
        out[name] = jnp.asarray(drawn.astype(out[name].dtype))
    for name, factor in factors.items():
        out[name] = (out[name] * factor).astype(out[name].dtype)
    return out
```

```python
from contextlib import ExitStack

import concourse.bass as bass
from concourse import mybir

F32 = mybir.dt.float32
F32R = mybir.dt.float32r
F16 = mybir.dt.float16
BF16 = mybir.dt.bfloat16
I32 = mybir.dt.int32
ALU = mybir.AluOpType
ACT = mybir.ActivationFunctionType
AX = mybir.AxisListType

P = 128
EPS = 1e-5
SILU_2MOM = 1.679177
AVG_NEIGHBORS = 10.0
LEAK = 0.01


class Shapes:

    def __init__(self, x, src, edge_attr_8, mlp1, comp):
        self.N, self.D = x.shape
        self.E = src.shape[0]
        self.R8 = edge_attr_8.shape[1]
        self.HID = mlp1.shape[1]
        self.RELS, self.BASES = comp.shape
        self.BINS = self.N // P
        self.COLS = self.E // P
        self.PAIRS = -(-self.E // (2 * P)) + self.BINS
        self.TILES = 2 * self.PAIRS
        self.ROW = 8 + 2 * self.HID
        self.KT = self.D // P


class Shared:
    pass


def broadcast_rows(ap, n):
    return bass.AP(ap.tensor, 0, [[0, P], [1, n]])


def build_program(nc, a, out):
    z = Shapes(a["x"], a["src"], a["edge_attr_8"], a["L1_gnn_W_mlp1"], a["L3_gnn_comp0"])
    N, D, BINS, COLS, TILES, PAIRS, ROW, KT, HID = z.N, z.D, z.BINS, z.COLS, z.TILES, z.PAIRS, z.ROW, z.KT, z.HID
    assert D == 4 * P and HID == 64 and COLS % 8 == 0 and PAIRS % 4 == 0 and BINS == 8

    slots = nc.dram_tensor("edge_slots", [(TILES + 2) * P, ROW], F32).ap()
    up_table = nc.dram_tensor("up_table", [N, D], F32).ap()
    rel_table = [nc.dram_tensor(f"rel_table_{n}", [z.RELS * N, D], F32).ap() for n in range(2)]

    with ExitStack() as ctx:
        def sb(name, shape, dt=F32, c=ctx):
            return c.enter_context(nc.sbuf_tensor(name, shape, dt))

        def sem(name):
            return ctx.enter_context(nc.semaphore(name))

        ps = ctx.enter_context(nc.psum_tensor("ps", [P, 8, 512], F32))
        x = sb("x_rows", [P, BINS, D])
        h = sb("h_rows", [P, BINS, D])
        hT = sb("h_cols", [P, KT, N])
        by_src = sb("counts_by_src", [P, BINS, N])
        by_dst = sb("counts_by_dst", [P, BINS, N])
        weights = sb("weights", [P, 4, KT, D])
        meta = sb("slot_meta", [P, TILES, 8])
        ident = sb("ident", [P, P])
        iota1 = sb("iota1", [P, P])
        tile_bin = sb("tile_bin", [P, 80], I32)
        stats = sb("stats", [P, BINS, 6])
        moments = sb("moments", [P, BINS, 2])
        rstd = sb("rstd", [P, BINS])
        shift = sb("shift", [P, BINS])
        dinv_gcn = sb("dinv_gcn", [P, BINS])
        dinv_cheb = sb("dinv_cheb", [P, BINS])
        ndinv_cheb = sb("ndinv_cheb", [P, BINS])
        minus_half = sb("minus_half", [P, BINS])
        vec = sb("vec", [P, 1, D])

        x_in = sem("x_in")
        weights_in = [sem(f"weights_in{n}") for n in range(4)]
        consts = sem("consts")

        v = Shared()
        v.z = z
        v.N = N
        v.D = D
        v.BINS = BINS
        v.COLS = COLS
        v.TILES = TILES
        v.PAIRS = PAIRS
        v.ROW = ROW
        v.KT = KT
        v.HID = HID
        v.slots = slots
        v.up_table = up_table
        v.rel_table = rel_table
        v.ps = ps
        v.x = x
        v.h = h
        v.hT = hT
        v.by_src = by_src
        v.by_dst = by_dst
        v.weights = weights
        v.meta = meta
        v.ident = ident
        v.iota1 = iota1
        v.tile_bin = tile_bin
        v.stats = stats
        v.moments = moments
        v.rstd = rstd
        v.shift = shift
        v.dinv_gcn = dinv_gcn
        v.dinv_cheb = dinv_cheb
        v.ndinv_cheb = ndinv_cheb
        v.minus_half = minus_half
        v.vec = vec
        v.x_in = x_in
        v.weights_in = weights_in
        edges_block(nc, a, v)
        counts_block(nc, a, v)
        gcn_block(nc, a, v)
        tensor_product_block(nc, a, v)
        cheb_block(nc, a, v)
        relational_block(nc, a, v, out)


def edges_block(nc, a, v):
    z, N, BINS, COLS, TILES, PAIRS, ROW, HID = v.z, v.N, v.BINS, v.COLS, v.TILES, v.PAIRS, v.ROW, v.HID
    G = 4
    ITERS = COLS // (2 * G)
    with nc.cleanup_on_exit(), ExitStack() as c:
        def sb(name, shape, dt=F32):
            return c.enter_context(nc.sbuf_tensor(name, shape, dt))

        def sem(name):
            return nc.alloc_semaphore(name="edge_" + name)
        ps = v.ps
        dst_i, src_i, type_i, bin_i = (sb(n, [P, COLS], I32) for n in ("dst_i", "src_i", "type_i", "bin_i"))
        weight, dst_f, bin_f, pos = (sb(n, [P, COLS]) for n in ("weight", "dst_f", "bin_f", "pos"))
        y = sb("y", [P, COLS, 4])
        attr = sb("attr", [P, COLS, z.R8])
        edge_meta = sb("edge_meta", [P, COLS, 8])
        in_bin, no_carry, seen, place = (v.by_src[:, 2 * k:2 * k + 2, :].rearrange("p a n -> p (a n)")[:, 0:BINS * COLS]
                                         .rearrange("p (b j) -> p b j", j=COLS) for k in range(4))
        row_total, ones8, pairs_f, pair_end, offset = (sb(n, [P, BINS]) for n in ("row_total", "ones8", "pairs_f", "pair_end", "offset"))
        pairs_i = sb("pairs_i", [P, BINS], I32)
        lower = sb("lower", [P, P])
        ones = sb("ones", [P, P])
        pair_no = sb("pair_no", [P, PAIRS])
        passed = sb("passed", [P, PAIRS, BINS])
        bin_of = sb("bin_of", [P, PAIRS])
        zeros = sb("zeros", [P, 1024])
        w1 = sb("w1", [G * z.R8, 2, P])
        w2 = sb("w2", [P, P])
        w3 = sb("w3", [P, P])
        a8 = [sb(f"a8_{b}", [P, G * z.R8]) for b in range(2)]
        a8T = [sb(f"a8T_{b}", [G * z.R8, P]) for b in range(2)]
        h1, h2, h3 = ([sb(f"{n}_{b}", [P, 2 * P]) for b in range(2)] for n in ("h1", "h2", "h3"))
        payload = [sb(f"payload{b}", [P, G, ROW]) for b in range(2)]
        row_f = [sb(f"row_f{b}", [P, G], I32) for b in range(2)]
        row_i = [sb(f"row_i{b}", [P, G], I32) for b in range(2)]
        zero_g = sb("zero_g", [P, G], I32)

        dst_in, edges_in, blocks_zero, mlp_in = sem("dst_in"), sem("edges_in"), sem("blocks_zero"), sem("mlp_in")
        scattered = [sem(f"scattered{b}") for b in range(2)]
        zeros_set, slots_zeroed, index_step, totals_ready, pool_step = sem("zeros_set"), sem("slots_zeroed"), sem("index_step"), sem("totals_ready"), sem("pool_step")
        places_done, parts_done, staged, attr_turned, attr_cols = sem("places_done"), sem("parts_done"), sem("staged"), sem("attr_turned"), sem("attr_cols")
        pre_act, acted, hidden_turned, packed, rows_set = sem("pre_act"), sem("acted"), sem("hidden_turned"), sem("packed"), sem("rows_set")
        row_total_at = []
        zero_dmas = -(-(TILES + 2) * ROW // 2048)
        blk = c.enter_context(nc.Block())

        @blk.sync
        def _(sp):
            sp.dma_start(dst_i[:], a["dst"].rearrange("(p j) -> p j", p=P)).then_inc(dst_in, 16)
            sp.dma_start(attr[:], a["edge_attr_8"].rearrange("(p j) r -> p j r", p=P)).then_inc(edges_in, 16)
            sp.dma_start(src_i[:], a["src"].rearrange("(p j) -> p j", p=P)).then_inc(edges_in, 16)
            sp.dma_start(type_i[:], a["edge_type_8"].rearrange("(p j) -> p j", p=P)).then_inc(edges_in, 16)
            sp.dma_start(weight[:], a["edge_weight"].rearrange("(p j) -> p j", p=P)).then_inc(edges_in, 16)
            sp.dma_start(y[:], a["edge_attr_4"].rearrange("(p j) r -> p j r", p=P)).then_inc(edges_in, 16)
            sp.wait_ge(zeros_set, 1)
            flat = v.slots.rearrange("(p q) r -> p (q r)", p=P)
            per = flat.shape[1]
            half = per // 2
            for b in range(2):
                cuts = list(range(b * half, (b + 1) * half, 1024)) + [(b + 1) * half]
                assert per % 2 == 0
                for lo, hi in zip(cuts, cuts[1:]):
                    sp.dma_start(flat[:, lo:hi], zeros[:, 0:hi - lo]).then_inc(slots_zeroed, 16)
            sp.dma_start(v.x[:], a["x"].rearrange("(t p) d -> p t d", p=P)).then_inc(v.x_in, 16)
            sp.dma_start(v.weights[:, 0], a["L0_gnn_weight"].rearrange("(k p) n -> p k n", p=P)).then_inc(v.weights_in[0], 16)
            sp.dma_start(v.vec[:, 0, :], broadcast_rows(a["L0_gnn_bias"], v.D)).then_inc(v.weights_in[0], 16)
            for b in range(2):
                sp.wait_ge(scattered[b], 16 * G * ITERS)

        @blk.gpsimd
        def _(pool):
            pool.memset(zeros[:], 0.0).then_inc(zeros_set, 1)
            pool.memset(v.ident[:], 0.0).then_inc(pool_step, 1)
            pool.memset(ones[:], 1.0).then_inc(pool_step, 1)
            pool.memset(lower[:], 1.0).then_inc(pool_step, 1)
            pool.memset(no_carry, 1.0).then_inc(pool_step, 1)
            pool.memset(ones8[:], 1.0).then_inc(pool_step, 1)
            pool.memset(v.minus_half[:], -0.5).then_inc(pool_step, 1)
            pool.memset(zero_g[:], 0).then_inc(pool_step, 1)
            pool.wait_ge(pool_step, 7)
            pool.affine_select(out=v.ident[:], in_=v.ident[:], compare_op=ALU.not_equal, fill=1.0, base=0,
                               pattern=[[-1, P]], channel_multiplier=1).then_inc(pool_step, 1)
            pool.affine_select(out=lower[:], in_=lower[:], compare_op=ALU.is_gt, fill=0.0, base=0,
                               pattern=[[1, P]], channel_multiplier=-1).then_inc(pool_step, 1)
            pool.memset(no_carry[:, :, 0:1], 0.0).then_inc(pool_step, 1)
            pool.iota(v.iota1[:], pattern=[[1, P]], base=1, channel_multiplier=0,
                      allow_small_or_imprecise_dtypes=True).then_inc(pool_step, 1)
            pool.iota(pair_no[:], pattern=[[1, PAIRS]], base=0, channel_multiplier=0,
                      allow_small_or_imprecise_dtypes=True).then_inc(pool_step, 1)
            pool.memset(w1[:], 0.0).then_inc(blocks_zero, 1)
            pool.memset(w2[:], 0.0).then_inc(blocks_zero, 1)
            pool.memset(w3[:], 0.0).then_inc(blocks_zero, 1)
            pool.wait_ge(slots_zeroed, 2 * 16 * zero_dmas)
            with pool.Fori(0, ITERS) as i:
                for b in range(2):
                    pool.sem_clear(rows_set)
                    pool.wait_ge(packed, 4 * i + 2 * b + 2)
                    pool.tensor_tensor(row_i[b][:], row_f[b][:], zero_g[:], ALU.add).then_inc(rows_set, 1)
                    pool.wait_ge(rows_set, 1)
                    for k in range(G):
                        pool.indirect_dma_start(out=v.slots, out_offset=bass.IndirectOffsetOnAxis(ap=row_i[b][:, k:k + 1], axis=0),
                                                in_=payload[b][:, k, :], in_offset=None).then_inc(scattered[b], 16)

        @blk.vector
        def _(dve):
            steps = [0]

            def step(ins):
                steps[0] += 1
                ins.then_inc(index_step, 1)
                dve.wait_ge(index_step, steps[0])

            dve.wait_ge(dst_in, 16)
            dve.tensor_scalar(bin_i[:], dst_i[:], 7, None, ALU.arith_shift_right).then_inc(index_step, 1)
            dve.tensor_copy(dst_f[:], dst_i[:]).then_inc(index_step, 1)
            steps[0] += 2
            dve.wait_ge(index_step, steps[0])
            step(dve.tensor_copy(bin_f[:], bin_i[:]))
            for b in range(BINS):
                ins = dve.tensor_scalar(in_bin[:, b, :], bin_f[:], float(b), None, ALU.is_equal)
                ins.then_inc(index_step, 1)
                steps[0] += 1
            dve.wait_ge(index_step, steps[0])
            dve.wait_ge(pool_step, 12)
            step(dve.tensor_tensor_scan(seen.rearrange("p b j -> p (b j)"), no_carry.rearrange("p b j -> p (b j)"),
                                        in_bin.rearrange("p b j -> p (b j)"), 0.0, ALU.mult, ALU.add))
            dve.tensor_copy(row_total[:], seen[:, :, COLS - 1]).then_inc(index_step, 1)
            steps[0] += 1
            row_total_at.append(steps[0])
            dve.wait_ge(totals_ready, 1)
            step(dve.tensor_scalar(pairs_f[:], ps[:, 0, 8:16], float(2 * P - 1), None, ALU.add))
            step(dve.tensor_copy(pairs_i[:], pairs_f[:]))
            step(dve.tensor_scalar(pairs_i[:], pairs_i[:], 8, None, ALU.arith_shift_right))
            step(dve.tensor_copy(pairs_f[:], pairs_i[:]))
            step(dve.tensor_tensor_scan(pair_end[:], ones8[:], pairs_f[:], 0.0, ALU.mult, ALU.add))
            step(dve.tensor_tensor(offset[:], pair_end[:], pairs_f[:], ALU.subtract))
            step(dve.tensor_scalar(offset[:], offset[:], float(2 * P), -1.0, ALU.mult, ALU.add))
            step(dve.tensor_tensor(offset[:], offset[:], ps[:, 0, 0:8], ALU.add))
            for b in range(BINS):
                dve.scalar_tensor_tensor(place[:, b, :], seen[:, b, :], offset[:, b:b + 1], in_bin[:, b, :],
                                         ALU.add, ALU.mult).then_inc(index_step, 1)
                steps[0] += 1
            dve.wait_ge(index_step, steps[0])
            step(dve.tensor_reduce(pos[:], place.rearrange("p b j -> p j b"), AX.X, ALU.add))
            step(dve.tensor_tensor(passed[:], pair_no[:].unsqueeze(2).to_broadcast([P, PAIRS, BINS]),
                                   pair_end[:].unsqueeze(1).to_broadcast([P, PAIRS, BINS]), ALU.is_ge))
            step(dve.tensor_reduce(bin_of[:], passed[:], AX.X, ALU.add))
            step(dve.tensor_scalar(bin_of[:], bin_of[:], float(BINS - 1), None, ALU.min))
            dve.memset(v.tile_bin[:], 0).then_inc(index_step, 1)
            steps[0] += 1
            dve.wait_ge(index_step, steps[0])
            step(dve.tensor_copy(v.tile_bin[:, 1:PAIRS + 1], bin_of[:]))
            dve.wait_ge(edges_in, 80)
            em = edge_meta
            em_i = edge_meta[:].bitcast(I32)
            dve.tensor_copy(em_i[:, :, 0], src_i[:]).then_inc(index_step, 1)
            dve.scalar_tensor_tensor(em[:, :, 1], bin_f[:], float(-P), dst_f[:], ALU.mult, ALU.add).then_inc(index_step, 1)
            dve.tensor_copy(em[:, :, 2], weight[:]).then_inc(index_step, 1)
            dve.scalar_tensor_tensor(em_i[:, :, 3], type_i[:], float(N), src_i[:], ALU.mult, ALU.add).then_inc(index_step, 1)
            dve.tensor_copy(em[:, :, 4:8], y[:]).then_inc(index_step, 1)
            steps[0] += 5
            dve.wait_ge(index_step, steps[0])
            dve.tensor_scalar(em[:, :, 1], em[:, :, 1], 1.0, None, ALU.add).then_inc(index_step, 1)
            steps[0] += 1
            dve.wait_ge(index_step, steps[0])

            def pack(i, scattered_before):
                for b in range(2):
                    cols = bass.ds(i * (2 * G) + b * G, G)
                    dve.tensor_copy(a8[b][:].rearrange("p (j r) -> p j r", r=z.R8), attr[:, cols, :]).then_inc(staged, 1)
                for b in range(2):
                    cols = bass.ds(i * (2 * G) + b * G, G)
                    if scattered_before:
                        dve.wait_ge(scattered[b], 16 * G * i)
                    dve.tensor_copy(row_f[b][:], pos[:, cols]).then_inc(packed, 1)
                    dve.wait_ge(hidden_turned, 2 * i + b + 1)
                    hid = ps[:, 4 * b + 3, 0:G * HID].rearrange("p (j h) -> p j h", h=HID)
                    dve.tensor_copy(payload[b][:, :, 8:8 + HID].bitcast(F32R), hid).then_inc(parts_done, 1)
                    dve.tensor_copy(payload[b][:, :, 0:8], edge_meta[:, cols, :]).then_inc(places_done, 1)
                    dve.wait_ge(parts_done, 2 * i + b + 1)
                    dve.tensor_tensor(payload[b][:, :, 8 + HID:ROW], hid, payload[b][:, :, 8:8 + HID], ALU.subtract).then_inc(packed, 1)

            pack(0, False)
            with dve.Fori(1, ITERS) as i:
                pack(i, True)

        @blk.tensor
        def _(pe):
            pe.wait_ge(pool_step, 12)
            pe.wait_ge(index_step, row_total_at[0])
            pe.matmul(ps[:, 0, 0:8], lower[:], row_total[:], start=True, stop=True)
            pe.matmul(ps[:, 0, 8:16], ones[:], row_total[:], start=True, stop=True).then_inc(totals_ready, 1)
            pe.wait_ge(mlp_in, 16 * (G + 4))
            with pe.Fori(0, ITERS) as i:
                for b in range(2):
                    pe.wait_ge(staged, 2 * i + b + 1)
                    pe.transpose(ps[0:G * z.R8, 4 * b, 0:P], a8[b][:], v.ident[:]).then_inc(attr_turned, 1)
                for b in range(2):
                    pe.wait_ge(attr_cols, 2 * i + b + 1)
                    for jj in range(2):
                        last = pe.matmul(ps[:, 4 * b + 1, jj * P:(jj + 1) * P], w1[:, jj, :], a8T[b][:], start=True, stop=True)
                    last.then_inc(pre_act, 1)
                for layer, (w, hin, bank) in enumerate(((w2, h1, 2), (w3, h2, 1))):
                    for b in range(2):
                        pe.wait_ge(acted, 6 * i + 2 * layer + b + 1)
                        pe.matmul(ps[:, 4 * b + bank, 0:2 * P], w[:], hin[b][:], start=True, stop=True).then_inc(pre_act, 1)
                for b in range(2):
                    pe.wait_ge(acted, 6 * i + 4 + b + 1)
                    for jj in range(2):
                        last = pe.transpose(ps[:, 4 * b + 3, jj * P:(jj + 1) * P], h3[b][:, jj * P:(jj + 1) * P], v.ident[:])
                    last.then_inc(hidden_turned, 1)

        @blk.scalar
        def _(act):
            act.wait_ge(blocks_zero, 3)
            for j in range(G):
                act.dma_start(w1[j * z.R8:(j + 1) * z.R8, j // 2, (j % 2) * HID:(j % 2 + 1) * HID], a["L1_gnn_W_mlp1"]).then_inc(mlp_in, 16)
            for w, name in ((w2, "L1_gnn_W_mlp2"), (w3, "L1_gnn_W_mlp3")):
                for k in range(2):
                    act.dma_start(w[k * HID:(k + 1) * HID, k * HID:(k + 1) * HID], a[name]).then_inc(mlp_in, 16)
            with act.Fori(0, ITERS) as i:
                for b in range(2):
                    act.wait_ge(attr_turned, 2 * i + b + 1)
                    act.activation(a8T[b][:], ps[0:G * z.R8, 4 * b, 0:P], ACT.Copy).then_inc(attr_cols, 1)
                for layer, (hout, bank, scale) in enumerate(((h1, 1, z.R8 ** -0.5), (h2, 2, SILU_2MOM * HID ** -0.5), (h3, 1, SILU_2MOM * HID ** -0.5))):
                    for b in range(2):
                        act.wait_ge(pre_act, 6 * i + 2 * layer + b + 1)
                        act.activation(hout[b][:], ps[:, 4 * b + bank, 0:2 * P], ACT.Silu, scale=scale).then_inc(acted, 1)



def counts_block(nc, a, v):
    z, BINS, TILES, PAIRS, ROW = v.z, v.BINS, v.TILES, v.PAIRS, v.ROW
    HALF = v.N // 2
    RING = 4
    STEPS = TILES // RING
    with nc.cleanup_on_exit(), ExitStack() as c:
        def sb(name, shape, dt=F32):
            return c.enter_context(nc.sbuf_tensor(name, shape, dt))

        def sem(name):
            return nc.alloc_semaphore(name="count_" + name)
        ps = v.ps
        node_no = sb("node_no", [P, v.N], F16)
        src_f = sb("src_f", [P, TILES])
        zero_b = sb("zero_b", [P, HALF], BF16)
        src_hot = [sb(f"src_hot{r}", [P, HALF], BF16) for r in range(RING)]
        dst_hot = [sb(f"dst_hot{r}", [P, P], BF16) for r in range(RING)]
        meta_in, set_up, hot, hot_used, half_summed, half_kept, src_ready = (
            sem(n) for n in ("meta_in", "set_up", "hot", "hot_used", "half_summed", "half_kept", "src_ready"))
        blk = c.enter_context(nc.Block())

        @blk.sync
        def _(sp):
            with nc.allow_non_contiguous_dma(reason="slot meta"):
                sp.dma_start(v.meta[:], v.slots[0:TILES * P, 0:8].rearrange("(t p) r -> p t r", p=P)).then_inc(meta_in, 16)

        @blk.gpsimd
        def _(pool):
            pool.iota(node_no[:], pattern=[[1, v.N]], base=0, channel_multiplier=0,
                      allow_small_or_imprecise_dtypes=True).then_inc(set_up, 1)
            pool.memset(zero_b[:], 0.0).then_inc(set_up, 1)

        @blk.vector
        def _(dve):
            dve.wait_ge(meta_in, 16)
            dve.tensor_copy(src_f[:], v.meta[:].bitcast(I32)[:, :, 0]).then_inc(src_ready, 1)
            dve.wait_ge(src_ready, 1)
            dve.wait_ge(set_up, 2)
            for half in range(2):
                with dve.Fori(0, STEPS) as i:
                    for r in range(RING):
                        t = i * RING + r
                        dve.wait_ge(hot_used, t + 1 + half * TILES)
                        dve.tensor_scalar(src_hot[r][:], node_no[:, half * HALF:(half + 1) * HALF],
                                          src_f[:, bass.ds(t, 1)], None, ALU.is_equal).then_inc(hot, 1)
                        dve.tensor_scalar(dst_hot[r][:], v.iota1[:], v.meta[:, bass.ds(t, 1), 1:2].rearrange("p a b -> p (a b)"), None,
                                          ALU.is_equal).then_inc(hot, 1)
                dve.wait_ge(half_summed, half + 1)
                for b in range(0, BINS, 2):
                    dve.tensor_copy(v.by_dst[:, b, half * HALF:(half + 1) * HALF], ps[:, b, :]).then_inc(half_kept, 1)

        @blk.scalar
        def _(act):
            for half in range(2):
                act.wait_ge(half_summed, half + 1)
                for b in range(1, BINS, 2):
                    act.activation(v.by_dst[:, b, half * HALF:(half + 1) * HALF], ps[:, b, :], ACT.Copy).then_inc(half_kept, 1)

        @blk.tensor
        def _(pe):
            pe.wait_ge(set_up, 2)
            pe.sem_inc(hot_used, RING)
            for half in range(2):
                if half:
                    pe.wait_ge(half_kept, BINS * half)
                for b in range(BINS):
                    pe.matmul(ps[:, b, :], zero_b[:, 0:P], zero_b[:], start=True, stop=False, skip_group_check=True)
                with pe.Fori(0, STEPS) as i:
                    for r in range(RING):
                        t = i * RING + r
                        if r % 2 == 0:
                            b = pe.value_load(v.tile_bin[0:1, bass.ds(i * (RING // 2) + r // 2 + 1, 1)], min_val=0, max_val=BINS - 1)
                        pe.wait_ge(hot, 2 * t + 2 + half * 2 * TILES)
                        pe.matmul(ps[:, bass.ds(b, 1), :], dst_hot[r][:], src_hot[r][:], start=False, stop=False,
                                  skip_group_check=True).then_inc(hot_used, 1)
                pe.matmul(ps[:, 0, :], zero_b[:, 0:P], zero_b[:], start=False, stop=True, skip_group_check=True).then_inc(half_summed, 1)


def layer_norm_dve(dve, v, rows_ready, norm_step, rooted, norm_ready):
    for t in range(v.BINS):
        rows_ready(t)
        dve.bn_stats(v.stats[:, t, :], v.x[:, t, :]).then_inc(norm_step, 1)
    for t in range(v.BINS):
        dve.wait_ge(norm_step, t + 1)
        dve.bn_aggr(v.moments[:, t, :], v.stats[:, t, :]).then_inc(norm_step, 1)
    n = 2 * v.BINS
    dve.wait_ge(norm_step, n)
    dve.tensor_scalar(v.rstd[:], v.moments[:, :, 1], EPS, None, ALU.add).then_inc(norm_step, 1)
    dve.wait_ge(rooted, 1)
    dve.scalar_tensor_tensor(v.shift[:], v.moments[:, :, 0], -1.0, v.rstd[:], ALU.mult, ALU.mult).then_inc(norm_ready, 1)


def root_pool(pool, v, values, done, at, rooted):
    pool.wait_ge(done, at)
    pool.tensor_tensor(values, values, v.minus_half[:, 0:values.shape[1]], ALU.pow).then_inc(rooted, 1)


def layer_norm_act(act, v, norm_ready, h_ready):
    act.wait_ge(norm_ready, 1)
    for t in range(v.BINS):
        act.activation(v.h[:, t, :], v.x[:, t, :], ACT.Relu, bias=v.shift[:, t:t + 1], scale=v.rstd[:, t:t + 1]).then_inc(h_ready, 1)


def transposes_pe(pe, v, blocks, banks, h_ready, h_base, turned, kept, kept_base):
    for t in range(v.BINS):
        pe.wait_ge(h_ready, h_base + t + 1)
        if t >= len(banks):
            pe.wait_ge(kept, kept_base + t - len(banks) + 1)
        for k, block in enumerate(blocks(t)):
            last = pe.transpose(v.ps[:, banks[t % len(banks)], k * P:(k + 1) * P], block, v.ident[:])
        last.then_inc(turned, 1)


def gcn_block(nc, a, v):
    z, BINS, KT, N = v.z, v.BINS, v.KT, v.N
    with nc.cleanup_on_exit(), ExitStack() as c:
        def sem(name):
            return nc.alloc_semaphore(name="gcn_" + name)

        def sb(name, shape, dt=F32):
            return c.enter_context(nc.sbuf_tensor(name, shape, dt))
        ps, x, h, hT, by_src, by_dst = v.ps, v.x, v.h, v.hT, v.by_src, v.by_dst
        out_degree = sb("out_degree", [P, 8])
        has_out = sb("has_out", [P, 8])
        (norm_step, rooted, norm_ready, h_ready, turned, kept, projected, h_kept, counts_turned, counts_kept, adj_step, adj_ready,
         scaled, summed, row_step, x_kept, degree_step) = (sem(n) for n in (
             "norm_step", "rooted", "norm_ready", "h_ready", "turned", "kept", "projected", "h_kept", "counts_turned", "counts_kept",
             "adj_step", "adj_ready", "scaled", "summed", "row_step", "x_kept", "degree_step"))
        blk = c.enter_context(nc.Block())

        @blk.sync
        def _(sp):
            sp.wait_ge(projected, BINS)

        @blk.gpsimd
        def _(pool):
            root_pool(pool, v, v.rstd[:], norm_step, 2 * BINS + 1, rooted)
            root_pool(pool, v, v.dinv_gcn[:], adj_step, 4 * BINS, rooted)
            root_pool(pool, v, v.dinv_cheb[:], degree_step, 1, rooted)

        @blk.vector
        def _(dve):
            layer_norm_dve(dve, v, lambda t: dve.wait_ge(v.x_in, 16), norm_step, rooted, norm_ready)
            for t in range(BINS):
                dve.wait_ge(turned, t + 1)
                dve.tensor_copy(hT[:, :, t * P:(t + 1) * P], ps[:, t % 4, :].rearrange("p (k n) -> p k n", n=P)).then_inc(kept, 1)
            dve.wait_ge(counts_kept, BINS)
            for t in range(BINS):
                dve.tensor_tensor(by_dst[:, t, :], by_dst[:, t, :], by_src[:, t, :], ALU.add).then_inc(adj_step, 1)
            for t in range(BINS):
                dve.wait_ge(adj_step, t + 1)
                dve.tensor_scalar(by_dst[:, t, :], by_dst[:, t, :], 1.0, None, ALU.min).then_inc(adj_step, 1)
            for t in range(BINS):
                dve.wait_ge(adj_step, BINS + t + 1)
                dve.tensor_tensor(by_dst[:, t, t * P:(t + 1) * P], by_dst[:, t, t * P:(t + 1) * P], v.ident[:], ALU.add).then_inc(adj_step, 1)
            for t in range(BINS):
                dve.wait_ge(adj_step, 2 * BINS + t + 1)
                dve.reduce_sum(v.dinv_gcn[:, t:t + 1], by_dst[:, t, :], AX.X).then_inc(adj_step, 1)
            dve.tensor_scalar(v.dinv_cheb[:], out_degree[:], 1.0, None, ALU.max).then_inc(degree_step, 1)
            dve.wait_ge(rooted, 3)
            dve.tensor_scalar(has_out[:], out_degree[:], 0.0, None, ALU.is_gt).then_inc(degree_step, 1)
            dve.wait_ge(degree_step, 2)
            dve.tensor_tensor(v.dinv_cheb[:], v.dinv_cheb[:], has_out[:], ALU.mult).then_inc(degree_step, 1)
            dve.wait_ge(degree_step, 3)
            dve.tensor_scalar(v.ndinv_cheb[:], v.dinv_cheb[:], -1.0, None, ALU.mult).then_inc(degree_step, 1)
            for t in range(BINS):
                dve.wait_ge(summed, t + 1)
                dve.scalar_tensor_tensor(x[:, t, :], ps[:, t, :], v.dinv_gcn[:, t:t + 1], x[:, t, :], ALU.mult, ALU.add).then_inc(row_step, 1)
                dve.wait_ge(row_step, t + 1)
                dve.tensor_tensor(x[:, t, :], x[:, t, :], v.vec[:, 0, :], ALU.add).then_inc(x_kept, 1)

        @blk.scalar
        def _(act):
            layer_norm_act(act, v, norm_ready, h_ready)
            for t in range(BINS):
                act.wait_ge(projected, t + 1)
                act.activation(h[:, t, :], ps[:, 4 + t % 4, :], ACT.Copy).then_inc(h_kept, 1)
            for t in range(BINS):
                act.wait_ge(counts_turned, t + 1)
                g = 2 * (t % 4)
                act.activation(by_src[:, t, :], ps[:, g:g + 2, :].rearrange("p a n -> p (a n)"), ACT.Copy,
                               accum_out=out_degree[:, t:t + 1]).then_inc(counts_kept, 1)
            act.wait_ge(rooted, 2)
            for t in range(BINS):
                act.activation(h[:, t, :], h[:, t, :], ACT.Copy, scale=v.dinv_gcn[:, t:t + 1]).then_inc(scaled, 1)

        @blk.tensor
        def _(pe):
            transposes_pe(pe, v, lambda t: [h[:, t, k * P:(k + 1) * P] for k in range(KT)], [0, 1, 2, 3], h_ready, 0, turned, kept, 0)
            pe.wait_ge(v.weights_in[0], 32)
            for t in range(BINS):
                pe.wait_ge(kept, t + 1)
                if t >= 4:
                    pe.wait_ge(h_kept, t - 3)
                for k in range(KT):
                    last = pe.matmul(ps[:, 4 + t % 4, :], hT[:, k, t * P:(t + 1) * P], v.weights[:, 0, k, :], start=(k == 0), stop=(k == KT - 1))
                last.then_inc(projected, 1)
            pe.wait_ge(h_kept, BINS)
            for t in range(BINS):
                if t >= 4:
                    pe.wait_ge(counts_kept, t - 3)
                for b in range(BINS):
                    last = pe.transpose(ps[:, 2 * (t % 4) + b // 4, (b % 4) * P:(b % 4 + 1) * P], by_dst[:, b, t * P:(t + 1) * P], v.ident[:])
                last.then_inc(counts_turned, 1)
            pe.wait_ge(scaled, BINS)
            for t in range(BINS):
                for m in range(BINS):
                    last = pe.matmul(ps[:, t, :], by_dst[:, m, t * P:(t + 1) * P], h[:, m, :], start=(m == 0), stop=(m == BINS - 1))
                last.then_inc(summed, 1)


def tensor_product_block(nc, a, v):
    z, BINS, KT, N, D, PAIRS, ROW, HID = v.z, v.BINS, v.KT, v.N, v.D, v.PAIRS, v.ROW, v.HID
    RING = 4
    Y = range(4)
    acc = v.by_dst
    x, h, hT, ps = v.x, v.h, v.hT, v.ps
    with nc.cleanup_on_exit(), ExitStack() as c0:
        def sb0(name, shape, dt=F32):
            return c0.enter_context(nc.sbuf_tensor(name, shape, dt))

        def sem0(name):
            return nc.alloc_semaphore(name="sum_" + name)
        up = sb0("w_up", [P, 2, P])
        w4 = sb0("w_mlp4", [P, D])
        w4_parts = sb0("w_mlp4_parts", [P, 2, D], F32R)
        wo = sb0("w_out", [P, 2, 2, P])
        rows = sb0("up_rows", [P, 2, D])
        tp_weights, w_step, w_scaled = sem0("tp_weights"), sem0("w_step"), sem0("w_scaled")

        with nc.cleanup_on_exit(), ExitStack() as c:
            def sem(name):
                return nc.alloc_semaphore(name="sum_" + name)
            norm_step, rooted, norm_ready, h_ready, turned, kept, projected, staged, table_out = (sem(n) for n in (
                "tp_norm_step", "tp_rooted", "tp_norm_ready", "tp_h_ready", "tp_turned", "tp_kept", "tp_projected", "tp_staged", "table_out"))
            blk = c.enter_context(nc.Block())

            @blk.sync
            def _(sp):
                sp.dma_start(up[:, 0, :], a["L1_gnn_W_up0"]).then_inc(tp_weights, 16)
                sp.dma_start(up[:, 1, :], a["L1_gnn_W_up1"]).then_inc(tp_weights, 16)
                sp.dma_start(w4[0:HID, :], a["L1_gnn_W_mlp4"]).then_inc(tp_weights, 16)
                sp.dma_start(w4[HID:P, :], a["L1_gnn_W_mlp4"]).then_inc(tp_weights, 16)
                sp.dma_start(wo[:, 0], a["L1_gnn_W_out0"].rearrange("(q u) n -> u q n", u=P)).then_inc(tp_weights, 16)
                sp.dma_start(wo[:, 1], a["L1_gnn_W_out1"].rearrange("(q u) n -> u q n", u=P)).then_inc(tp_weights, 16)
                for t in range(BINS):
                    sp.wait_ge(staged, t + 1)
                    sp.dma_start(v.up_table[t * P:(t + 1) * P, :], rows[:, t % 2, :]).then_inc(table_out, 16)
                    sp.wait_ge(table_out, 16 * (t + 1))
                for n, name in enumerate(("L2_gnn_W1_0", "L2_gnn_W1_1", "L2_gnn_W2_0", "L2_gnn_W2_1")):
                    sp.dma_start(v.weights[:, n], a[name].rearrange("(k p) n -> p k n", p=P)).then_inc(v.weights_in[n], 16)

            @blk.vector
            def _(dve):
                layer_norm_dve(dve, v, lambda t: None, norm_step, rooted, norm_ready)
                for t in range(BINS):
                    dve.wait_ge(turned, t + 1)
                    dve.tensor_copy(hT[:, :, t * P:(t + 1) * P], ps[:, t % 4, :].rearrange("p (k n) -> p k n", n=P)).then_inc(kept, 1)
                for t in range(BINS):
                    dve.wait_ge(projected, t + 1)
                    if t >= 2:
                        dve.wait_ge(table_out, 16 * (t - 1))
                    dve.tensor_scalar(rows[:, t % 2, :], ps[:, 4 + t % 4, :], P ** -0.5, None, ALU.mult).then_inc(staged, 1)

            @blk.gpsimd
            def _(pool):
                root_pool(pool, v, v.rstd[:], norm_step, 2 * BINS + 1, rooted)
                pool.memset(acc[:], 0.0).then_inc(w_step, 1)
                pool.wait_ge(w_scaled, 2)
                pool.tensor_copy(w4_parts[:, 0, :], w4[:]).then_inc(w_scaled, 1)
                pool.wait_ge(w_scaled, 3)
                pool.tensor_tensor(w4_parts[:, 1, :], w4[:], w4_parts[:, 0, :].bitcast(F32), ALU.subtract).then_inc(w_step, 1)

            @blk.scalar
            def _(act):
                layer_norm_act(act, v, norm_ready, h_ready)
                act.wait_ge(tp_weights, 96)
                c4 = SILU_2MOM * HID ** -0.5
                co = (2 * P) ** -0.5 / AVG_NEIGHBORS
                act.activation(w4[:, 0:3 * P], w4[:, 0:3 * P], ACT.Copy, scale=c4).then_inc(w_scaled, 1)
                act.activation(w4[:, 3 * P:], w4[:, 3 * P:], ACT.Copy, scale=c4 * 3.0 ** -0.5).then_inc(w_scaled, 1)
                act.activation(wo[:].rearrange("p a q n -> p (a q n)"), wo[:].rearrange("p a q n -> p (a q n)"), ACT.Copy, scale=co).then_inc(w_step, 1)

            @blk.tensor
            def _(pe):
                transposes_pe(pe, v, lambda t: [h[:, t, 0:P]] + [h[:, t, P + m:D:3] for m in range(3)], [0, 1, 2, 3],
                              h_ready, 0, turned, kept, 0)
                pe.wait_ge(tp_weights, 96)
                for t in range(BINS):
                    pe.wait_ge(kept, t + 1)
                    if t >= 4:
                        pe.wait_ge(staged, t - 3)
                    for k in range(4):
                        last = pe.matmul(ps[:, 4 + t % 4, k * P:(k + 1) * P], hT[:, k, t * P:(t + 1) * P], up[:, min(k, 1), :], start=True, stop=True)
                    last.then_inc(projected, 1)

        with nc.cleanup_on_exit(), ExitStack() as c:
            def sb(name, shape, dt=F32):
                return c.enter_context(nc.sbuf_tensor(name, shape, dt))

            def sem(name):
                return nc.alloc_semaphore(name="sum_" + name)
            G = hT[:].rearrange("p k n -> p (k n)").rearrange("p (r q d) -> p r q d", r=RING, q=2)
            slot = [sb(f"slot{r}", [P, 2, ROW]) for r in range(RING)]
            nodes = [[sb(f"nodes{r}{q}", [P, 1], I32) for q in range(2)] for r in range(RING)]
            zero1 = sb("zero1", [P, 1], I32)
            hidT = [sb(f"hidT{b}", [P, 2, P], F32R) for b in range(2)]
            hot = [[sb(f"hot{r}{q}", [P, P]) for q in range(2)] for r in range(RING)]
            hot_y = [[sb(f"hot_y{b}{q}", [P, 4, P]) for q in range(2)] for b in range(2)]
            dots = [[sb(f"dots{b}{q}", [P, P]) for q in range(2)] for b in range(2)]
            msg = [[sb(f"msg{b}{q}", [P, 6, P]) for q in range(2)] for b in range(2)]
            fT = [sb(f"fT{b}", [P, 8, P]) for b in range(2)]
            slot_in = [sem(f"slot_in{r}") for r in range(RING)]
            rows_in = [sem(f"rows_in{r}") for r in range(RING)]
            (slot_free, index_set, pool_set, hid_turned, hid_kept, weighted, hot_set, hot_scaled, dot_step, msg_done, summed, added,
             f_turned, f_kept, mixed, x_step, vector_msg, gathers_free) = (sem(n) for n in (
                 "slot_free", "index_set", "pool_set", "hid_turned", "hid_kept", "weighted", "hot_set", "hot_scaled", "dot_step",
                 "msg_done", "summed", "added", "f_turned", "f_kept", "mixed", "x_step", "vector_msg", "gathers_free"))
            STEPS = PAIRS // RING
            blk = c.enter_context(nc.Block())
            acc_banks = lambda b: ps[:, 4 + 2 * b:6 + 2 * b, :]

            @blk.sync
            def _(sp):
                view = v.slots.rearrange("(s q p) r -> s p q r", q=2, p=P)

                def load(r, pair):
                    sp.dma_start(slot[r][:], pair).then_inc(slot_in[r], 16)

                for r in range(RING):
                    load(r, view[r])
                with sp.Fori(0, STEPS - 1) as i:
                    for r in range(RING):
                        sp.wait_ge(msg_done, 8 * i + 2 * r + 2)
                        sp.wait_ge(hot_scaled, 8 * i + 2 * r + 2)
                        load(r, view[bass.ds((i + 1) * RING + r, 1)].rearrange("a p q r -> p (a q) r"))

            @blk.gpsimd
            def _(pool):
                pool.memset(zero1[:], 0).then_inc(pool_set, 1)
                pool.wait_ge(pool_set, 1)
                with pool.Fori(0, STEPS) as i:
                    for r in range(RING):
                        pool.sem_clear(index_set)
                        pool.wait_ge(gathers_free, 4 * i + r + 1)
                        pool.wait_ge(slot_in[r], 16 * i + 16)
                        for q in range(2):
                            pool.tensor_tensor(nodes[r][q][:], slot[r][:, q, 0:1].bitcast(I32), zero1[:], ALU.add).then_inc(index_set, 1)
                        pool.wait_ge(index_set, 2)
                        for q in range(2):
                            pool.indirect_dma_start(out=G[:, r, q, :], out_offset=None, in_=v.up_table,
                                                    in_offset=bass.IndirectOffsetOnAxis(ap=nodes[r][q][:], axis=0)).then_inc(rows_in[r], 16)
                        for q in range(2):
                            pool.tensor_scalar(hot[r][q][:], v.iota1[:], slot[r][:, q, 1:2], None, ALU.is_equal).then_inc(hot_set, 1)

            @blk.vector
            def _(dve):
                dve.sem_inc(gathers_free, RING - 1)
                with dve.Fori(0, STEPS) as i:
                    for r in range(RING):
                        b = r % 2
                        for q in range(2):
                            n = 8 * i + 2 * r + q
                            s, g, m = slot[r][:, q, :], G[:, r, q, :], msg[b][q]
                            dve.wait_ge(slot_in[r], 16 * i + 16)
                            dve.wait_ge(rows_in[r], 32 * i + 32)
                            dve.tensor_scalar(dots[b][q][:], g[:, P:2 * P], s[:, 5:6], None, ALU.mult).then_inc(dot_step, 1)
                            dve.wait_ge(weighted, n + 1)
                            wv = ps[:, q, :]
                            dve.tensor_tensor(m[:, 0:6:5, :], wv[:, 0:2 * P].rearrange("p (a n) -> p a n", n=P),
                                              g[:, 0:P].unsqueeze(1).to_broadcast([P, 2, P]), ALU.mult).then_inc(dot_step, 1)
                            dve.wait_ge(dot_step, 4 * n + 1)
                            dve.scalar_tensor_tensor(dots[b][q][:], g[:, 2 * P:3 * P], s[:, 6:7], dots[b][q][:], ALU.mult, ALU.add).then_inc(dot_step, 1)
                            dve.tensor_tensor(m[:, 1:4, :], wv[:, 2 * P:3 * P].unsqueeze(1).to_broadcast([P, 3, P]),
                                              g[:, P:4 * P].rearrange("p (a n) -> p a n", n=P), ALU.mult).then_inc(vector_msg, 1)
                            dve.wait_ge(dot_step, 4 * n + 3)
                            dve.scalar_tensor_tensor(dots[b][q][:], g[:, 3 * P:4 * P], s[:, 7:8], dots[b][q][:], ALU.mult, ALU.add).then_inc(dot_step, 1)
                            dve.wait_ge(dot_step, 4 * n + 4)
                            dve.tensor_tensor(m[:, 4, :], wv[:, 3 * P:4 * P], dots[b][q][:], ALU.mult).then_inc(msg_done, 1)
                        last_bin = dve.value_load(v.tile_bin[0:1, bass.ds(i * RING + r, 1)], min_val=0, max_val=BINS - 1)
                        dve.wait_ge(summed, 8 * i + 2 * r + 1)
                        dst = acc[:, bass.ds(last_bin, 1), :]
                        dve.tensor_tensor(dst, dst, acc_banks(1 - b).rearrange("p a n -> p (a n)").unsqueeze(1), ALU.add).then_inc(added, 1)
                        dve.wait_ge(added, 4 * i + r + 1)
                        dve.sem_inc(gathers_free, 1)
                last_bin = dve.value_load(v.tile_bin[0:1, PAIRS:PAIRS + 1], min_val=0, max_val=BINS - 1)
                dve.wait_ge(summed, 2 * PAIRS + 1)
                dst = acc[:, bass.ds(last_bin, 1), :]
                dve.tensor_tensor(dst, dst, acc_banks(1).rearrange("p a n -> p (a n)").unsqueeze(1), ALU.add).then_inc(added, 1)
                for t in range(BINS):
                    xr = x[:, t, :]
                    dve.wait_ge(mixed, t + 1)
                    dve.tensor_tensor(xr[:, 0:P], xr[:, 0:P], ps[:, 4 + t % 4, 0:P], ALU.add).then_inc(x_step, 1)
                    xm = xr[:, P:D].rearrange("p (n m) -> p m n", m=3)
                    dve.tensor_tensor(xm, xm, ps[:, 4 + t % 4, P:D].rearrange("p (m n) -> p m n", m=3), ALU.add).then_inc(x_step, 1)

            @blk.scalar
            def _(act):
                with act.Fori(0, STEPS) as i:
                    for r in range(RING):
                        b = r % 2
                        act.wait_ge(hid_turned, 4 * i + r + 1)
                        act.activation(hidT[b][:].rearrange("p q e -> p (q e)"), ps[:, 2 + b, 0:2 * P], ACT.Copy).then_inc(hid_kept, 1)
                        for q in range(2):
                            act.wait_ge(hot_set, 8 * i + 2 * r + q + 1)
                            for m in Y:
                                last = act.activation(hot_y[b][q][:, m, :], hot[r][q][:], ACT.Copy, scale=slot[r][:, q, 4 + m:5 + m])
                            last.then_inc(hot_scaled, 1)
                for t in range(BINS):
                    act.wait_ge(f_turned, t + 1)
                    g = 2 * (t % 2)
                    act.activation(fT[t % 2][:].rearrange("p a n -> p (a n)"), ps[:, g:g + 2, :].rearrange("p a n -> p (a n)"), ACT.Copy).then_inc(f_kept, 1)

            def mix(pe, t):
                f = fT[t % 2]
                pe.wait_ge(f_kept, t + 1)
                if t >= 4:
                    pe.wait_ge(x_step, 2 * (t - 3))
                o = ps[:, 4 + t % 4, :]
                pe.matmul(o[:, 0:P], f[:, 0, :], wo[:, 0, 0, :], start=True, stop=False, skip_group_check=True)
                last = pe.matmul(o[:, 0:P], f[:, 4, :], wo[:, 0, 1, :], start=False, stop=True, skip_group_check=True)
                for m in range(3):
                    pe.matmul(o[:, (m + 1) * P:(m + 2) * P], f[:, 5 + m, :], wo[:, 1, 0, :], start=False, stop=False, skip_group_check=True)
                    last = pe.matmul(o[:, (m + 1) * P:(m + 2) * P], f[:, 1 + m, :], wo[:, 1, 1, :], start=False, stop=True, skip_group_check=True)
                last.then_inc(mixed, 1)

            @blk.tensor
            def _(pe):
                def turn_hidden(rr, at):
                    pe.wait_ge(slot_in[rr], at)
                    for q in range(2):
                        last = pe.transpose(ps[:, 2 + rr % 2, q * P:(q + 1) * P], slot[rr][:, q, 8:ROW], v.ident[:])
                    last.then_inc(hid_turned, 1)

                def path_weights(rr, q):
                    pe.matmul(ps[:, q, :], hidT[rr % 2][:, q, :], w4_parts[:, 0, :], start=True, stop=False)
                    pe.matmul(ps[:, q, :], hidT[rr % 2][:, q, :], w4_parts[:, 1, :], start=False, stop=True).then_inc(weighted, 1)

                pe.wait_ge(w_step, 3)
                for j in range(2):
                    last = pe.matmul(ps[:, 6 + j, :], acc[:, 0, 0:P], acc[:, 0, 0:D], start=True, stop=True)
                last.then_inc(summed, 1)
                turn_hidden(0, 16)
                pe.wait_ge(hid_kept, 1)
                path_weights(0, 0)
                path_weights(0, 1)

                def pair(i, r, more):
                    b, nxt = r % 2, (r + 1) % RING
                    if more:
                        turn_hidden(nxt, 16 * i + 16 + (16 if nxt == 0 else 0))
                    for q in range(2):
                        pe.wait_ge(msg_done, 8 * i + 2 * r + q + 1)
                        if more:
                            pe.wait_ge(hid_kept, 4 * i + r + 2)
                            path_weights(nxt, q)
                        pe.wait_ge(hot_scaled, 8 * i + 2 * r + q + 1)
                        m, hy, first, lastq = msg[b][q], hot_y[b][q], q == 0, q == 1
                        A, B = ps[:, 4 + 2 * b, :], ps[:, 5 + 2 * b, :]
                        pe.matmul(A, hy[:, 0, :], m[:, 0:4, :], start=first, stop=lastq, skip_group_check=True)
                        pe.matmul(B[:, 0:P], hot[r][q][:], m[:, 4, :], start=first, stop=lastq, skip_group_check=True)
                        for k in range(3):
                            last = pe.matmul(B[:, (k + 1) * P:(k + 2) * P], hy[:, k + 1, :], m[:, 5, :], start=False, stop=lastq, skip_group_check=True)
                        last.then_inc(summed, 1)

                with pe.Fori(0, STEPS - 1) as i:
                    for r in range(RING):
                        pair(i, r, True)
                for r in range(RING):
                    pair(STEPS - 1, r, r < RING - 1)
                pe.wait_ge(added, PAIRS + 1)
                for t in range(BINS):
                    g = 2 * (t % 2)
                    if t >= 2:
                        pe.wait_ge(f_kept, t - 1)
                    for k in range(8):
                        last = pe.transpose(ps[:, g + k // 4, (k % 4) * P:(k % 4 + 1) * P], acc[:, t, k * P:(k + 1) * P], v.ident[:])
                    last.then_inc(f_turned, 1)
                    if t >= 1:
                        mix(pe, t - 1)
                mix(pe, BINS - 1)


def cheb_block(nc, a, v):
    z, BINS, KT, N, D = v.z, v.BINS, v.KT, v.N, v.D
    x, h, hT, ps, by_src = v.x, v.h, v.hT, v.ps, v.by_src
    r = v.by_dst[:, :, 0:D]
    with nc.cleanup_on_exit(), ExitStack() as c:
        def sem(name):
            return nc.alloc_semaphore(name=name)
        affine = c.enter_context(nc.sbuf_tensor("affine", [P, 4, D], F32))
        names = ("norm_step", "rooted", "norm_ready", "h_ready", "turned", "kept", "projected", "scaled", "summed", "row_step", "affine_in", "leaky")
        S = {n: sem("cheb_" + n) for n in names}
        blk = c.enter_context(nc.Block())
        NB2 = 2 * BINS

        @blk.sync
        def _(sp):
            for k, name in enumerate(("L2_gnn_b1", "L2_gnn_b2", "L2_gnn_gamma", "L2_gnn_beta")):
                sp.dma_start(affine[:, k, :], broadcast_rows(a[name], D)).then_inc(S["affine_in"], 16)
            sp.wait_ge(S["affine_in"], 64)

        @blk.gpsimd
        def _(pool):
            root_pool(pool, v, v.rstd[:], S["norm_step"], 2 * BINS + 1, S["rooted"])
            root_pool(pool, v, v.rstd[:], S["norm_step"], 4 * BINS + 2, S["rooted"])

        @blk.vector
        def _(dve):
            layer_norm_dve(dve, v, lambda t: None, S["norm_step"], S["rooted"], S["norm_ready"])
            dve.wait_ge(S["affine_in"], 64)
            for conv in range(2):
                for t in range(BINS):
                    dve.wait_ge(S["turned"], conv * BINS + t + 1)
                    dve.tensor_copy(hT[:, :, t * P:(t + 1) * P], ps[:, t % 4, :].rearrange("p (k n) -> p k n", n=P)).then_inc(S["kept"], 1)
                for t in range(BINS):
                    dve.wait_ge(S["summed"], conv * BINS + t + 1)
                    g = 2 * (t % 4)
                    own, far = ps[:, g, :], ps[:, g + 1, :]
                    if conv == 0:
                        dve.scalar_tensor_tensor(r[:, t, :], far, v.ndinv_cheb[:, t:t + 1], affine[:, 0, :], ALU.mult, ALU.add).then_inc(S["row_step"], 1)
                        dve.wait_ge(S["row_step"], 2 * t + 1)
                        dve.tensor_tensor(r[:, t, :], r[:, t, :], own, ALU.add).then_inc(S["row_step"], 1)
                    else:
                        at = NB2 + 3 * t
                        dve.scalar_tensor_tensor(x[:, t, :], far, v.ndinv_cheb[:, t:t + 1], x[:, t, :], ALU.mult, ALU.add).then_inc(S["row_step"], 1)
                        dve.wait_ge(S["row_step"], at + 1)
                        dve.tensor_tensor(x[:, t, :], x[:, t, :], own, ALU.add).then_inc(S["row_step"], 1)
                        dve.wait_ge(S["row_step"], at + 2)
                        dve.tensor_tensor(x[:, t, :], x[:, t, :], affine[:, 1, :], ALU.add).then_inc(S["row_step"], 1)
                if conv == 0:
                    n0 = 2 * BINS + 1
                    for t in range(BINS):
                        dve.wait_ge(S["row_step"], 2 * t + 2)
                        dve.bn_stats(v.stats[:, t, :], r[:, t, :]).then_inc(S["norm_step"], 1)
                    for t in range(BINS):
                        dve.wait_ge(S["norm_step"], n0 + t + 1)
                        dve.bn_aggr(v.moments[:, t, :], v.stats[:, t, :]).then_inc(S["norm_step"], 1)
                    dve.wait_ge(S["norm_step"], n0 + 2 * BINS)
                    dve.tensor_scalar(v.rstd[:], v.moments[:, :, 1], EPS, None, ALU.add).then_inc(S["norm_step"], 1)
                    dve.wait_ge(S["rooted"], 2)
                    for t in range(BINS):
                        at = 4 * t
                        dve.tensor_scalar(r[:, t, :], r[:, t, :], v.moments[:, t, 0:1], v.rstd[:, t:t + 1], ALU.subtract, ALU.mult).then_inc(S["leaky"], 1)
                        dve.wait_ge(S["leaky"], at + 1)
                        dve.tensor_tensor(r[:, t, :], r[:, t, :], affine[:, 2, :], ALU.mult).then_inc(S["leaky"], 1)
                        dve.wait_ge(S["leaky"], at + 2)
                        dve.tensor_tensor(r[:, t, :], r[:, t, :], affine[:, 3, :], ALU.add).then_inc(S["leaky"], 1)
                        dve.wait_ge(S["leaky"], at + 3)
                        dve.scalar_tensor_tensor(r[:, t, :], r[:, t, :], LEAK, r[:, t, :], ALU.mult, ALU.max).then_inc(S["leaky"], 1)

        @blk.scalar
        def _(act):
            layer_norm_act(act, v, S["norm_ready"], S["h_ready"])
            for conv in range(2):
                for t in range(BINS):
                    act.wait_ge(S["projected"], conv * BINS + t + 1)
                    act.activation(h[:, t, :], ps[:, 4 + t % 4, :], ACT.Copy, scale=v.dinv_cheb[:, t:t + 1]).then_inc(S["scaled"], 1)

        @blk.tensor
        def _(pe):
            for conv in range(2):
                if conv == 0:
                    transposes_pe(pe, v, lambda t: [h[:, t, k * P:(k + 1) * P] for k in range(KT)], [0, 1, 2, 3], S["h_ready"], 0, S["turned"], S["kept"], 0)
                else:
                    for t in range(BINS):
                        pe.wait_ge(S["leaky"], 4 * t + 4)
                        if t >= 4:
                            pe.wait_ge(S["kept"], BINS + t - 3)
                        for k in range(KT):
                            last = pe.transpose(ps[:, t % 4, k * P:(k + 1) * P], r[:, t, k * P:(k + 1) * P], v.ident[:])
                        last.then_inc(S["turned"], 1)
                pe.wait_ge(v.weights_in[2 * conv + 1], 16)
                for t in range(BINS):
                    pe.wait_ge(S["kept"], conv * BINS + t + 1)
                    if t >= 4:
                        pe.wait_ge(S["scaled"], conv * BINS + t - 3)
                    for k in range(KT):
                        last = pe.matmul(ps[:, 4 + t % 4, :], hT[:, k, t * P:(t + 1) * P], v.weights[:, 2 * conv + 1, k, :], start=(k == 0), stop=(k == KT - 1))
                    last.then_inc(S["projected"], 1)
                pe.wait_ge(v.weights_in[2 * conv], 32 if conv == 0 else 16)
                pe.wait_ge(S["scaled"], conv * BINS + BINS)
                for t in range(BINS):
                    if t >= 4:
                        pe.wait_ge(S["row_step"], 2 * (t - 3) if conv == 0 else NB2 + 3 * (t - 3))
                    g = 2 * (t % 4)
                    for k in range(KT):
                        pe.matmul(ps[:, g, :], hT[:, k, t * P:(t + 1) * P], v.weights[:, 2 * conv, k, :], start=(k == 0), stop=(k == KT - 1))
                    for m in range(BINS):
                        last = pe.matmul(ps[:, g + 1, :], by_src[:, m, t * P:(t + 1) * P], h[:, m, :], start=(m == 0), stop=(m == BINS - 1))
                    last.then_inc(S["summed"], 1)


def relational_block(nc, a, v, out):
    z, BINS, KT, N, D, TILES, PAIRS = v.z, v.BINS, v.KT, v.N, v.D, v.TILES, v.PAIRS
    RELS, BASES = z.RELS, z.BASES
    x, h, hT, ps = v.x, v.h, v.hT, v.ps
    RING = 8
    STEPS = TILES // RING
    stage = v.by_dst[:].rearrange("p a n -> p (a n)").rearrange("p (b r d) -> p b r d", b=2, r=RELS)
    G = v.by_src[:].rearrange("p a n -> p (a n)").rearrange("p (g d) -> p g d", d=D)
    with nc.cleanup_on_exit(), ExitStack() as c0:
        comp = c0.enter_context(nc.sbuf_tensor("comp", [P, 2, RELS * BASES], F32))
        bias = c0.enter_context(nc.sbuf_tensor("bias", [P, 2, D], F32))
        loop_w = c0.enter_context(nc.sbuf_tensor("loop_w", [P, KT, D], F32))
        row_no = c0.enter_context(nc.sbuf_tensor("row_no", [P, TILES], I32))
        for layer in range(2):
            with nc.cleanup_on_exit(), ExitStack() as c:
                def sb(name, shape, dt=F32):
                    return c.enter_context(nc.sbuf_tensor(f"{name}_{layer}", shape, dt))

                def sem(name):
                    return nc.alloc_semaphore(name=f"rel{layer}_{name}")
                rel_block = relational_layer(nc, a, v, out, layer, c, sb, sem, comp, bias, loop_w, row_no, stage, G, RING, STEPS)


def relational_layer(nc, a, v, out, layer, c, sb, sem, comp, bias, loop_w, row_no, stage, G, RING, STEPS):
    z, BINS, KT, N, D, TILES = v.z, v.BINS, v.KT, v.N, v.D, v.TILES
    RELS, BASES = z.RELS, z.BASES
    x, h, hT, ps = v.x, v.h, v.hT, v.ps
    table = v.rel_table[layer]
    table_rows = table.rearrange("(r t p) d -> t p r d", r=RELS, p=P)
    nodes = [sb(f"nodes{r}", [P, 1], I32) for r in range(RING)]
    hot = [sb(f"hot{r}", [P, P]) for r in range(RING)]
    basis_in = [sem(f"basis_in{b}") for b in range(BASES)]
    rows_in = [sem(f"rows_in{r}") for r in range(RING)]
    table_out = [sem(f"table_out{b}") for b in range(2)]
    (small_in, norm_step, rooted, norm_ready, h_ready, turned, kept, based, first_term, mix_step, mixed, index_set, hot_set, tile_summed,
     row_step, relu_done, out_done, looped) = (sem(n) for n in (
         "small_in", "norm_step", "rooted", "norm_ready", "h_ready", "turned", "kept", "based", "first_term", "mix_step", "mixed", "index_set",
         "hot_set", "tile_summed", "row_step", "relu_done", "out_done", "looped"))
    blk = c.enter_context(nc.Block())
    PER = RELS * (BASES - 1)

    @blk.sync
    def _(sp):
        for b in range(BASES):
            sp.dma_start(v.weights[:, b], a[f"L3_gnn_basis{layer}"][b].rearrange("(k p) n -> p k n", p=P)).then_inc(basis_in[b], 16)
        sp.dma_start(comp[:, layer, :], broadcast_rows(a[f"L3_gnn_comp{layer}"], RELS * BASES)).then_inc(small_in, 16)
        sp.dma_start(bias[:, layer, :], broadcast_rows(a[f"L3_gnn_bias{layer}"], D)).then_inc(small_in, 16)
        sp.dma_start(loop_w[:], a[f"L3_gnn_loop{layer}"].rearrange("(k p) n -> p k n", p=P)).then_inc(small_in, 16)
        for t in range(BINS):
            sp.wait_ge(mix_step, PER * (t + 1))
            sp.dma_start(table_rows[t], stage[:, t % 2]).then_inc(table_out[t % 2], 16)
        if layer == 1:
            for t in range(BINS):
                sp.wait_ge(row_step, 2 * t + 2)
                sp.dma_start(out[t * P:(t + 1) * P, :], x[:, t, :]).then_inc(out_done, 16)
            sp.wait_ge(out_done, 16 * BINS)

    @blk.gpsimd
    def _(pool):
        if layer == 0:
            root_pool(pool, v, v.rstd[:], norm_step, 2 * BINS + 1, rooted)
        for b in range(2):
            pool.wait_ge(table_out[b], 16 * BINS // 2)
        with pool.Fori(0, STEPS) as i:
            for r in range(RING):
                pool.sem_clear(index_set)
                pool.wait_ge(tile_summed, i * RING + r + 1)
                pool.tensor_copy(nodes[r][:], row_no[:, bass.ds(i * RING + r, 1)]).then_inc(index_set, 1)
                pool.wait_ge(index_set, 1)
                pool.indirect_dma_start(out=G[:, r, :], out_offset=None, in_=table,
                                        in_offset=bass.IndirectOffsetOnAxis(ap=nodes[r][:], axis=0)).then_inc(rows_in[r], 16)

    @blk.vector
    def _(dve):
        if layer == 0:
            dve.tensor_copy(row_no[:], v.meta[:].bitcast(I32)[:, :, 3]).then_inc(looped, 1)
            layer_norm_dve(dve, v, lambda t: None, norm_step, rooted, norm_ready)
        for t in range(BINS):
            dve.wait_ge(turned, t + 1)
            dve.tensor_copy(hT[:, :, t * P:(t + 1) * P], ps[:, t % 4, :].rearrange("p (k n) -> p k n", n=P)).then_inc(kept, 1)
        for t in range(BINS):
            for b in range(1, BASES):
                for rel in range(RELS):
                    if b == 1:
                        dve.wait_ge(first_term, RELS * t + rel + 1)
                    else:
                        dve.wait_ge(mix_step, PER * t + RELS * (b - 2) + rel + 1)
                    row = stage[:, t % 2, rel, :]
                    k = rel * BASES + b
                    dve.scalar_tensor_tensor(row, ps[:, 4 * (t % 2) + b, :], comp[:, layer, k:k + 1], row, ALU.mult, ALU.add).then_inc(mix_step, 1)
        with dve.Fori(0, STEPS) as i:
            for r in range(RING):
                dve.wait_ge(tile_summed, i * RING + r + 1)
                t = bass.ds(i * RING + r, 1)
                dve.tensor_scalar(hot[r][:], v.iota1[:], v.meta[:, t, 1:2].rearrange("p a b -> p (a b)"),
                                  v.meta[:, t, 2:3].rearrange("p a b -> p (a b)"), ALU.is_equal, ALU.mult).then_inc(hot_set, 1)
        dve.wait_ge(tile_summed, TILES + RING)
        for t in range(BINS):
            rows = h if layer == 0 else x
            if layer == 0:
                dve.tensor_tensor(h[:, t, :], ps[:, t, :], bias[:, layer, :], ALU.add).then_inc(row_step, 1)
                dve.wait_ge(row_step, 2 * t + 1)
                dve.tensor_scalar(h[:, t, :], h[:, t, :], 0.0, None, ALU.max).then_inc(row_step, 1)
            else:
                dve.tensor_tensor(x[:, t, :], ps[:, t, :], x[:, t, :], ALU.add).then_inc(row_step, 1)
                dve.wait_ge(row_step, 2 * t + 1)
                dve.tensor_tensor(x[:, t, :], x[:, t, :], bias[:, layer, :], ALU.add).then_inc(row_step, 1)

    @blk.scalar
    def _(act):
        if layer == 0:
            layer_norm_act(act, v, norm_ready, h_ready)
        act.wait_ge(small_in, 48)
        for t in range(BINS):
            act.wait_ge(based, t + 1)
            if t >= 2:
                act.wait_ge(table_out[t % 2], 16 * (t // 2))
            for rel in range(RELS):
                k = rel * BASES
                act.activation(stage[:, t % 2, rel, :], ps[:, 4 * (t % 2), :], ACT.Copy, scale=comp[:, layer, k:k + 1]).then_inc(first_term, 1)

    @blk.tensor
    def _(pe):
        for t in range(BINS):
            if layer == 0:
                pe.wait_ge(h_ready, t + 1)
            if t >= 4:
                pe.wait_ge(kept, t - 3)
            for k in range(KT):
                last = pe.transpose(ps[:, t % 4, k * P:(k + 1) * P], h[:, t, k * P:(k + 1) * P], v.ident[:])
            last.then_inc(turned, 1)
        for b in range(BASES):
            pe.wait_ge(basis_in[b], 16)
        pe.wait_ge(kept, BINS)
        for t in range(BINS):
            if t >= 2:
                pe.wait_ge(mix_step, PER * (t - 1))
            for b in range(BASES):
                for k in range(KT):
                    last = pe.matmul(ps[:, 4 * (t % 2) + b, :], hT[:, k, t * P:(t + 1) * P], v.weights[:, b, k, :], start=(k == 0), stop=(k == KT - 1))
            last.then_inc(based, 1)
        pe.wait_ge(mix_step, PER * BINS)
        pe.wait_ge(small_in, 48)
        for t in range(BINS):
            for k in range(KT):
                last = pe.matmul(ps[:, t, :], hT[:, k, t * P:(t + 1) * P], loop_w[:, k, :], start=(k == 0), stop=False, skip_group_check=True)
        pe.sem_inc(tile_summed, RING)
        with pe.Fori(0, STEPS) as i:
            for r in range(RING):
                t = i * RING + r
                if r % 2 == 0:
                    b = pe.value_load(v.tile_bin[0:1, bass.ds(i * (RING // 2) + r // 2 + 1, 1)], min_val=0, max_val=BINS - 1)
                pe.wait_ge(hot_set, t + 1)
                pe.wait_ge(rows_in[r], 16 * i + 16)
                pe.matmul(ps[:, bass.ds(b, 1), :], hot[r][:], G[:, r, :], start=False, stop=False, skip_group_check=True).then_inc(tile_summed, 1)


def kernel(**inputs):
    import numpy as np
    import concourse.bacc as bacc
    from concourse.bass_utils import run_bass_kernel_spmd as run

    nc = bacc.Bacc("TRN2", target_bir_lowering=False, num_devices=1)
    arrays, aps = {}, {}
    for name, value in inputs.items():
        arr = np.ascontiguousarray(value)
        arrays[f"in_{name}"] = arr
        aps[name] = nc.dram_tensor(f"in_{name}", arr.shape, mybir.dt.from_np(arr.dtype), kind="ExternalInput").ap()
    out = nc.dram_tensor("out", inputs["x"].shape, F32, kind="ExternalOutput").ap()
    build_program(nc, aps, out)
    return run(nc, [arrays], core_ids=[0]).results[0]["out"]
```

```python
from contextlib import ExitStack

import concourse.bass as bass
from concourse import mybir

F32 = mybir.dt.float32
F32R = mybir.dt.float32r
F16 = mybir.dt.float16
BF16 = mybir.dt.bfloat16
I32 = mybir.dt.int32
ALU = mybir.AluOpType
ACT = mybir.ActivationFunctionType
AX = mybir.AxisListType

P = 128
EPS = 1e-5
SILU_2MOM = 1.679177
AVG_NEIGHBORS = 10.0
LEAK = 0.01


class Shapes:

    def __init__(self, x, src, edge_attr_8, mlp1, comp):
        self.N, self.D = x.shape
        self.E = src.shape[0]
        self.R8 = edge_attr_8.shape[1]
        self.HID = mlp1.shape[1]
        self.RELS, self.BASES = comp.shape
        self.BINS = self.N // P
        self.COLS = self.E // P
        self.PAIRS = -(-self.E // (2 * P)) + self.BINS
        self.TILES = 2 * self.PAIRS
        self.ROW = 8 + 2 * self.HID
        self.KT = self.D // P


class Shared:
    pass


def broadcast_rows(ap, n):
    return bass.AP(ap.tensor, 0, [[0, P], [1, n]])


def build_program(nc, a, out):
    z = Shapes(a["x"], a["src"], a["edge_attr_8"], a["L1_gnn_W_mlp1"], a["L3_gnn_comp0"])
    N, D, BINS, COLS, TILES, PAIRS, ROW, KT, HID = z.N, z.D, z.BINS, z.COLS, z.TILES, z.PAIRS, z.ROW, z.KT, z.HID
    assert D == 4 * P and HID == 64 and COLS % 8 == 0 and PAIRS % 4 == 0 and BINS == 8

    slots = nc.dram_tensor("edge_slots", [(TILES + 2) * P, ROW], F32).ap()
    up_table = nc.dram_tensor("up_table", [N, D], F32).ap()
    rel_table = [nc.dram_tensor(f"rel_table_{n}", [z.RELS * N, D], F32).ap() for n in range(2)]

    with ExitStack() as ctx:
        def sb(name, shape, dt=F32, c=ctx):
            return c.enter_context(nc.sbuf_tensor(name, shape, dt))

        def sem(name):
            return ctx.enter_context(nc.semaphore(name))

        ps = ctx.enter_context(nc.psum_tensor("ps", [P, 8, 512], F32))
        x = sb("x_rows", [P, BINS, D])
        h = sb("h_rows", [P, BINS, D])
        hT = sb("h_cols", [P, KT, N])
        by_src = sb("counts_by_src", [P, BINS, N])
        by_dst = sb("counts_by_dst", [P, BINS, N])
        weights = sb("weights", [P, 4, KT, D])
        meta = sb("slot_meta", [P, TILES, 8])
        ident = sb("ident", [P, P])
        iota1 = sb("iota1", [P, P])
        tile_bin = sb("tile_bin", [P, 80], I32)
        stats = sb("stats", [P, BINS, 6])
        moments = sb("moments", [P, BINS, 2])
        rstd = sb("rstd", [P, BINS])
        shift = sb("shift", [P, BINS])
        dinv_gcn = sb("dinv_gcn", [P, BINS])
        dinv_cheb = sb("dinv_cheb", [P, BINS])
        ndinv_cheb = sb("ndinv_cheb", [P, BINS])
        minus_half = sb("minus_half", [P, BINS])
        vec = sb("vec", [P, 1, D])

        x_in = sem("x_in")
        weights_in = [sem(f"weights_in{n}") for n in range(4)]
        consts = sem("consts")

        v = Shared()
        v.z = z
        v.N = N
        v.D = D
        v.BINS = BINS
        v.COLS = COLS
        v.TILES = TILES
        v.PAIRS = PAIRS
        v.ROW = ROW
        v.KT = KT
        v.HID = HID
        v.slots = slots
        v.up_table = up_table
        v.rel_table = rel_table
        v.ps = ps
        v.x = x
        v.h = h
        v.hT = hT
        v.by_src = by_src
        v.by_dst = by_dst
        v.weights = weights
        v.meta = meta
        v.ident = ident
        v.iota1 = iota1
        v.tile_bin = tile_bin
        v.stats = stats
        v.moments = moments
        v.rstd = rstd
        v.shift = shift
        v.dinv_gcn = dinv_gcn
        v.dinv_cheb = dinv_cheb
        v.ndinv_cheb = ndinv_cheb
        v.minus_half = minus_half
        v.vec = vec
        v.x_in = x_in
        v.weights_in = weights_in
        edges_block(nc, a, v)
        counts_block(nc, a, v)
        gcn_block(nc, a, v)
        tensor_product_block(nc, a, v)
        v.basis = [sb("basis0", [P, z.BASES, KT, D]), weights]
        v.loop_w = sb("loop_w", [P, KT, D])
        v.comp = sb("comp", [P, 2, z.RELS * z.BASES])
        v.rel_bias = sb("rel_bias", [P, 2, D])
        v.relational_in = [sem(f"relational_in{n}") for n in range(2)]
        v.loop_in = sem("loop_in")
        cheb_block(nc, a, v)
        relational_block(nc, a, v, out)


def load_relational(sp, a, v, layer):
    z, done = v.z, v.relational_in[layer]
    for b in range(z.BASES):
        sp.dma_start(v.basis[layer][:, b], a[f"L3_gnn_basis{layer}"][b].rearrange("(k p) n -> p k n", p=P)).then_inc(done, 16)
    sp.dma_start(v.comp[:, layer, :], broadcast_rows(a[f"L3_gnn_comp{layer}"], z.RELS * z.BASES)).then_inc(done, 16)
    sp.dma_start(v.rel_bias[:, layer, :], broadcast_rows(a[f"L3_gnn_bias{layer}"], v.D)).then_inc(done, 16)


def load_loop(sp, a, v, layer):
    sp.dma_start(v.loop_w[:], a[f"L3_gnn_loop{layer}"].rearrange("(k p) n -> p k n", p=P)).then_inc(v.loop_in, 16)


def edges_block(nc, a, v):
    z, N, BINS, COLS, TILES, PAIRS, ROW, HID = v.z, v.N, v.BINS, v.COLS, v.TILES, v.PAIRS, v.ROW, v.HID
    G = 4
    ITERS = COLS // (2 * G)
    with nc.cleanup_on_exit(), ExitStack() as c:
        def sb(name, shape, dt=F32):
            return c.enter_context(nc.sbuf_tensor(name, shape, dt))

        def sem(name):
            return nc.alloc_semaphore(name="edge_" + name)
        ps = v.ps
        dst_i, src_i, type_i, bin_i = (sb(n, [P, COLS], I32) for n in ("dst_i", "src_i", "type_i", "bin_i"))
        weight, dst_f, bin_f, pos = (sb(n, [P, COLS]) for n in ("weight", "dst_f", "bin_f", "pos"))
        y = sb("y", [P, COLS, 4])
        attr = sb("attr", [P, COLS, z.R8])
        edge_meta = sb("edge_meta", [P, COLS, 8])
        in_bin, no_carry, seen, place = (v.by_src[:, 2 * k:2 * k + 2, :].rearrange("p a n -> p (a n)")[:, 0:BINS * COLS]
                                         .rearrange("p (b j) -> p b j", j=COLS) for k in range(4))
        row_total, ones8, pairs_f, pair_end, offset = (sb(n, [P, BINS]) for n in ("row_total", "ones8", "pairs_f", "pair_end", "offset"))
        pairs_i = sb("pairs_i", [P, BINS], I32)
        lower = sb("lower", [P, P])
        ones = sb("ones", [P, P])
        pair_no = sb("pair_no", [P, PAIRS])
        passed = sb("passed", [P, PAIRS, BINS])
        bin_of = sb("bin_of", [P, PAIRS])
        zeros = sb("zeros", [P, 1024])
        w1 = sb("w1", [G * z.R8, 2, P])
        w2 = sb("w2", [P, P])
        w3 = sb("w3", [P, P])
        a8 = [sb(f"a8_{b}", [P, G * z.R8]) for b in range(2)]
        a8T = [sb(f"a8T_{b}", [G * z.R8, P]) for b in range(2)]
        h1, h2, h3 = ([sb(f"{n}_{b}", [P, 2 * P]) for b in range(2)] for n in ("h1", "h2", "h3"))
        payload = [sb(f"payload{b}", [P, G, ROW]) for b in range(2)]
        row_f = [sb(f"row_f{b}", [P, G], I32) for b in range(2)]
        row_i = [sb(f"row_i{b}", [P, G], I32) for b in range(2)]
        zero_g = sb("zero_g", [P, G], I32)

        dst_in, edges_in, blocks_zero, mlp_in = sem("dst_in"), sem("edges_in"), sem("blocks_zero"), sem("mlp_in")
        scattered = [sem(f"scattered{b}") for b in range(2)]
        zeros_set, slots_zeroed, index_step, totals_ready, pool_step = sem("zeros_set"), sem("slots_zeroed"), sem("index_step"), sem("totals_ready"), sem("pool_step")
        places_done, parts_done, staged, attr_turned, attr_cols = sem("places_done"), sem("parts_done"), sem("staged"), sem("attr_turned"), sem("attr_cols")
        pre_act, acted, hidden_turned, packed, rows_set = sem("pre_act"), sem("acted"), sem("hidden_turned"), sem("packed"), sem("rows_set")
        row_total_at = []
        zero_dmas = -(-(TILES + 2) * ROW // 2048)
        blk = c.enter_context(nc.Block())

        @blk.sync
        def _(sp):
            sp.dma_start(dst_i[:], a["dst"].rearrange("(p j) -> p j", p=P)).then_inc(dst_in, 16)
            sp.dma_start(attr[:], a["edge_attr_8"].rearrange("(p j) r -> p j r", p=P)).then_inc(edges_in, 16)
            sp.dma_start(src_i[:], a["src"].rearrange("(p j) -> p j", p=P)).then_inc(edges_in, 16)
            sp.dma_start(type_i[:], a["edge_type_8"].rearrange("(p j) -> p j", p=P)).then_inc(edges_in, 16)
            sp.dma_start(weight[:], a["edge_weight"].rearrange("(p j) -> p j", p=P)).then_inc(edges_in, 16)
            sp.dma_start(y[:], a["edge_attr_4"].rearrange("(p j) r -> p j r", p=P)).then_inc(edges_in, 16)
            sp.wait_ge(zeros_set, 1)
            flat = v.slots.rearrange("(p q) r -> p (q r)", p=P)
            per = flat.shape[1]
            half = per // 2
            for b in range(2):
                cuts = list(range(b * half, (b + 1) * half, 1024)) + [(b + 1) * half]
                assert per % 2 == 0
                for lo, hi in zip(cuts, cuts[1:]):
                    sp.dma_start(flat[:, lo:hi], zeros[:, 0:hi - lo]).then_inc(slots_zeroed, 16)
            sp.dma_start(v.x[:], a["x"].rearrange("(t p) d -> p t d", p=P)).then_inc(v.x_in, 16)
            sp.dma_start(v.weights[:, 0], a["L0_gnn_weight"].rearrange("(k p) n -> p k n", p=P)).then_inc(v.weights_in[0], 16)
            sp.dma_start(v.vec[:, 0, :], broadcast_rows(a["L0_gnn_bias"], v.D)).then_inc(v.weights_in[0], 16)
            for b in range(2):
                sp.wait_ge(scattered[b], 16 * G * ITERS)

        @blk.gpsimd
        def _(pool):
            pool.memset(zeros[:], 0.0).then_inc(zeros_set, 1)
            pool.memset(v.ident[:], 0.0).then_inc(pool_step, 1)
            pool.memset(ones[:], 1.0).then_inc(pool_step, 1)
            pool.memset(lower[:], 1.0).then_inc(pool_step, 1)
            pool.memset(no_carry, 1.0).then_inc(pool_step, 1)
            pool.memset(ones8[:], 1.0).then_inc(pool_step, 1)
            pool.memset(v.minus_half[:], -0.5).then_inc(pool_step, 1)
            pool.memset(zero_g[:], 0).then_inc(pool_step, 1)
            pool.wait_ge(pool_step, 7)
            pool.affine_select(out=v.ident[:], in_=v.ident[:], compare_op=ALU.not_equal, fill=1.0, base=0,
                               pattern=[[-1, P]], channel_multiplier=1).then_inc(pool_step, 1)
            pool.affine_select(out=lower[:], in_=lower[:], compare_op=ALU.is_gt, fill=0.0, base=0,
                               pattern=[[1, P]], channel_multiplier=-1).then_inc(pool_step, 1)
            pool.memset(no_carry[:, :, 0:1], 0.0).then_inc(pool_step, 1)
            pool.iota(v.iota1[:], pattern=[[1, P]], base=1, channel_multiplier=0,
                      allow_small_or_imprecise_dtypes=True).then_inc(pool_step, 1)
            pool.iota(pair_no[:], pattern=[[1, PAIRS]], base=0, channel_multiplier=0,
                      allow_small_or_imprecise_dtypes=True).then_inc(pool_step, 1)
            pool.memset(w1[:], 0.0).then_inc(blocks_zero, 1)
            pool.memset(w2[:], 0.0).then_inc(blocks_zero, 1)
            pool.memset(w3[:], 0.0).then_inc(blocks_zero, 1)
            pool.wait_ge(slots_zeroed, 2 * 16 * zero_dmas)
            with pool.Fori(0, ITERS) as i:
                for b in range(2):
                    pool.sem_clear(rows_set)
                    pool.wait_ge(packed, 4 * i + 2 * b + 2)
                    pool.tensor_tensor(row_i[b][:], row_f[b][:], zero_g[:], ALU.add).then_inc(rows_set, 1)
                    pool.wait_ge(rows_set, 1)
                    for k in range(G):
                        pool.indirect_dma_start(out=v.slots, out_offset=bass.IndirectOffsetOnAxis(ap=row_i[b][:, k:k + 1], axis=0),
                                                in_=payload[b][:, k, :], in_offset=None).then_inc(scattered[b], 16)

        @blk.vector
        def _(dve):
            steps = [0]

            def step(ins):
                steps[0] += 1
                ins.then_inc(index_step, 1)
                dve.wait_ge(index_step, steps[0])

            dve.wait_ge(dst_in, 16)
            dve.tensor_scalar(bin_i[:], dst_i[:], 7, None, ALU.arith_shift_right).then_inc(index_step, 1)
            dve.tensor_copy(dst_f[:], dst_i[:]).then_inc(index_step, 1)
            steps[0] += 2
            dve.wait_ge(index_step, steps[0])
            step(dve.tensor_copy(bin_f[:], bin_i[:]))
            for b in range(BINS):
                ins = dve.tensor_scalar(in_bin[:, b, :], bin_f[:], float(b), None, ALU.is_equal)
                ins.then_inc(index_step, 1)
                steps[0] += 1
            dve.wait_ge(index_step, steps[0])
            dve.wait_ge(pool_step, 12)
            step(dve.tensor_tensor_scan(seen.rearrange("p b j -> p (b j)"), no_carry.rearrange("p b j -> p (b j)"),
                                        in_bin.rearrange("p b j -> p (b j)"), 0.0, ALU.mult, ALU.add))
            dve.tensor_copy(row_total[:], seen[:, :, COLS - 1]).then_inc(index_step, 1)
            steps[0] += 1
            row_total_at.append(steps[0])
            dve.wait_ge(totals_ready, 1)
            step(dve.tensor_scalar(pairs_f[:], ps[:, 0, 8:16], float(2 * P - 1), None, ALU.add))
            step(dve.tensor_copy(pairs_i[:], pairs_f[:]))
            step(dve.tensor_scalar(pairs_i[:], pairs_i[:], 8, None, ALU.arith_shift_right))
            step(dve.tensor_copy(pairs_f[:], pairs_i[:]))
            step(dve.tensor_tensor_scan(pair_end[:], ones8[:], pairs_f[:], 0.0, ALU.mult, ALU.add))
            step(dve.tensor_tensor(offset[:], pair_end[:], pairs_f[:], ALU.subtract))
            step(dve.tensor_scalar(offset[:], offset[:], float(2 * P), -1.0, ALU.mult, ALU.add))
            step(dve.tensor_tensor(offset[:], offset[:], ps[:, 0, 0:8], ALU.add))
            for b in range(BINS):
                dve.scalar_tensor_tensor(place[:, b, :], seen[:, b, :], offset[:, b:b + 1], in_bin[:, b, :],
                                         ALU.add, ALU.mult).then_inc(index_step, 1)
                steps[0] += 1
            dve.wait_ge(index_step, steps[0])
            step(dve.tensor_reduce(pos[:], place.rearrange("p b j -> p j b"), AX.X, ALU.add))
            step(dve.tensor_tensor(passed[:], pair_no[:].unsqueeze(2).to_broadcast([P, PAIRS, BINS]),
                                   pair_end[:].unsqueeze(1).to_broadcast([P, PAIRS, BINS]), ALU.is_ge))
            step(dve.tensor_reduce(bin_of[:], passed[:], AX.X, ALU.add))
            step(dve.tensor_scalar(bin_of[:], bin_of[:], float(BINS - 1), None, ALU.min))
            dve.memset(v.tile_bin[:], 0).then_inc(index_step, 1)
            steps[0] += 1
            dve.wait_ge(index_step, steps[0])
            step(dve.tensor_copy(v.tile_bin[:, 1:PAIRS + 1], bin_of[:]))
            dve.wait_ge(edges_in, 80)
            em = edge_meta
            em_i = edge_meta[:].bitcast(I32)
            dve.tensor_copy(em_i[:, :, 0], src_i[:]).then_inc(index_step, 1)
            dve.scalar_tensor_tensor(em[:, :, 1], bin_f[:], float(-P), dst_f[:], ALU.mult, ALU.add).then_inc(index_step, 1)
            dve.tensor_copy(em[:, :, 2], weight[:]).then_inc(index_step, 1)
            dve.scalar_tensor_tensor(em_i[:, :, 3], type_i[:], float(N), src_i[:], ALU.mult, ALU.add).then_inc(index_step, 1)
            dve.tensor_copy(em[:, :, 4:8], y[:]).then_inc(index_step, 1)
            steps[0] += 5
            dve.wait_ge(index_step, steps[0])
            dve.tensor_scalar(em[:, :, 1], em[:, :, 1], 1.0, None, ALU.add).then_inc(index_step, 1)
            steps[0] += 1
            dve.wait_ge(index_step, steps[0])

            def pack(i, scattered_before):
                for b in range(2):
                    cols = bass.ds(i * (2 * G) + b * G, G)
                    dve.tensor_copy(a8[b][:].rearrange("p (j r) -> p j r", r=z.R8), attr[:, cols, :]).then_inc(staged, 1)
                for b in range(2):
                    cols = bass.ds(i * (2 * G) + b * G, G)
                    if scattered_before:
                        dve.wait_ge(scattered[b], 16 * G * i)
                    dve.tensor_copy(row_f[b][:], pos[:, cols]).then_inc(packed, 1)
                    dve.wait_ge(hidden_turned, 2 * i + b + 1)
                    hid = ps[:, 4 * b + 3, 0:G * HID].rearrange("p (j h) -> p j h", h=HID)
                    dve.tensor_copy(payload[b][:, :, 8:8 + HID].bitcast(F32R), hid).then_inc(parts_done, 1)
                    dve.tensor_copy(payload[b][:, :, 0:8], edge_meta[:, cols, :]).then_inc(places_done, 1)
                    dve.wait_ge(parts_done, 2 * i + b + 1)
                    dve.tensor_tensor(payload[b][:, :, 8 + HID:ROW], hid, payload[b][:, :, 8:8 + HID], ALU.subtract).then_inc(packed, 1)

            pack(0, False)
            with dve.Fori(1, ITERS) as i:
                pack(i, True)

        @blk.tensor
        def _(pe):
            pe.wait_ge(pool_step, 12)
            pe.wait_ge(index_step, row_total_at[0])
            pe.matmul(ps[:, 0, 0:8], lower[:], row_total[:], start=True, stop=True)
            pe.matmul(ps[:, 0, 8:16], ones[:], row_total[:], start=True, stop=True).then_inc(totals_ready, 1)
            pe.wait_ge(mlp_in, 16 * (G + 4))
            with pe.Fori(0, ITERS) as i:
                for b in range(2):
                    pe.wait_ge(staged, 2 * i + b + 1)
                    pe.transpose(ps[0:G * z.R8, 4 * b, 0:P], a8[b][:], v.ident[:]).then_inc(attr_turned, 1)
                for b in range(2):
                    pe.wait_ge(attr_cols, 2 * i + b + 1)
                    for jj in range(2):
                        last = pe.matmul(ps[:, 4 * b + 1, jj * P:(jj + 1) * P], w1[:, jj, :], a8T[b][:], start=True, stop=True)
                    last.then_inc(pre_act, 1)
                for layer, (w, hin, bank) in enumerate(((w2, h1, 2), (w3, h2, 1))):
                    for b in range(2):
                        pe.wait_ge(acted, 6 * i + 2 * layer + b + 1)
                        pe.matmul(ps[:, 4 * b + bank, 0:2 * P], w[:], hin[b][:], start=True, stop=True).then_inc(pre_act, 1)
                for b in range(2):
                    pe.wait_ge(acted, 6 * i + 4 + b + 1)
                    for jj in range(2):
                        last = pe.transpose(ps[:, 4 * b + 3, jj * P:(jj + 1) * P], h3[b][:, jj * P:(jj + 1) * P], v.ident[:])
                    last.then_inc(hidden_turned, 1)

        @blk.scalar
        def _(act):
            act.wait_ge(blocks_zero, 3)
            for j in range(G):
                act.dma_start(w1[j * z.R8:(j + 1) * z.R8, j // 2, (j % 2) * HID:(j % 2 + 1) * HID], a["L1_gnn_W_mlp1"]).then_inc(mlp_in, 16)
            for w, name in ((w2, "L1_gnn_W_mlp2"), (w3, "L1_gnn_W_mlp3")):
                for k in range(2):
                    act.dma_start(w[k * HID:(k + 1) * HID, k * HID:(k + 1) * HID], a[name]).then_inc(mlp_in, 16)
            with act.Fori(0, ITERS) as i:
                for b in range(2):
                    act.wait_ge(attr_turned, 2 * i + b + 1)
                    act.activation(a8T[b][:], ps[0:G * z.R8, 4 * b, 0:P], ACT.Copy).then_inc(attr_cols, 1)
                for layer, (hout, bank, scale) in enumerate(((h1, 1, z.R8 ** -0.5), (h2, 2, SILU_2MOM * HID ** -0.5), (h3, 1, SILU_2MOM * HID ** -0.5))):
                    for b in range(2):
                        act.wait_ge(pre_act, 6 * i + 2 * layer + b + 1)
                        act.activation(hout[b][:], ps[:, 4 * b + bank, 0:2 * P], ACT.Silu, scale=scale).then_inc(acted, 1)



def counts_block(nc, a, v):
    z, BINS, TILES, PAIRS, ROW = v.z, v.BINS, v.TILES, v.PAIRS, v.ROW
    HALF = v.N // 2
    SET = 4
    SETS = TILES // SET
    STEPS = SETS // 2
    with nc.cleanup_on_exit(), ExitStack() as c:
        def sb(name, shape, dt=F32):
            return c.enter_context(nc.sbuf_tensor(name, shape, dt))

        def sem(name):
            return nc.alloc_semaphore(name="count_" + name)
        ps = v.ps
        node_no = sb("node_no", [P, v.N], F16)
        src_f = sb("src_f", [P, TILES])
        zero_b = sb("zero_b", [P, HALF], BF16)
        src_hot = [sb(f"src_hot{b}", [P, SET, HALF], BF16) for b in range(2)]
        dst_hot = sb("dst_hot", [P, TILES, P], BF16)
        place_no = sb("place_no", [P, P], F16)
        dst_h = sb("dst_h", [P, TILES], F16)
        meta_in, set_up, src_set, dst_set, hot_used, half_summed, half_kept, src_ready = (
            sem(n) for n in ("meta_in", "set_up", "src_set", "dst_set", "hot_used", "half_summed", "half_kept", "src_ready"))
        blk = c.enter_context(nc.Block())

        @blk.sync
        def _(sp):
            with nc.allow_non_contiguous_dma(reason="slot meta"):
                sp.dma_start(v.meta[:], v.slots[0:TILES * P, 0:8].rearrange("(t p) r -> p t r", p=P)).then_inc(meta_in, 16)

        @blk.gpsimd
        def _(pool):
            pool.iota(node_no[:], pattern=[[1, v.N]], base=0, channel_multiplier=0,
                      allow_small_or_imprecise_dtypes=True).then_inc(set_up, 1)
            pool.memset(zero_b[:], 0.0).then_inc(set_up, 1)
            pool.iota(place_no[:], pattern=[[1, P]], base=1, channel_multiplier=0,
                      allow_small_or_imprecise_dtypes=True).then_inc(set_up, 1)

        @blk.vector
        def _(dve):
            dve.wait_ge(meta_in, 16)
            dve.tensor_copy(src_f[:], v.meta[:].bitcast(I32)[:, :, 0]).then_inc(src_ready, 1)
            dve.tensor_copy(dst_h[:], v.meta[:, :, 1]).then_inc(src_ready, 1)
            dve.wait_ge(src_ready, 2)
            dve.wait_ge(set_up, 3)
            for half in range(2):
                with dve.Fori(0, STEPS) as i:
                    if half == 0:
                        tiles = bass.ds(2 * SET * i, 2 * SET)
                        dve.tensor_tensor(dst_hot[:, tiles, :], place_no[:].unsqueeze(1).to_broadcast([P, 2 * SET, P]),
                                          dst_h[:, tiles].unsqueeze(2).to_broadcast([P, 2 * SET, P]), ALU.is_equal).then_inc(dst_set, 1)
                    for b in range(2):
                        dve.wait_ge(hot_used, half * SETS + 2 * i + b + 1)
                        for k in range(SET):
                            last = dve.tensor_scalar(src_hot[b][:, k, :], node_no[:, half * HALF:(half + 1) * HALF],
                                                     src_f[:, bass.ds((2 * i + b) * SET + k, 1)], None, ALU.is_equal)
                            last.then_inc(src_set, 1)
                dve.wait_ge(half_summed, half + 1)
                for b in range(0, BINS, 2):
                    dve.tensor_copy(v.by_dst[:, b, half * HALF:(half + 1) * HALF], ps[:, b, :]).then_inc(half_kept, 1)

        @blk.scalar
        def _(act):
            for half in range(2):
                act.wait_ge(half_summed, half + 1)
                for b in range(1, BINS, 2):
                    act.activation(v.by_dst[:, b, half * HALF:(half + 1) * HALF], ps[:, b, :], ACT.Copy).then_inc(half_kept, 1)

        @blk.tensor
        def _(pe):
            bins = [pe.alloc_register(f"count_bin{k}") for k in range(SET)]
            pe.wait_ge(set_up, 3)
            pe.sem_inc(hot_used, 2)
            for half in range(2):
                if half:
                    pe.wait_ge(half_kept, BINS * half)
                for b in range(BINS):
                    pe.matmul(ps[:, b, :], zero_b[:, 0:P], zero_b[:], start=True, stop=False, skip_group_check=True)
                with pe.Fori(0, STEPS) as i:
                    pe.load(bins, v.tile_bin[0:1, bass.ds(i * SET + 1, SET)])
                    at = [pe.snap(reg, min_val=0, max_val=BINS - 1) for reg in bins]
                    for b in range(2):
                        if half == 0 and b == 0:
                            pe.wait_ge(dst_set, i + 1)
                        pe.wait_ge(src_set, SET * (half * SETS + 2 * i + b + 1))
                        for k in range(SET):
                            last = pe.matmul(ps[:, bass.ds(at[2 * b + k // 2], 1), :], dst_hot[:, bass.ds((2 * i + b) * SET + k, 1), :].rearrange("p a n -> p (a n)"), src_hot[b][:, k, :],
                                             start=False, stop=False, skip_group_check=True)
                        last.then_inc(hot_used, 1)
                pe.matmul(ps[:, 0, :], zero_b[:, 0:P], zero_b[:], start=False, stop=True, skip_group_check=True).then_inc(half_summed, 1)


def layer_norm_dve(dve, v, rows_ready, norm_step, rooted, norm_ready):
    for t in range(v.BINS):
        rows_ready(t)
        dve.bn_stats(v.stats[:, t, :], v.x[:, t, :]).then_inc(norm_step, 1)
    for t in range(v.BINS):
        dve.wait_ge(norm_step, t + 1)
        dve.bn_aggr(v.moments[:, t, :], v.stats[:, t, :]).then_inc(norm_step, 1)
    n = 2 * v.BINS
    dve.wait_ge(norm_step, n)
    dve.tensor_scalar(v.rstd[:], v.moments[:, :, 1], EPS, None, ALU.add).then_inc(norm_step, 1)
    dve.wait_ge(rooted, 1)
    dve.scalar_tensor_tensor(v.shift[:], v.moments[:, :, 0], -1.0, v.rstd[:], ALU.mult, ALU.mult).then_inc(norm_ready, 1)


def root_pool(pool, v, values, done, at, rooted):
    pool.wait_ge(done, at)
    pool.tensor_tensor(values, values, v.minus_half[:, 0:values.shape[1]], ALU.pow).then_inc(rooted, 1)


def layer_norm_act(act, v, norm_ready, h_ready):
    act.wait_ge(norm_ready, 1)
    for t in range(v.BINS):
        act.activation(v.h[:, t, :], v.x[:, t, :], ACT.Relu, bias=v.shift[:, t:t + 1], scale=v.rstd[:, t:t + 1]).then_inc(h_ready, 1)


def transposes_pe(pe, v, blocks, banks, h_ready, h_base, turned, kept, kept_base):
    for t in range(v.BINS):
        pe.wait_ge(h_ready, h_base + t + 1)
        if t >= len(banks):
            pe.wait_ge(kept, kept_base + t - len(banks) + 1)
        for k, block in enumerate(blocks(t)):
            last = pe.transpose(v.ps[:, banks[t % len(banks)], k * P:(k + 1) * P], block, v.ident[:])
        last.then_inc(turned, 1)


def gcn_block(nc, a, v):
    z, BINS, KT, N = v.z, v.BINS, v.KT, v.N
    with nc.cleanup_on_exit(), ExitStack() as c:
        def sem(name):
            return nc.alloc_semaphore(name="gcn_" + name)

        def sb(name, shape, dt=F32):
            return c.enter_context(nc.sbuf_tensor(name, shape, dt))
        ps, x, h, hT, by_src, by_dst = v.ps, v.x, v.h, v.hT, v.by_src, v.by_dst
        out_degree = sb("out_degree", [P, 8])
        has_out = sb("has_out", [P, 8])
        (norm_step, rooted, norm_ready, h_ready, turned, kept, projected, h_kept, counts_turned, counts_kept, adj_step, adj_ready,
         scaled, summed, row_step, x_kept, degree_step) = (sem(n) for n in (
             "norm_step", "rooted", "norm_ready", "h_ready", "turned", "kept", "projected", "h_kept", "counts_turned", "counts_kept",
             "adj_step", "adj_ready", "scaled", "summed", "row_step", "x_kept", "degree_step"))
        blk = c.enter_context(nc.Block())

        @blk.sync
        def _(sp):
            sp.wait_ge(projected, BINS)

        @blk.gpsimd
        def _(pool):
            root_pool(pool, v, v.rstd[:], norm_step, 2 * BINS + 1, rooted)
            root_pool(pool, v, v.dinv_gcn[:], adj_step, 4 * BINS, rooted)
            root_pool(pool, v, v.dinv_cheb[:], degree_step, 1, rooted)

        @blk.vector
        def _(dve):
            layer_norm_dve(dve, v, lambda t: dve.wait_ge(v.x_in, 16), norm_step, rooted, norm_ready)
            for t in range(BINS):
                dve.wait_ge(turned, t + 1)
                dve.tensor_copy(hT[:, :, t * P:(t + 1) * P], ps[:, t % 4, :].rearrange("p (k n) -> p k n", n=P)).then_inc(kept, 1)
            dve.wait_ge(counts_kept, BINS)
            for t in range(BINS):
                dve.tensor_tensor(by_dst[:, t, :], by_dst[:, t, :], by_src[:, t, :], ALU.add).then_inc(adj_step, 1)
            for t in range(BINS):
                dve.wait_ge(adj_step, t + 1)
                dve.tensor_scalar(by_dst[:, t, :], by_dst[:, t, :], 1.0, None, ALU.min).then_inc(adj_step, 1)
            for t in range(BINS):
                dve.wait_ge(adj_step, BINS + t + 1)
                dve.tensor_tensor(by_dst[:, t, t * P:(t + 1) * P], by_dst[:, t, t * P:(t + 1) * P], v.ident[:], ALU.add).then_inc(adj_step, 1)
            for t in range(BINS):
                dve.wait_ge(adj_step, 2 * BINS + t + 1)
                dve.reduce_sum(v.dinv_gcn[:, t:t + 1], by_dst[:, t, :], AX.X).then_inc(adj_step, 1)
            dve.tensor_scalar(v.dinv_cheb[:], out_degree[:], 1.0, None, ALU.max).then_inc(degree_step, 1)
            dve.wait_ge(rooted, 3)
            dve.tensor_scalar(has_out[:], out_degree[:], 0.0, None, ALU.is_gt).then_inc(degree_step, 1)
            dve.wait_ge(degree_step, 2)
            dve.tensor_tensor(v.dinv_cheb[:], v.dinv_cheb[:], has_out[:], ALU.mult).then_inc(degree_step, 1)
            dve.wait_ge(degree_step, 3)
            dve.tensor_scalar(v.ndinv_cheb[:], v.dinv_cheb[:], -1.0, None, ALU.mult).then_inc(degree_step, 1)
            for t in range(BINS):
                dve.wait_ge(summed, t + 1)
                dve.scalar_tensor_tensor(x[:, t, :], ps[:, t, :], v.dinv_gcn[:, t:t + 1], x[:, t, :], ALU.mult, ALU.add).then_inc(row_step, 1)
                dve.wait_ge(row_step, t + 1)
                dve.tensor_tensor(x[:, t, :], x[:, t, :], v.vec[:, 0, :], ALU.add).then_inc(x_kept, 1)

        @blk.scalar
        def _(act):
            layer_norm_act(act, v, norm_ready, h_ready)
            for t in range(BINS):
                act.wait_ge(projected, t + 1)
                act.activation(h[:, t, :], ps[:, 4 + t % 4, :], ACT.Copy).then_inc(h_kept, 1)
            for t in range(BINS):
                act.wait_ge(counts_turned, t + 1)
                g = 2 * (t % 4)
                act.activation(by_src[:, t, :], ps[:, g:g + 2, :].rearrange("p a n -> p (a n)"), ACT.Copy,
                               accum_out=out_degree[:, t:t + 1]).then_inc(counts_kept, 1)
            act.wait_ge(rooted, 2)
            for t in range(BINS):
                act.activation(h[:, t, :], h[:, t, :], ACT.Copy, scale=v.dinv_gcn[:, t:t + 1]).then_inc(scaled, 1)

        @blk.tensor
        def _(pe):
            transposes_pe(pe, v, lambda t: [h[:, t, k * P:(k + 1) * P] for k in range(KT)], [0, 1, 2, 3], h_ready, 0, turned, kept, 0)
            pe.wait_ge(v.weights_in[0], 32)
            for t in range(BINS):
                pe.wait_ge(kept, t + 1)
                if t >= 4:
                    pe.wait_ge(h_kept, t - 3)
                for k in range(KT):
                    last = pe.matmul(ps[:, 4 + t % 4, :], hT[:, k, t * P:(t + 1) * P], v.weights[:, 0, k, :], start=(k == 0), stop=(k == KT - 1))
                last.then_inc(projected, 1)
            pe.wait_ge(h_kept, BINS)
            for t in range(BINS):
                if t >= 4:
                    pe.wait_ge(counts_kept, t - 3)
                for b in range(BINS):
                    last = pe.transpose(ps[:, 2 * (t % 4) + b // 4, (b % 4) * P:(b % 4 + 1) * P], by_dst[:, b, t * P:(t + 1) * P], v.ident[:])
                last.then_inc(counts_turned, 1)
            pe.wait_ge(scaled, BINS)
            for t in range(BINS):
                for m in range(BINS):
                    last = pe.matmul(ps[:, t, :], by_dst[:, m, t * P:(t + 1) * P], h[:, m, :], start=(m == 0), stop=(m == BINS - 1))
                last.then_inc(summed, 1)


def tensor_product_block(nc, a, v):
    z, BINS, KT, N, D, PAIRS, ROW, HID = v.z, v.BINS, v.KT, v.N, v.D, v.PAIRS, v.ROW, v.HID
    RING = 4
    Y = range(4)
    acc = v.by_dst
    x, h, hT, ps = v.x, v.h, v.hT, v.ps
    with nc.cleanup_on_exit(), ExitStack() as c0:
        def sb0(name, shape, dt=F32):
            return c0.enter_context(nc.sbuf_tensor(name, shape, dt))

        def sem0(name):
            return nc.alloc_semaphore(name="sum_" + name)
        up = sb0("w_up", [P, 2, P])
        w4 = sb0("w_mlp4", [P, D])
        w4_parts = sb0("w_mlp4_parts", [P, 2, D], F32R)
        wo = sb0("w_out", [P, 2, 2, P])
        rows = sb0("up_rows", [P, 2, D])
        tp_weights, w_step, w_scaled = sem0("tp_weights"), sem0("w_step"), sem0("w_scaled")

        with nc.cleanup_on_exit(), ExitStack() as c:
            def sem(name):
                return nc.alloc_semaphore(name="sum_" + name)
            norm_step, rooted, norm_ready, h_ready, turned, kept, projected, staged, table_out = (sem(n) for n in (
                "tp_norm_step", "tp_rooted", "tp_norm_ready", "tp_h_ready", "tp_turned", "tp_kept", "tp_projected", "tp_staged", "table_out"))
            blk = c.enter_context(nc.Block())

            @blk.sync
            def _(sp):
                sp.dma_start(up[:, 0, :], a["L1_gnn_W_up0"]).then_inc(tp_weights, 16)
                sp.dma_start(up[:, 1, :], a["L1_gnn_W_up1"]).then_inc(tp_weights, 16)
                sp.dma_start(w4[0:HID, :], a["L1_gnn_W_mlp4"]).then_inc(tp_weights, 16)
                sp.dma_start(w4[HID:P, :], a["L1_gnn_W_mlp4"]).then_inc(tp_weights, 16)
                sp.dma_start(wo[:, 0], a["L1_gnn_W_out0"].rearrange("(q u) n -> u q n", u=P)).then_inc(tp_weights, 16)
                sp.dma_start(wo[:, 1], a["L1_gnn_W_out1"].rearrange("(q u) n -> u q n", u=P)).then_inc(tp_weights, 16)
                for t in range(BINS):
                    sp.wait_ge(staged, t + 1)
                    sp.dma_start(v.up_table[t * P:(t + 1) * P, :], rows[:, t % 2, :]).then_inc(table_out, 16)
                    sp.wait_ge(table_out, 16 * (t + 1))
                for n, name in enumerate(("L2_gnn_W1_0", "L2_gnn_W1_1", "L2_gnn_W2_0", "L2_gnn_W2_1")):
                    sp.dma_start(v.weights[:, n], a[name].rearrange("(k p) n -> p k n", p=P)).then_inc(v.weights_in[n], 16)

            @blk.vector
            def _(dve):
                layer_norm_dve(dve, v, lambda t: None, norm_step, rooted, norm_ready)
                for t in range(BINS):
                    dve.wait_ge(turned, t + 1)
                    dve.tensor_copy(hT[:, :, t * P:(t + 1) * P], ps[:, t % 4, :].rearrange("p (k n) -> p k n", n=P)).then_inc(kept, 1)
                for t in range(BINS):
                    dve.wait_ge(projected, t + 1)
                    if t >= 2:
                        dve.wait_ge(table_out, 16 * (t - 1))
                    dve.tensor_scalar(rows[:, t % 2, :], ps[:, 4 + t % 4, :], P ** -0.5, None, ALU.mult).then_inc(staged, 1)

            @blk.gpsimd
            def _(pool):
                root_pool(pool, v, v.rstd[:], norm_step, 2 * BINS + 1, rooted)
                pool.memset(acc[:], 0.0).then_inc(w_step, 1)
                pool.wait_ge(w_scaled, 2)
                pool.tensor_copy(w4_parts[:, 0, :], w4[:]).then_inc(w_scaled, 1)
                pool.wait_ge(w_scaled, 3)
                pool.tensor_tensor(w4_parts[:, 1, :], w4[:], w4_parts[:, 0, :].bitcast(F32), ALU.subtract).then_inc(w_step, 1)

            @blk.scalar
            def _(act):
                layer_norm_act(act, v, norm_ready, h_ready)
                act.wait_ge(tp_weights, 96)
                c4 = SILU_2MOM * HID ** -0.5
                co = (2 * P) ** -0.5 / AVG_NEIGHBORS
                act.activation(w4[:, 0:3 * P], w4[:, 0:3 * P], ACT.Copy, scale=c4).then_inc(w_scaled, 1)
                act.activation(w4[:, 3 * P:], w4[:, 3 * P:], ACT.Copy, scale=c4 * 3.0 ** -0.5).then_inc(w_scaled, 1)
                act.activation(wo[:].rearrange("p a q n -> p (a q n)"), wo[:].rearrange("p a q n -> p (a q n)"), ACT.Copy, scale=co).then_inc(w_step, 1)

            @blk.tensor
            def _(pe):
                transposes_pe(pe, v, lambda t: [h[:, t, 0:P]] + [h[:, t, P + m:D:3] for m in range(3)], [0, 1, 2, 3],
                              h_ready, 0, turned, kept, 0)
                pe.wait_ge(tp_weights, 96)
                for t in range(BINS):
                    pe.wait_ge(kept, t + 1)
                    if t >= 4:
                        pe.wait_ge(staged, t - 3)
                    for k in range(4):
                        last = pe.matmul(ps[:, 4 + t % 4, k * P:(k + 1) * P], hT[:, k, t * P:(t + 1) * P], up[:, min(k, 1), :], start=True, stop=True)
                    last.then_inc(projected, 1)

        with nc.cleanup_on_exit(), ExitStack() as c:
            def sb(name, shape, dt=F32):
                return c.enter_context(nc.sbuf_tensor(name, shape, dt))

            def sem(name):
                return nc.alloc_semaphore(name="sum_" + name)
            G = hT[:].rearrange("p k n -> p (k n)").rearrange("p (r q d) -> p r q d", r=RING, q=2)
            slot = [sb(f"slot{r}", [P, 2, ROW]) for r in range(RING)]
            nodes = [[sb(f"nodes{r}{q}", [P, 1], I32) for q in range(2)] for r in range(RING)]
            zero1 = sb("zero1", [P, 1], I32)
            hidT = [sb(f"hidT{b}", [P, 2, P], F32R) for b in range(2)]
            hot = [[sb(f"hot{r}{q}", [P, P]) for q in range(2)] for r in range(RING)]
            hot_y = [[sb(f"hot_y{b}{q}", [P, 4, P]) for q in range(2)] for b in range(2)]
            dots = [[sb(f"dots{b}{q}", [P, P]) for q in range(2)] for b in range(2)]
            msg = [[sb(f"msg{b}{q}", [P, 6, P]) for q in range(2)] for b in range(2)]
            fT = [sb(f"fT{b}", [P, 8, P]) for b in range(2)]
            slot_in = [sem(f"slot_in{r}") for r in range(RING)]
            rows_in = [sem(f"rows_in{r}") for r in range(RING)]
            (slot_free, index_set, pool_set, hid_turned, hid_kept, weighted, hot_set, hot_scaled, dot_step, msg_done, summed, added,
             f_turned, f_kept, mixed, x_step, vector_msg, gathers_free) = (sem(n) for n in (
                 "slot_free", "index_set", "pool_set", "hid_turned", "hid_kept", "weighted", "hot_set", "hot_scaled", "dot_step",
                 "msg_done", "summed", "added", "f_turned", "f_kept", "mixed", "x_step", "vector_msg", "gathers_free"))
            STEPS = PAIRS // RING
            blk = c.enter_context(nc.Block())
            acc_banks = lambda b: ps[:, 4 + 2 * b:6 + 2 * b, :]

            @blk.sync
            def _(sp):
                view = v.slots.rearrange("(s q p) r -> s p q r", q=2, p=P)

                def load(r, pair):
                    sp.dma_start(slot[r][:], pair).then_inc(slot_in[r], 16)

                for r in range(RING):
                    load(r, view[r])
                with sp.Fori(0, STEPS - 1) as i:
                    for r in range(RING):
                        sp.wait_ge(msg_done, 8 * i + 2 * r + 2)
                        sp.wait_ge(hot_scaled, 8 * i + 2 * r + 2)
                        load(r, view[bass.ds((i + 1) * RING + r, 1)].rearrange("a p q r -> p (a q) r"))

            @blk.gpsimd
            def _(pool):
                pool.memset(zero1[:], 0).then_inc(pool_set, 1)
                pool.wait_ge(pool_set, 1)
                with pool.Fori(0, STEPS) as i:
                    for r in range(RING):
                        pool.sem_clear(index_set)
                        pool.wait_ge(gathers_free, 4 * i + r + 1)
                        pool.wait_ge(slot_in[r], 16 * i + 16)
                        for q in range(2):
                            pool.tensor_tensor(nodes[r][q][:], slot[r][:, q, 0:1].bitcast(I32), zero1[:], ALU.add).then_inc(index_set, 1)
                        pool.wait_ge(index_set, 2)
                        for q in range(2):
                            pool.indirect_dma_start(out=G[:, r, q, :], out_offset=None, in_=v.up_table,
                                                    in_offset=bass.IndirectOffsetOnAxis(ap=nodes[r][q][:], axis=0)).then_inc(rows_in[r], 16)
                        for q in range(2):
                            pool.tensor_scalar(hot[r][q][:], v.iota1[:], slot[r][:, q, 1:2], None, ALU.is_equal).then_inc(hot_set, 1)

            @blk.vector
            def _(dve):
                dve.sem_inc(gathers_free, RING - 1)
                with dve.Fori(0, STEPS) as i:
                    for r in range(RING):
                        b = r % 2
                        for q in range(2):
                            n = 8 * i + 2 * r + q
                            s, g, m = slot[r][:, q, :], G[:, r, q, :], msg[b][q]
                            dve.wait_ge(slot_in[r], 16 * i + 16)
                            dve.wait_ge(rows_in[r], 32 * i + 32)
                            dve.tensor_scalar(dots[b][q][:], g[:, P:2 * P], s[:, 5:6], None, ALU.mult).then_inc(dot_step, 1)
                            dve.wait_ge(weighted, n + 1)
                            wv = ps[:, q, :]
                            dve.tensor_tensor(m[:, 0:6:5, :], wv[:, 0:2 * P].rearrange("p (a n) -> p a n", n=P),
                                              g[:, 0:P].unsqueeze(1).to_broadcast([P, 2, P]), ALU.mult).then_inc(dot_step, 1)
                            dve.wait_ge(dot_step, 4 * n + 1)
                            dve.scalar_tensor_tensor(dots[b][q][:], g[:, 2 * P:3 * P], s[:, 6:7], dots[b][q][:], ALU.mult, ALU.add).then_inc(dot_step, 1)
                            dve.tensor_tensor(m[:, 1:4, :], wv[:, 2 * P:3 * P].unsqueeze(1).to_broadcast([P, 3, P]),
                                              g[:, P:4 * P].rearrange("p (a n) -> p a n", n=P), ALU.mult).then_inc(vector_msg, 1)
                            dve.wait_ge(dot_step, 4 * n + 3)
                            dve.scalar_tensor_tensor(dots[b][q][:], g[:, 3 * P:4 * P], s[:, 7:8], dots[b][q][:], ALU.mult, ALU.add).then_inc(dot_step, 1)
                            dve.wait_ge(dot_step, 4 * n + 4)
                            dve.tensor_tensor(m[:, 4, :], wv[:, 3 * P:4 * P], dots[b][q][:], ALU.mult).then_inc(msg_done, 1)
                        last_bin = dve.value_load(v.tile_bin[0:1, bass.ds(i * RING + r, 1)], min_val=0, max_val=BINS - 1)
                        dve.wait_ge(summed, 8 * i + 2 * r + 1)
                        dst = acc[:, bass.ds(last_bin, 1), :]
                        dve.tensor_tensor(dst, dst, acc_banks(1 - b).rearrange("p a n -> p (a n)").unsqueeze(1), ALU.add).then_inc(added, 1)
                        dve.wait_ge(added, 4 * i + r + 1)
                        dve.sem_inc(gathers_free, 1)
                last_bin = dve.value_load(v.tile_bin[0:1, PAIRS:PAIRS + 1], min_val=0, max_val=BINS - 1)
                dve.wait_ge(summed, 2 * PAIRS + 1)
                dst = acc[:, bass.ds(last_bin, 1), :]
                dve.tensor_tensor(dst, dst, acc_banks(1).rearrange("p a n -> p (a n)").unsqueeze(1), ALU.add).then_inc(added, 1)
                for t in range(BINS):
                    xr = x[:, t, :]
                    dve.wait_ge(mixed, t + 1)
                    dve.tensor_tensor(xr[:, 0:P], xr[:, 0:P], ps[:, 4 + t % 4, 0:P], ALU.add).then_inc(x_step, 1)
                    xm = xr[:, P:D].rearrange("p (n m) -> p m n", m=3)
                    dve.tensor_tensor(xm, xm, ps[:, 4 + t % 4, P:D].rearrange("p (m n) -> p m n", m=3), ALU.add).then_inc(x_step, 1)

            @blk.scalar
            def _(act):
                with act.Fori(0, STEPS) as i:
                    for r in range(RING):
                        b = r % 2
                        act.wait_ge(hid_turned, 4 * i + r + 1)
                        act.activation(hidT[b][:].rearrange("p q e -> p (q e)"), ps[:, 2 + b, 0:2 * P], ACT.Copy).then_inc(hid_kept, 1)
                        for q in range(2):
                            act.wait_ge(hot_set, 8 * i + 2 * r + q + 1)
                            for m in Y:
                                last = act.activation(hot_y[b][q][:, m, :], hot[r][q][:], ACT.Copy, scale=slot[r][:, q, 4 + m:5 + m])
                            last.then_inc(hot_scaled, 1)
                for t in range(BINS):
                    act.wait_ge(f_turned, t + 1)
                    g = 2 * (t % 2)
                    act.activation(fT[t % 2][:].rearrange("p a n -> p (a n)"), ps[:, g:g + 2, :].rearrange("p a n -> p (a n)"), ACT.Copy).then_inc(f_kept, 1)

            def mix(pe, t):
                f = fT[t % 2]
                pe.wait_ge(f_kept, t + 1)
                if t >= 4:
                    pe.wait_ge(x_step, 2 * (t - 3))
                o = ps[:, 4 + t % 4, :]
                pe.matmul(o[:, 0:P], f[:, 0, :], wo[:, 0, 0, :], start=True, stop=False, skip_group_check=True)
                last = pe.matmul(o[:, 0:P], f[:, 4, :], wo[:, 0, 1, :], start=False, stop=True, skip_group_check=True)
                for m in range(3):
                    pe.matmul(o[:, (m + 1) * P:(m + 2) * P], f[:, 5 + m, :], wo[:, 1, 0, :], start=False, stop=False, skip_group_check=True)
                    last = pe.matmul(o[:, (m + 1) * P:(m + 2) * P], f[:, 1 + m, :], wo[:, 1, 1, :], start=False, stop=True, skip_group_check=True)
                last.then_inc(mixed, 1)

            @blk.tensor
            def _(pe):
                def turn_hidden(rr, at):
                    pe.wait_ge(slot_in[rr], at)
                    for q in range(2):
                        last = pe.transpose(ps[:, 2 + rr % 2, q * P:(q + 1) * P], slot[rr][:, q, 8:ROW], v.ident[:])
                    last.then_inc(hid_turned, 1)

                def path_weights(rr, q):
                    pe.matmul(ps[:, q, :], hidT[rr % 2][:, q, :], w4_parts[:, 0, :], start=True, stop=False)
                    pe.matmul(ps[:, q, :], hidT[rr % 2][:, q, :], w4_parts[:, 1, :], start=False, stop=True).then_inc(weighted, 1)

                pe.wait_ge(w_step, 3)
                for j in range(2):
                    last = pe.matmul(ps[:, 6 + j, :], acc[:, 0, 0:P], acc[:, 0, 0:D], start=True, stop=True)
                last.then_inc(summed, 1)
                turn_hidden(0, 16)
                pe.wait_ge(hid_kept, 1)
                path_weights(0, 0)
                path_weights(0, 1)

                def pair(i, r, more):
                    b, nxt = r % 2, (r + 1) % RING
                    if more:
                        turn_hidden(nxt, 16 * i + 16 + (16 if nxt == 0 else 0))
                    for q in range(2):
                        pe.wait_ge(msg_done, 8 * i + 2 * r + q + 1)
                        if more:
                            pe.wait_ge(hid_kept, 4 * i + r + 2)
                            path_weights(nxt, q)
                        pe.wait_ge(hot_scaled, 8 * i + 2 * r + q + 1)
                        m, hy, first, lastq = msg[b][q], hot_y[b][q], q == 0, q == 1
                        A, B = ps[:, 4 + 2 * b, :], ps[:, 5 + 2 * b, :]
                        pe.matmul(A, hy[:, 0, :], m[:, 0:4, :], start=first, stop=lastq, skip_group_check=True)
                        pe.matmul(B[:, 0:P], hot[r][q][:], m[:, 4, :], start=first, stop=lastq, skip_group_check=True)
                        for k in range(3):
                            last = pe.matmul(B[:, (k + 1) * P:(k + 2) * P], hy[:, k + 1, :], m[:, 5, :], start=False, stop=lastq, skip_group_check=True)
                        last.then_inc(summed, 1)

                with pe.Fori(0, STEPS - 1) as i:
                    for r in range(RING):
                        pair(i, r, True)
                for r in range(RING):
                    pair(STEPS - 1, r, r < RING - 1)
                pe.wait_ge(added, PAIRS + 1)
                for t in range(BINS):
                    g = 2 * (t % 2)
                    if t >= 2:
                        pe.wait_ge(f_kept, t - 1)
                    for k in range(8):
                        last = pe.transpose(ps[:, g + k // 4, (k % 4) * P:(k % 4 + 1) * P], acc[:, t, k * P:(k + 1) * P], v.ident[:])
                    last.then_inc(f_turned, 1)
                    if t >= 1:
                        mix(pe, t - 1)
                mix(pe, BINS - 1)


def cheb_block(nc, a, v):
    z, BINS, KT, N, D = v.z, v.BINS, v.KT, v.N, v.D
    x, h, hT, ps, by_src = v.x, v.h, v.hT, v.ps, v.by_src
    r = v.by_dst[:, :, 0:D]
    with nc.cleanup_on_exit(), ExitStack() as c:
        def sem(name):
            return nc.alloc_semaphore(name=name)
        affine = c.enter_context(nc.sbuf_tensor("affine", [P, 4, D], F32))
        names = ("norm_step", "rooted", "norm_ready", "h_ready", "turned", "kept", "projected", "scaled", "summed", "row_step", "affine_in", "leaky")
        S = {n: sem("cheb_" + n) for n in names}
        blk = c.enter_context(nc.Block())
        NB2 = 2 * BINS

        @blk.sync
        def _(sp):
            for k, name in enumerate(("L2_gnn_b1", "L2_gnn_b2", "L2_gnn_gamma", "L2_gnn_beta")):
                sp.dma_start(affine[:, k, :], broadcast_rows(a[name], D)).then_inc(S["affine_in"], 16)
            sp.wait_ge(S["affine_in"], 64)
            load_relational(sp, a, v, 0)
            load_loop(sp, a, v, 0)

        @blk.gpsimd
        def _(pool):
            root_pool(pool, v, v.rstd[:], S["norm_step"], 2 * BINS + 1, S["rooted"])
            root_pool(pool, v, v.rstd[:], S["norm_step"], 4 * BINS + 2, S["rooted"])

        @blk.vector
        def _(dve):
            layer_norm_dve(dve, v, lambda t: None, S["norm_step"], S["rooted"], S["norm_ready"])
            dve.wait_ge(S["affine_in"], 64)
            for conv in range(2):
                for t in range(BINS):
                    dve.wait_ge(S["turned"], conv * BINS + t + 1)
                    dve.tensor_copy(hT[:, :, t * P:(t + 1) * P], ps[:, t % 4, :].rearrange("p (k n) -> p k n", n=P)).then_inc(S["kept"], 1)
                for t in range(BINS):
                    dve.wait_ge(S["summed"], conv * BINS + t + 1)
                    g = 2 * (t % 4)
                    own, far = ps[:, g, :], ps[:, g + 1, :]
                    if conv == 0:
                        dve.scalar_tensor_tensor(r[:, t, :], far, v.ndinv_cheb[:, t:t + 1], affine[:, 0, :], ALU.mult, ALU.add).then_inc(S["row_step"], 1)
                        dve.wait_ge(S["row_step"], 2 * t + 1)
                        dve.tensor_tensor(r[:, t, :], r[:, t, :], own, ALU.add).then_inc(S["row_step"], 1)
                    else:
                        at = NB2 + 3 * t
                        dve.scalar_tensor_tensor(x[:, t, :], far, v.ndinv_cheb[:, t:t + 1], x[:, t, :], ALU.mult, ALU.add).then_inc(S["row_step"], 1)
                        dve.wait_ge(S["row_step"], at + 1)
                        dve.tensor_tensor(x[:, t, :], x[:, t, :], own, ALU.add).then_inc(S["row_step"], 1)
                        dve.wait_ge(S["row_step"], at + 2)
                        dve.tensor_tensor(x[:, t, :], x[:, t, :], affine[:, 1, :], ALU.add).then_inc(S["row_step"], 1)
                if conv == 0:
                    n0 = 2 * BINS + 1
                    for t in range(BINS):
                        dve.wait_ge(S["row_step"], 2 * t + 2)
                        dve.bn_stats(v.stats[:, t, :], r[:, t, :]).then_inc(S["norm_step"], 1)
                    for t in range(BINS):
                        dve.wait_ge(S["norm_step"], n0 + t + 1)
                        dve.bn_aggr(v.moments[:, t, :], v.stats[:, t, :]).then_inc(S["norm_step"], 1)
                    dve.wait_ge(S["norm_step"], n0 + 2 * BINS)
                    dve.tensor_scalar(v.rstd[:], v.moments[:, :, 1], EPS, None, ALU.add).then_inc(S["norm_step"], 1)
                    dve.wait_ge(S["rooted"], 2)
                    for t in range(BINS):
                        at = 4 * t
                        dve.tensor_scalar(r[:, t, :], r[:, t, :], v.moments[:, t, 0:1], v.rstd[:, t:t + 1], ALU.subtract, ALU.mult).then_inc(S["leaky"], 1)
                        dve.wait_ge(S["leaky"], at + 1)
                        dve.tensor_tensor(r[:, t, :], r[:, t, :], affine[:, 2, :], ALU.mult).then_inc(S["leaky"], 1)
                        dve.wait_ge(S["leaky"], at + 2)
                        dve.tensor_tensor(r[:, t, :], r[:, t, :], affine[:, 3, :], ALU.add).then_inc(S["leaky"], 1)
                        dve.wait_ge(S["leaky"], at + 3)
                        dve.scalar_tensor_tensor(r[:, t, :], r[:, t, :], LEAK, r[:, t, :], ALU.mult, ALU.max).then_inc(S["leaky"], 1)

        @blk.scalar
        def _(act):
            layer_norm_act(act, v, S["norm_ready"], S["h_ready"])
            for conv in range(2):
                for t in range(BINS):
                    act.wait_ge(S["projected"], conv * BINS + t + 1)
                    act.activation(h[:, t, :], ps[:, 4 + t % 4, :], ACT.Copy, scale=v.dinv_cheb[:, t:t + 1]).then_inc(S["scaled"], 1)

        @blk.tensor
        def _(pe):
            for conv in range(2):
                if conv == 0:
                    transposes_pe(pe, v, lambda t: [h[:, t, k * P:(k + 1) * P] for k in range(KT)], [0, 1, 2, 3], S["h_ready"], 0, S["turned"], S["kept"], 0)
                else:
                    for t in range(BINS):
                        pe.wait_ge(S["leaky"], 4 * t + 4)
                        if t >= 4:
                            pe.wait_ge(S["kept"], BINS + t - 3)
                        for k in range(KT):
                            last = pe.transpose(ps[:, t % 4, k * P:(k + 1) * P], r[:, t, k * P:(k + 1) * P], v.ident[:])
                        last.then_inc(S["turned"], 1)
                pe.wait_ge(v.weights_in[2 * conv + 1], 16)
                for t in range(BINS):
                    pe.wait_ge(S["kept"], conv * BINS + t + 1)
                    if t >= 4:
                        pe.wait_ge(S["scaled"], conv * BINS + t - 3)
                    for k in range(KT):
                        last = pe.matmul(ps[:, 4 + t % 4, :], hT[:, k, t * P:(t + 1) * P], v.weights[:, 2 * conv + 1, k, :], start=(k == 0), stop=(k == KT - 1))
                    last.then_inc(S["projected"], 1)
                pe.wait_ge(v.weights_in[2 * conv], 32 if conv == 0 else 16)
                pe.wait_ge(S["scaled"], conv * BINS + BINS)
                for t in range(BINS):
                    if t >= 4:
                        pe.wait_ge(S["row_step"], 2 * (t - 3) if conv == 0 else NB2 + 3 * (t - 3))
                    g = 2 * (t % 4)
                    for k in range(KT):
                        pe.matmul(ps[:, g, :], hT[:, k, t * P:(t + 1) * P], v.weights[:, 2 * conv, k, :], start=(k == 0), stop=(k == KT - 1))
                    for m in range(BINS):
                        last = pe.matmul(ps[:, g + 1, :], by_src[:, m, t * P:(t + 1) * P], h[:, m, :], start=(m == 0), stop=(m == BINS - 1))
                    last.then_inc(S["summed"], 1)


def relational_block(nc, a, v, out):
    row_no = v.meta[:].bitcast(I32)[:, :, 3]
    with nc.cleanup_on_exit(), ExitStack() as c0:
        ones_row = c0.enter_context(nc.sbuf_tensor("ones_row", [1, P], F32))
        for layer in range(2):
            with nc.cleanup_on_exit(), ExitStack() as c:
                relational_layer(nc, a, v, out, layer, c, row_no, ones_row)


def relational_layer(nc, a, v, out, layer, c, row_no, ones_row):
    z, BINS, KT, N, D, TILES = v.z, v.BINS, v.KT, v.N, v.D, v.TILES
    RELS, BASES = z.RELS, z.BASES
    x, h, hT, ps = v.x, v.h, v.hT, v.ps
    basis, loop_w, comp, bias = v.basis[layer], v.loop_w, v.comp, v.rel_bias
    SET = 4
    RING = 2 * SET
    STEPS = TILES // RING
    DVE_RELS = 6
    POOL_RELS = RELS - DVE_RELS
    DVE_TERMS = DVE_RELS * (BASES - 1)
    POOL_TERMS = POOL_RELS * (BASES - 1)
    ACT_TERMS = DVE_RELS + POOL_RELS * BASES

    def sb(name, shape, dt=F32):
        return c.enter_context(nc.sbuf_tensor(f"{name}_{layer}", shape, dt))

    def sem(name):
        return nc.alloc_semaphore(name=f"rel{layer}_{name}")
    stage = v.by_dst[:].rearrange("p a n -> p (a n)").rearrange("p (b r d) -> p b r d", b=2, r=RELS)
    rows_room = v.by_src[:].rearrange("p a n -> p (a n)").rearrange("p (g d) -> p g d", d=D)
    terms = rows_room[:, 0:2 * POOL_TERMS, :].rearrange("p (b r k) d -> p b r k d", b=2, r=POOL_RELS)
    G = rows_room[:, 0:RING, :]
    table = v.rel_table[layer]
    table_rows = table.rearrange("(r t p) d -> t p r d", r=RELS, p=P)
    nodes = [sb(f"nodes{b}", [P, SET], I32) for b in range(2)]
    hot = [sb(f"hot{r}", [P, P]) for r in range(RING)]
    rows_in = [sem(f"rows_in{r}") for r in range(RING)]
    table_out = [sem(f"table_out{b}") for b in range(2)]
    (norm_step, rooted, norm_ready, h_ready, turned, kept, based, act_term, dve_mix, pool_mix, index_set, hot_set, tile_summed,
     row_step, out_done, bias_added, ones_set) = (sem(n) for n in (
         "norm_step", "rooted", "norm_ready", "h_ready", "turned", "kept", "based", "act_term", "dve_mix", "pool_mix", "index_set",
         "hot_set", "tile_summed", "row_step", "out_done", "bias_added", "ones_set"))
    blk = c.enter_context(nc.Block())

    @blk.sync
    def _(sp):
        if layer == 0:
            load_relational(sp, a, v, 1)
        else:
            load_loop(sp, a, v, 1)
        for t in range(BINS):
            sp.wait_ge(dve_mix, DVE_TERMS * (t + 1))
            sp.wait_ge(pool_mix, POOL_TERMS * (t + 1))
            sp.dma_start(table_rows[t], stage[:, t % 2]).then_inc(table_out[t % 2], 16)
        if layer == 1:
            for t in range(BINS):
                sp.wait_ge(row_step, t + 1)
                sp.dma_start(out[t * P:(t + 1) * P, :], x[:, t, :]).then_inc(out_done, 16)
            sp.wait_ge(out_done, 16 * BINS)

    @blk.gpsimd
    def _(pool):
        if layer == 0:
            pool.memset(ones_row[:], 1.0).then_inc(ones_set, 1)
            root_pool(pool, v, v.rstd[:], norm_step, 2 * BINS + 1, rooted)
        for t in range(BINS):
            for b in range(1, BASES):
                for rel in range(POOL_RELS):
                    if b == 1:
                        pool.wait_ge(act_term, ACT_TERMS * t + POOL_TERMS + DVE_RELS + rel + 1)
                    else:
                        pool.wait_ge(pool_mix, POOL_TERMS * t + POOL_RELS * (b - 2) + rel + 1)
                    row = stage[:, t % 2, DVE_RELS + rel, :]
                    pool.tensor_tensor(row, row, terms[:, t % 2, rel, b - 1, :], ALU.add).then_inc(pool_mix, 1)
        for b in range(2):
            pool.wait_ge(table_out[b], 16 * BINS // 2)
        pool.wait_ge(pool_mix, POOL_TERMS * BINS)
        with pool.Fori(0, STEPS) as i:
            for b in range(2):
                pool.sem_clear(index_set)
                pool.wait_ge(tile_summed, i * RING + (b + 1) * SET)
                pool.tensor_copy(nodes[b][:], row_no[:, bass.ds(i * RING + b * SET, SET)]).then_inc(index_set, 1)
                pool.wait_ge(index_set, 1)
                for k in range(SET):
                    pool.indirect_dma_start(out=G[:, b * SET + k, :], out_offset=None, in_=table,
                                            in_offset=bass.IndirectOffsetOnAxis(ap=nodes[b][:, k:k + 1], axis=0)).then_inc(rows_in[b * SET + k], 16)

    @blk.vector
    def _(dve):
        if layer == 0:
            layer_norm_dve(dve, v, lambda t: None, norm_step, rooted, norm_ready)
        for t in range(BINS):
            dve.wait_ge(turned, t + 1)
            dve.tensor_copy(hT[:, :, t * P:(t + 1) * P], ps[:, t % 4, :].rearrange("p (k n) -> p k n", n=P)).then_inc(kept, 1)
        for t in range(BINS):
            for b in range(1, BASES):
                for rel in range(DVE_RELS):
                    if b == 1:
                        dve.wait_ge(act_term, ACT_TERMS * t + POOL_TERMS + rel + 1)
                    else:
                        dve.wait_ge(dve_mix, DVE_TERMS * t + DVE_RELS * (b - 2) + rel + 1)
                    row = stage[:, t % 2, rel, :]
                    k = rel * BASES + b
                    dve.scalar_tensor_tensor(row, ps[:, 4 * (t % 2) + b, :], comp[:, layer, k:k + 1], row, ALU.mult, ALU.add).then_inc(dve_mix, 1)
        if layer == 1:
            for t in range(BINS):
                dve.tensor_tensor(x[:, t, :], x[:, t, :], bias[:, layer, :], ALU.add).then_inc(bias_added, 1)
        with dve.Fori(0, STEPS) as i:
            for r in range(RING):
                dve.wait_ge(tile_summed, i * RING + r + 1)
                t = bass.ds(i * RING + r, 1)
                dve.tensor_scalar(hot[r][:], v.iota1[:], v.meta[:, t, 1:2].rearrange("p a b -> p (a b)"),
                                  v.meta[:, t, 2:3].rearrange("p a b -> p (a b)"), ALU.is_equal, ALU.mult).then_inc(hot_set, 1)
        dve.wait_ge(tile_summed, TILES + RING)
        if layer == 0:
            for t in range(0, BINS, 2):
                dve.tensor_scalar(h[:, t, :], ps[:, t, :], 0.0, None, ALU.max).then_inc(row_step, 1)
        else:
            dve.wait_ge(bias_added, BINS)
            for t in range(BINS):
                dve.tensor_tensor(x[:, t, :], ps[:, t, :], x[:, t, :], ALU.add).then_inc(row_step, 1)

    @blk.scalar
    def _(act):
        if layer == 0:
            layer_norm_act(act, v, norm_ready, h_ready)
        act.wait_ge(v.relational_in[layer], 16 * (BASES + 2))
        for t in range(BINS):
            act.wait_ge(based, t + 1)
            if t >= 2:
                act.wait_ge(pool_mix, POOL_TERMS * (t - 1))
            for b in range(1, BASES):
                for rel in range(DVE_RELS, RELS):
                    k = rel * BASES + b
                    act.activation(terms[:, t % 2, rel - DVE_RELS, b - 1, :], ps[:, 4 * (t % 2) + b, :], ACT.Copy,
                                   scale=comp[:, layer, k:k + 1]).then_inc(act_term, 1)
            if t >= 2:
                act.wait_ge(table_out[t % 2], 16 * (t // 2))
            for rel in range(RELS):
                k = rel * BASES
                act.activation(stage[:, t % 2, rel, :], ps[:, 4 * (t % 2), :], ACT.Copy, scale=comp[:, layer, k:k + 1]).then_inc(act_term, 1)
        if layer == 0:
            act.wait_ge(tile_summed, TILES + RING)
            for t in range(1, BINS, 2):
                act.activation(h[:, t, :], ps[:, t, :], ACT.Relu).then_inc(row_step, 1)

    @blk.tensor
    def _(pe):
        bins = [pe.alloc_register(f"rel{layer}_bin{k}") for k in range(RING // 2)]
        for t in range(BINS):
            if layer == 0:
                pe.wait_ge(h_ready, t + 1)
            if t >= 4:
                pe.wait_ge(kept, t - 3)
            for k in range(KT):
                last = pe.transpose(ps[:, t % 4, k * P:(k + 1) * P], h[:, t, k * P:(k + 1) * P], v.ident[:])
            last.then_inc(turned, 1)
        pe.wait_ge(v.relational_in[layer], 16 * (BASES + 2))
        pe.wait_ge(kept, BINS)
        for t in range(BINS):
            if t >= 2:
                pe.wait_ge(dve_mix, DVE_TERMS * (t - 1))
                pe.wait_ge(act_term, ACT_TERMS * (t - 1))
            for b in range(BASES):
                for k in range(KT):
                    last = pe.matmul(ps[:, 4 * (t % 2) + b, :], hT[:, k, t * P:(t + 1) * P], basis[:, b, k, :], start=(k == 0), stop=(k == KT - 1))
            last.then_inc(based, 1)
        pe.sem_inc(tile_summed, RING)
        if layer == 0:
            pe.wait_ge(ones_set, 1)
        pe.wait_ge(v.loop_in, 16 * (layer + 1))
        for t in range(BINS):
            if t in (0, 4):
                last_tile = BINS - 2 + t // 4
                pe.wait_ge(dve_mix, DVE_TERMS * (last_tile + 1))
                pe.wait_ge(act_term, ACT_TERMS * (last_tile + 1))
            for k in range(KT):
                pe.matmul(ps[:, t, :], hT[:, k, t * P:(t + 1) * P], loop_w[:, k, :], start=(k == 0), stop=False, skip_group_check=True)
            if layer == 0:
                pe.matmul(ps[:, t, :], ones_row[:], bias[0:1, layer, :], start=False, stop=False, skip_group_check=True)
        with pe.Fori(0, STEPS) as i:
            pe.load(bins, v.tile_bin[0:1, bass.ds(i * (RING // 2) + 1, RING // 2)])
            at = [pe.snap(reg, min_val=0, max_val=BINS - 1) for reg in bins]
            for r in range(RING):
                pe.wait_ge(hot_set, i * RING + r + 1)
                pe.wait_ge(rows_in[r], 16 * i + 16)
                pe.matmul(ps[:, bass.ds(at[r // 2], 1), :], hot[r][:], G[:, r, :], start=False, stop=False, skip_group_check=True).then_inc(tile_summed, 1)


def kernel(**inputs):
    import numpy as np
    import concourse.bacc as bacc
    from concourse.bass_utils import run_bass_kernel_spmd as run

    nc = bacc.Bacc("TRN2", target_bir_lowering=False, num_devices=1)
    arrays, aps = {}, {}
    for name, value in inputs.items():
        arr = np.ascontiguousarray(value)
        arrays[f"in_{name}"] = arr
        aps[name] = nc.dram_tensor(f"in_{name}", arr.shape, mybir.dt.from_np(arr.dtype), kind="ExternalInput").ap()
    out = nc.dram_tensor("out", inputs["x"].shape, F32, kind="ExternalOutput").ap()
    build_program(nc, aps, out)
    return run(nc, [arrays], core_ids=[0]).results[0]["out"]
```

```python
from contextlib import ExitStack

import concourse.bass as bass
from concourse import mybir

F32 = mybir.dt.float32
F32R = mybir.dt.float32r
F16 = mybir.dt.float16
BF16 = mybir.dt.bfloat16
I32 = mybir.dt.int32
ALU = mybir.AluOpType
ACT = mybir.ActivationFunctionType
AX = mybir.AxisListType

P = 128
EPS = 1e-5
SILU_2MOM = 1.679177
AVG_NEIGHBORS = 10.0
LEAK = 0.01


class Shapes:

    def __init__(self, x, src, edge_attr_8, mlp1, comp):
        self.N, self.D = x.shape
        self.E = src.shape[0]
        self.R8 = edge_attr_8.shape[1]
        self.HID = mlp1.shape[1]
        self.RELS, self.BASES = comp.shape
        self.BINS = self.N // P
        self.COLS = self.E // P
        self.PAIRS = -(-self.E // (2 * P)) + self.BINS
        self.TILES = 2 * self.PAIRS
        self.ROW = 8 + 2 * self.HID
        self.KT = self.D // P


class Shared:
    pass


def broadcast_rows(ap, n):
    return bass.AP(ap.tensor, 0, [[0, P], [1, n]])


def build_program(nc, a, out):
    z = Shapes(a["x"], a["src"], a["edge_attr_8"], a["L1_gnn_W_mlp1"], a["L3_gnn_comp0"])
    N, D, BINS, COLS, TILES, PAIRS, ROW, KT, HID = z.N, z.D, z.BINS, z.COLS, z.TILES, z.PAIRS, z.ROW, z.KT, z.HID
    assert D == 4 * P and HID == 64 and COLS % 8 == 0 and PAIRS % 4 == 0 and BINS == 8

    slots = nc.dram_tensor("edge_slots", [(TILES + 2) * P, ROW], F32).ap()
    up_table = nc.dram_tensor("up_table", [N, D], F32).ap()
    rel_table = [nc.dram_tensor(f"rel_table_{n}", [z.RELS * N, D], F32).ap() for n in range(2)]

    with ExitStack() as ctx:
        def sb(name, shape, dt=F32, c=ctx):
            return c.enter_context(nc.sbuf_tensor(name, shape, dt))

        def sem(name):
            return ctx.enter_context(nc.semaphore(name))

        ps = ctx.enter_context(nc.psum_tensor("ps", [P, 8, 512], F32))
        x = sb("x_rows", [P, BINS, D])
        h = sb("h_rows", [P, BINS, D])
        hT = sb("h_cols", [P, KT, N])
        by_src = sb("counts_by_src", [P, BINS, N])
        by_dst = sb("counts_by_dst", [P, BINS, N])
        meta = sb("slot_meta", [P, TILES, 8])
        ident = sb("ident", [P, P])
        iota1 = sb("iota1", [P, P])
        tile_bin = sb("tile_bin", [P, 80], I32)
        stats = sb("stats", [P, BINS, 6])
        moments = sb("moments", [P, BINS, 2])
        rstd = sb("rstd", [P, BINS])
        shift = sb("shift", [P, BINS])
        dinv_gcn = sb("dinv_gcn", [P, BINS])
        dinv_cheb = sb("dinv_cheb", [P, BINS])
        ndinv_cheb = sb("ndinv_cheb", [P, BINS])
        minus_half = sb("minus_half", [P, BINS])

        x_in = sem("x_in")
        weights_in = [sem(f"weights_in{n}") for n in range(4)]
        consts = sem("consts")

        v = Shared()
        v.z = z
        v.N = N
        v.D = D
        v.BINS = BINS
        v.COLS = COLS
        v.TILES = TILES
        v.PAIRS = PAIRS
        v.ROW = ROW
        v.KT = KT
        v.HID = HID
        v.slots = slots
        v.up_table = up_table
        v.rel_table = rel_table
        v.ps = ps
        v.x = x
        v.h = h
        v.hT = hT
        v.by_src = by_src
        v.by_dst = by_dst
        v.meta = meta
        v.ident = ident
        v.iota1 = iota1
        v.tile_bin = tile_bin
        v.stats = stats
        v.moments = moments
        v.rstd = rstd
        v.shift = shift
        v.dinv_gcn = dinv_gcn
        v.dinv_cheb = dinv_cheb
        v.ndinv_cheb = ndinv_cheb
        v.minus_half = minus_half
        v.x_in = x_in
        v.up = sb("w_up", [P, 2, P])
        v.w4 = sb("w_mlp4", [P, D])
        v.wo = sb("w_out", [P, 2, 2, P])
        v.tp_weights = sem("tp_weights")
        v.weights_in = weights_in
        with ExitStack() as first:
            v.w_gcn = sb("w_gcn", [P, KT, D], F32, first)
            v.b_gcn = sb("b_gcn", [P, D], F32, first)
            edges_block(nc, a, v)
            counts_block(nc, a, v)
            gcn_block(nc, a, v)
        weights = sb("weights", [P, 4, KT, D])
        v.weights = weights
        tensor_product_block(nc, a, v)
        v.basis = [sb("basis0", [P, z.BASES, KT, D]), weights]
        v.loop_w = sb("loop_w", [P, KT, D])
        v.comp = sb("comp", [P, 2, z.RELS * z.BASES])
        v.rel_bias = sb("rel_bias", [P, 2, D])
        v.relational_in = [sem(f"relational_in{n}") for n in range(2)]
        v.loop_in = sem("loop_in")
        cheb_block(nc, a, v)
        relational_block(nc, a, v, out)


def load_relational(sp, a, v, layer):
    z, done = v.z, v.relational_in[layer]
    for b in range(z.BASES):
        sp.dma_start(v.basis[layer][:, b], a[f"L3_gnn_basis{layer}"][b].rearrange("(k p) n -> p k n", p=P)).then_inc(done, 16)
    sp.dma_start(v.comp[:, layer, :], broadcast_rows(a[f"L3_gnn_comp{layer}"], z.RELS * z.BASES)).then_inc(done, 16)
    sp.dma_start(v.rel_bias[:, layer, :], broadcast_rows(a[f"L3_gnn_bias{layer}"], v.D)).then_inc(done, 16)


def load_loop(sp, a, v, layer):
    sp.dma_start(v.loop_w[:], a[f"L3_gnn_loop{layer}"].rearrange("(k p) n -> p k n", p=P)).then_inc(v.loop_in, 16)


def edges_block(nc, a, v):
    z, N, BINS, COLS, TILES, PAIRS, ROW, HID = v.z, v.N, v.BINS, v.COLS, v.TILES, v.PAIRS, v.ROW, v.HID
    G = 4
    ITERS = COLS // (2 * G)
    with nc.cleanup_on_exit(), ExitStack() as c:
        def sb(name, shape, dt=F32):
            return c.enter_context(nc.sbuf_tensor(name, shape, dt))

        def sem(name):
            return nc.alloc_semaphore(name="edge_" + name)
        ps = v.ps
        dst_i, src_i, type_i, bin_i = (sb(n, [P, COLS], I32) for n in ("dst_i", "src_i", "type_i", "bin_i"))
        weight, dst_f, bin_f, pos = (sb(n, [P, COLS]) for n in ("weight", "dst_f", "bin_f", "pos"))
        y = sb("y", [P, COLS, 4])
        attr = sb("attr", [P, COLS, z.R8])
        edge_meta = sb("edge_meta", [P, COLS, 8])
        in_bin, no_carry, seen, place = (v.by_src[:, 2 * k:2 * k + 2, :].rearrange("p a n -> p (a n)")[:, 0:BINS * COLS]
                                         .rearrange("p (b j) -> p b j", j=COLS) for k in range(4))
        row_total, ones8, pairs_f, pair_end, offset = (sb(n, [P, BINS]) for n in ("row_total", "ones8", "pairs_f", "pair_end", "offset"))
        pairs_i = sb("pairs_i", [P, BINS], I32)
        lower = sb("lower", [P, P])
        ones = sb("ones", [P, P])
        pair_no = sb("pair_no", [P, PAIRS])
        passed = sb("passed", [P, PAIRS, BINS])
        bin_of = sb("bin_of", [P, PAIRS])
        zeros = sb("zeros", [P, 1024])
        w1 = sb("w1", [G * z.R8, 2, P])
        w2 = sb("w2", [P, P])
        w3 = sb("w3", [P, P])
        a8 = [sb(f"a8_{b}", [P, G * z.R8]) for b in range(2)]
        a8T = [sb(f"a8T_{b}", [G * z.R8, P]) for b in range(2)]
        h1, h2, h3 = ([sb(f"{n}_{b}", [P, 2 * P]) for b in range(2)] for n in ("h1", "h2", "h3"))
        payload = [sb(f"payload{b}", [P, G, ROW]) for b in range(2)]
        row_f = [sb(f"row_f{b}", [P, G], I32) for b in range(2)]
        row_i = [sb(f"row_i{b}", [P, G], I32) for b in range(2)]
        zero_g = sb("zero_g", [P, G], I32)

        dst_in, edges_in, blocks_zero, mlp_in = sem("dst_in"), sem("edges_in"), sem("blocks_zero"), sem("mlp_in")
        scattered = [sem(f"scattered{b}") for b in range(2)]
        zeros_set, slots_zeroed, index_step, totals_ready, pool_step = sem("zeros_set"), sem("slots_zeroed"), sem("index_step"), sem("totals_ready"), sem("pool_step")
        places_done, parts_done, staged, attr_turned, attr_cols = sem("places_done"), sem("parts_done"), sem("staged"), sem("attr_turned"), sem("attr_cols")
        pre_act, acted, hidden_turned, packed, rows_set = sem("pre_act"), sem("acted"), sem("hidden_turned"), sem("packed"), sem("rows_set")
        row_total_at = []
        zero_dmas = -(-(TILES + 2) * ROW // 2048)
        blk = c.enter_context(nc.Block())

        @blk.sync
        def _(sp):
            sp.dma_start(dst_i[:], a["dst"].rearrange("(p j) -> p j", p=P)).then_inc(dst_in, 16)
            sp.dma_start(attr[:], a["edge_attr_8"].rearrange("(p j) r -> p j r", p=P)).then_inc(edges_in, 16)
            sp.dma_start(src_i[:], a["src"].rearrange("(p j) -> p j", p=P)).then_inc(edges_in, 16)
            sp.dma_start(type_i[:], a["edge_type_8"].rearrange("(p j) -> p j", p=P)).then_inc(edges_in, 16)
            sp.dma_start(weight[:], a["edge_weight"].rearrange("(p j) -> p j", p=P)).then_inc(edges_in, 16)
            sp.dma_start(y[:], a["edge_attr_4"].rearrange("(p j) r -> p j r", p=P)).then_inc(edges_in, 16)
            sp.wait_ge(zeros_set, 1)
            flat = v.slots.rearrange("(p q) r -> p (q r)", p=P)
            per = flat.shape[1]
            half = per // 2
            for b in range(2):
                cuts = list(range(b * half, (b + 1) * half, 1024)) + [(b + 1) * half]
                assert per % 2 == 0
                for lo, hi in zip(cuts, cuts[1:]):
                    sp.dma_start(flat[:, lo:hi], zeros[:, 0:hi - lo]).then_inc(slots_zeroed, 16)
            sp.dma_start(v.x[:], a["x"].rearrange("(t p) d -> p t d", p=P)).then_inc(v.x_in, 16)
            sp.dma_start(v.w_gcn[:], a["L0_gnn_weight"].rearrange("(k p) n -> p k n", p=P)).then_inc(v.weights_in[0], 16)
            sp.dma_start(v.b_gcn[:], broadcast_rows(a["L0_gnn_bias"], v.D)).then_inc(v.weights_in[0], 16)
            for b in range(2):
                sp.wait_ge(scattered[b], 16 * G * ITERS)

        @blk.gpsimd
        def _(pool):
            pool.memset(zeros[:], 0.0).then_inc(zeros_set, 1)
            pool.memset(v.ident[:], 0.0).then_inc(pool_step, 1)
            pool.memset(ones[:], 1.0).then_inc(pool_step, 1)
            pool.memset(lower[:], 1.0).then_inc(pool_step, 1)
            pool.memset(no_carry, 1.0).then_inc(pool_step, 1)
            pool.memset(ones8[:], 1.0).then_inc(pool_step, 1)
            pool.memset(v.minus_half[:], -0.5).then_inc(pool_step, 1)
            pool.memset(zero_g[:], 0).then_inc(pool_step, 1)
            pool.wait_ge(pool_step, 7)
            pool.affine_select(out=v.ident[:], in_=v.ident[:], compare_op=ALU.not_equal, fill=1.0, base=0,
                               pattern=[[-1, P]], channel_multiplier=1).then_inc(pool_step, 1)
            pool.affine_select(out=lower[:], in_=lower[:], compare_op=ALU.is_gt, fill=0.0, base=0,
                               pattern=[[1, P]], channel_multiplier=-1).then_inc(pool_step, 1)
            pool.memset(no_carry[:, :, 0:1], 0.0).then_inc(pool_step, 1)
            pool.iota(v.iota1[:], pattern=[[1, P]], base=1, channel_multiplier=0,
                      allow_small_or_imprecise_dtypes=True).then_inc(pool_step, 1)
            pool.iota(pair_no[:], pattern=[[1, PAIRS]], base=0, channel_multiplier=0,
                      allow_small_or_imprecise_dtypes=True).then_inc(pool_step, 1)
            pool.memset(w1[:], 0.0).then_inc(blocks_zero, 1)
            pool.memset(w2[:], 0.0).then_inc(blocks_zero, 1)
            pool.memset(w3[:], 0.0).then_inc(blocks_zero, 1)
            pool.wait_ge(slots_zeroed, 2 * 16 * zero_dmas)
            with pool.Fori(0, ITERS) as i:
                for b in range(2):
                    pool.sem_clear(rows_set)
                    pool.wait_ge(packed, 4 * i + 2 * b + 6)
                    pool.tensor_tensor(row_i[b][:], row_f[b][:], zero_g[:], ALU.add).then_inc(rows_set, 1)
                    pool.wait_ge(rows_set, 1)
                    for k in range(G):
                        pool.indirect_dma_start(out=v.slots, out_offset=bass.IndirectOffsetOnAxis(ap=row_i[b][:, k:k + 1], axis=0),
                                                in_=payload[b][:, k, :], in_offset=None).then_inc(scattered[b], 16)

        @blk.vector
        def _(dve):
            steps = [0]

            def step(ins):
                steps[0] += 1
                ins.then_inc(index_step, 1)
                dve.wait_ge(index_step, steps[0])

            dve.wait_ge(dst_in, 16)
            dve.tensor_scalar(bin_i[:], dst_i[:], 7, None, ALU.arith_shift_right).then_inc(index_step, 1)
            dve.tensor_copy(dst_f[:], dst_i[:]).then_inc(index_step, 1)
            steps[0] += 2
            dve.wait_ge(index_step, steps[0])
            step(dve.tensor_copy(bin_f[:], bin_i[:]))
            for b in range(BINS):
                ins = dve.tensor_scalar(in_bin[:, b, :], bin_f[:], float(b), None, ALU.is_equal)
                ins.then_inc(index_step, 1)
                steps[0] += 1
            dve.wait_ge(index_step, steps[0])
            dve.wait_ge(pool_step, 12)
            step(dve.tensor_tensor_scan(seen.rearrange("p b j -> p (b j)"), no_carry.rearrange("p b j -> p (b j)"),
                                        in_bin.rearrange("p b j -> p (b j)"), 0.0, ALU.mult, ALU.add))
            dve.tensor_copy(row_total[:], seen[:, :, COLS - 1]).then_inc(index_step, 1)
            steps[0] += 1
            row_total_at.append(steps[0])
            dve.wait_ge(totals_ready, 1)
            step(dve.tensor_scalar(pairs_f[:], ps[:, 0, 8:16], float(2 * P - 1), None, ALU.add))
            step(dve.tensor_copy(pairs_i[:], pairs_f[:]))
            step(dve.tensor_scalar(pairs_i[:], pairs_i[:], 8, None, ALU.arith_shift_right))
            step(dve.tensor_copy(pairs_f[:], pairs_i[:]))
            step(dve.tensor_tensor_scan(pair_end[:], ones8[:], pairs_f[:], 0.0, ALU.mult, ALU.add))
            step(dve.tensor_tensor(offset[:], pair_end[:], pairs_f[:], ALU.subtract))
            step(dve.tensor_scalar(offset[:], offset[:], float(2 * P), -1.0, ALU.mult, ALU.add))
            step(dve.tensor_tensor(offset[:], offset[:], ps[:, 0, 0:8], ALU.add))
            for b in range(BINS):
                dve.scalar_tensor_tensor(place[:, b, :], seen[:, b, :], offset[:, b:b + 1], in_bin[:, b, :],
                                         ALU.add, ALU.mult).then_inc(index_step, 1)
                steps[0] += 1
            dve.wait_ge(index_step, steps[0])
            step(dve.tensor_reduce(pos[:], place.rearrange("p b j -> p j b"), AX.X, ALU.add))
            step(dve.tensor_tensor(passed[:], pair_no[:].unsqueeze(2).to_broadcast([P, PAIRS, BINS]),
                                   pair_end[:].unsqueeze(1).to_broadcast([P, PAIRS, BINS]), ALU.is_ge))
            step(dve.tensor_reduce(bin_of[:], passed[:], AX.X, ALU.add))
            step(dve.tensor_scalar(bin_of[:], bin_of[:], float(BINS - 1), None, ALU.min))
            dve.memset(v.tile_bin[:], 0).then_inc(index_step, 1)
            steps[0] += 1
            dve.wait_ge(index_step, steps[0])
            step(dve.tensor_copy(v.tile_bin[:, 1:PAIRS + 1], bin_of[:]))
            dve.wait_ge(edges_in, 80)
            em = edge_meta
            em_i = edge_meta[:].bitcast(I32)
            dve.tensor_copy(em_i[:, :, 0], src_i[:]).then_inc(index_step, 1)
            dve.scalar_tensor_tensor(em[:, :, 1], bin_f[:], float(-P), dst_f[:], ALU.mult, ALU.add).then_inc(index_step, 1)
            dve.tensor_copy(em[:, :, 2], weight[:]).then_inc(index_step, 1)
            dve.scalar_tensor_tensor(em_i[:, :, 3], type_i[:], float(N), src_i[:], ALU.mult, ALU.add).then_inc(index_step, 1)
            dve.tensor_copy(em[:, :, 4:8], y[:]).then_inc(index_step, 1)
            steps[0] += 5
            dve.wait_ge(index_step, steps[0])
            dve.tensor_scalar(em[:, :, 1], em[:, :, 1], 1.0, None, ALU.add).then_inc(index_step, 1)
            steps[0] += 1
            dve.wait_ge(index_step, steps[0])

            def stage(i):
                for b in range(2):
                    cols = bass.ds(i * (2 * G) + b * G, G)
                    dve.tensor_copy(a8[b][:].rearrange("p (j r) -> p j r", r=z.R8), attr[:, cols, :]).then_inc(staged, 1)

            def keep_attr(i, used_before):
                if used_before:
                    dve.wait_ge(pre_act, 6 * i - 4)
                for b in range(2):
                    dve.wait_ge(attr_turned, 2 * i + b + 1)
                    dve.tensor_copy(a8T[b][:], ps[0:G * z.R8, 4 * b, 0:P]).then_inc(attr_cols, 1)

            def pack(i, scattered_before):
                for b in range(2):
                    cols = bass.ds(i * (2 * G) + b * G, G)
                    if scattered_before:
                        dve.wait_ge(scattered[b], 16 * G * i)
                    dve.tensor_copy(row_f[b][:], pos[:, cols]).then_inc(packed, 1)
                    dve.wait_ge(hidden_turned, 2 * i + b + 1)
                    hid = ps[:, 4 * b + 3, 0:G * HID].rearrange("p (j h) -> p j h", h=HID)
                    dve.tensor_copy(payload[b][:, :, 8:8 + HID].bitcast(F32R), hid).then_inc(parts_done, 1)
                    dve.tensor_copy(payload[b][:, :, 0:8], edge_meta[:, cols, :]).then_inc(places_done, 1)
                    dve.wait_ge(parts_done, 2 * i + b + 1)
                    dve.tensor_tensor(payload[b][:, :, 8 + HID:ROW], hid, payload[b][:, :, 8:8 + HID], ALU.subtract).then_inc(packed, 1)

            dve.sem_inc(packed, 4)
            stage(0)
            keep_attr(0, False)
            stage(1)
            keep_attr(1, True)
            stage(2)
            pack(0, False)
            with dve.Fori(1, ITERS - 2) as i:
                keep_attr(i + 1, True)
                stage(i + 2)
                pack(i, True)
            keep_attr(ITERS - 1, True)
            pack(ITERS - 2, True)
            pack(ITERS - 1, True)

        @blk.tensor
        def _(pe):
            pe.wait_ge(pool_step, 12)
            pe.wait_ge(index_step, row_total_at[0])
            pe.matmul(ps[:, 0, 0:8], lower[:], row_total[:], start=True, stop=True)
            pe.matmul(ps[:, 0, 8:16], ones[:], row_total[:], start=True, stop=True).then_inc(totals_ready, 1)
            pe.wait_ge(mlp_in, 16 * (G + 4))

            def turn_attr(i):
                for b in range(2):
                    pe.wait_ge(staged, 2 * i + b + 1)
                    pe.transpose(ps[0:G * z.R8, 4 * b, 0:P], a8[b][:], v.ident[:]).then_inc(attr_turned, 1)

            def network(i, more):
                for b in range(2):
                    pe.wait_ge(attr_cols, 2 * i + b + 1)
                    for jj in range(2):
                        last = pe.matmul(ps[:, 4 * b + 1, jj * P:(jj + 1) * P], w1[:, jj, :], a8T[b][:], start=True, stop=True)
                    last.then_inc(pre_act, 1)
                if more:
                    turn_attr(i + 1)
                for layer, (w, hin, bank) in enumerate(((w2, h1, 2), (w3, h2, 1))):
                    for b in range(2):
                        pe.wait_ge(acted, 6 * i + 2 * layer + b + 1)
                        pe.matmul(ps[:, 4 * b + bank, 0:2 * P], w[:], hin[b][:], start=True, stop=True).then_inc(pre_act, 1)
                pe.wait_ge(packed, 4 * i + 4)
                for b in range(2):
                    pe.wait_ge(acted, 6 * i + 4 + b + 1)
                    for jj in range(2):
                        last = pe.transpose(ps[:, 4 * b + 3, jj * P:(jj + 1) * P], h3[b][:, jj * P:(jj + 1) * P], v.ident[:])
                    last.then_inc(hidden_turned, 1)

            turn_attr(0)
            with pe.Fori(0, ITERS - 1) as i:
                network(i, True)
            network(ITERS - 1, False)

        @blk.scalar
        def _(act):
            act.wait_ge(blocks_zero, 3)
            for j in range(G):
                act.dma_start(w1[j * z.R8:(j + 1) * z.R8, j // 2, (j % 2) * HID:(j % 2 + 1) * HID], a["L1_gnn_W_mlp1"]).then_inc(mlp_in, 16)
            for w, name in ((w2, "L1_gnn_W_mlp2"), (w3, "L1_gnn_W_mlp3")):
                for k in range(2):
                    act.dma_start(w[k * HID:(k + 1) * HID, k * HID:(k + 1) * HID], a[name]).then_inc(mlp_in, 16)
            with act.Fori(0, ITERS) as i:
                for layer, (hout, bank, scale) in enumerate(((h1, 1, z.R8 ** -0.5), (h2, 2, SILU_2MOM * HID ** -0.5), (h3, 1, SILU_2MOM * HID ** -0.5))):
                    for b in range(2):
                        act.wait_ge(pre_act, 6 * i + 2 * layer + b + 1)
                        act.activation(hout[b][:], ps[:, 4 * b + bank, 0:2 * P], ACT.Silu, scale=scale).then_inc(acted, 1)



def counts_block(nc, a, v):
    z, BINS, TILES, PAIRS, ROW = v.z, v.BINS, v.TILES, v.PAIRS, v.ROW
    HALF = v.N // 2
    SET = 4
    SETS = TILES // SET
    STEPS = SETS // 2
    with nc.cleanup_on_exit(), ExitStack() as c:
        def sb(name, shape, dt=F32):
            return c.enter_context(nc.sbuf_tensor(name, shape, dt))

        def sem(name):
            return nc.alloc_semaphore(name="count_" + name)
        ps = v.ps
        node_no = sb("node_no", [P, v.N], F16)
        src_f = sb("src_f", [P, TILES])
        zero_b = sb("zero_b", [P, HALF], BF16)
        src_hot = [sb(f"src_hot{b}", [P, SET, HALF], BF16) for b in range(2)]
        dst_hot = sb("dst_hot", [P, TILES, P], BF16)
        place_no = sb("place_no", [P, P], F16)
        dst_h = sb("dst_h", [P, TILES], F16)
        meta_in, set_up, src_set, dst_set, hot_used, half_summed, half_kept, src_ready = (
            sem(n) for n in ("meta_in", "set_up", "src_set", "dst_set", "hot_used", "half_summed", "half_kept", "src_ready"))
        norm_step, rooted, norm_ready, h_ready, turned, kept = (
            sem(n) for n in ("norm_step", "rooted", "norm_ready", "h_ready", "turned", "kept"))
        blk = c.enter_context(nc.Block())

        @blk.sync
        def _(sp):
            with nc.allow_non_contiguous_dma(reason="slot meta"):
                sp.dma_start(v.meta[:], v.slots[0:TILES * P, 0:8].rearrange("(t p) r -> p t r", p=P)).then_inc(meta_in, 16)

        @blk.gpsimd
        def _(pool):
            pool.iota(node_no[:], pattern=[[1, v.N]], base=0, channel_multiplier=0,
                      allow_small_or_imprecise_dtypes=True).then_inc(set_up, 1)
            pool.memset(zero_b[:], 0.0).then_inc(set_up, 1)
            pool.iota(place_no[:], pattern=[[1, P]], base=1, channel_multiplier=0,
                      allow_small_or_imprecise_dtypes=True).then_inc(set_up, 1)
            root_pool(pool, v, v.rstd[:], norm_step, 2 * BINS + 1, rooted)

        @blk.vector
        def _(dve):
            layer_norm_dve(dve, v, lambda t: dve.wait_ge(v.x_in, 16), norm_step, rooted, norm_ready)
            dve.wait_ge(meta_in, 16)
            dve.tensor_copy(src_f[:], v.meta[:].bitcast(I32)[:, :, 0]).then_inc(src_ready, 1)
            dve.tensor_copy(dst_h[:], v.meta[:, :, 1]).then_inc(src_ready, 1)
            dve.wait_ge(src_ready, 2)
            dve.wait_ge(set_up, 3)
            for half in range(2):
                with dve.Fori(0, STEPS) as i:
                    if half == 0:
                        tiles = bass.ds(2 * SET * i, 2 * SET)
                        dve.tensor_tensor(dst_hot[:, tiles, :], place_no[:].unsqueeze(1).to_broadcast([P, 2 * SET, P]),
                                          dst_h[:, tiles].unsqueeze(2).to_broadcast([P, 2 * SET, P]), ALU.is_equal).then_inc(dst_set, 1)
                    for b in range(2):
                        dve.wait_ge(hot_used, half * SETS + 2 * i + b + 1)
                        for k in range(SET):
                            last = dve.tensor_scalar(src_hot[b][:, k, :], node_no[:, half * HALF:(half + 1) * HALF],
                                                     src_f[:, bass.ds((2 * i + b) * SET + k, 1)], None, ALU.is_equal)
                            last.then_inc(src_set, 1)
                dve.wait_ge(half_summed, half + 1)
                for b in range(0, BINS, 2):
                    dve.tensor_copy(v.by_dst[:, b, half * HALF:(half + 1) * HALF], ps[:, b, :]).then_inc(half_kept, 1)

        @blk.scalar
        def _(act):
            layer_norm_act(act, v, norm_ready, h_ready)
            for t in range(BINS):
                act.wait_ge(turned, t + 1)
                act.activation(v.hT[:, :, t * P:(t + 1) * P], ps[:, t % 4, :].rearrange("p (k n) -> p k n", n=P), ACT.Copy).then_inc(kept, 1)
            for half in range(2):
                act.wait_ge(half_summed, half + 1)
                for b in range(1, BINS, 2):
                    act.activation(v.by_dst[:, b, half * HALF:(half + 1) * HALF], ps[:, b, :], ACT.Copy).then_inc(half_kept, 1)

        @blk.tensor
        def _(pe):
            bins = [pe.alloc_register(f"count_bin{k}") for k in range(SET)]
            transposes_pe(pe, v, lambda t: [v.h[:, t, k * P:(k + 1) * P] for k in range(v.KT)], [0, 1, 2, 3], h_ready, 0, turned, kept, 0)
            pe.wait_ge(kept, BINS)
            pe.wait_ge(set_up, 3)
            pe.sem_inc(hot_used, 2)
            for half in range(2):
                if half:
                    pe.wait_ge(half_kept, BINS * half)
                for b in range(BINS):
                    pe.matmul(ps[:, b, :], zero_b[:, 0:P], zero_b[:], start=True, stop=False, skip_group_check=True)
                with pe.Fori(0, STEPS) as i:
                    pe.load(bins, v.tile_bin[0:1, bass.ds(i * SET + 1, SET)])
                    at = [pe.snap(reg, min_val=0, max_val=BINS - 1) for reg in bins]
                    for b in range(2):
                        if half == 0 and b == 0:
                            pe.wait_ge(dst_set, i + 1)
                        pe.wait_ge(src_set, SET * (half * SETS + 2 * i + b + 1))
                        for k in range(SET):
                            last = pe.matmul(ps[:, bass.ds(at[2 * b + k // 2], 1), :], dst_hot[:, bass.ds((2 * i + b) * SET + k, 1), :].rearrange("p a n -> p (a n)"), src_hot[b][:, k, :],
                                             start=False, stop=False, skip_group_check=True)
                        last.then_inc(hot_used, 1)
                pe.matmul(ps[:, 0, :], zero_b[:, 0:P], zero_b[:], start=False, stop=True, skip_group_check=True).then_inc(half_summed, 1)


def layer_norm_dve(dve, v, rows_ready, norm_step, rooted, norm_ready):
    for t in range(v.BINS):
        rows_ready(t)
        dve.bn_stats(v.stats[:, t, :], v.x[:, t, :]).then_inc(norm_step, 1)
    for t in range(v.BINS):
        dve.wait_ge(norm_step, t + 1)
        dve.bn_aggr(v.moments[:, t, :], v.stats[:, t, :]).then_inc(norm_step, 1)
    n = 2 * v.BINS
    dve.wait_ge(norm_step, n)
    dve.tensor_scalar(v.rstd[:], v.moments[:, :, 1], EPS, None, ALU.add).then_inc(norm_step, 1)
    dve.wait_ge(rooted, 1)
    dve.scalar_tensor_tensor(v.shift[:], v.moments[:, :, 0], -1.0, v.rstd[:], ALU.mult, ALU.mult).then_inc(norm_ready, 1)


def root_pool(pool, v, values, done, at, rooted):
    pool.wait_ge(done, at)
    pool.tensor_tensor(values, values, v.minus_half[:, 0:values.shape[1]], ALU.pow).then_inc(rooted, 1)


def layer_norm_act(act, v, norm_ready, h_ready):
    act.wait_ge(norm_ready, 1)
    for t in range(v.BINS):
        act.activation(v.h[:, t, :], v.x[:, t, :], ACT.Relu, bias=v.shift[:, t:t + 1], scale=v.rstd[:, t:t + 1]).then_inc(h_ready, 1)


def transposes_pe(pe, v, blocks, banks, h_ready, h_base, turned, kept, kept_base):
    for t in range(v.BINS):
        pe.wait_ge(h_ready, h_base + t + 1)
        if t >= len(banks):
            pe.wait_ge(kept, kept_base + t - len(banks) + 1)
        for k, block in enumerate(blocks(t)):
            last = pe.transpose(v.ps[:, banks[t % len(banks)], k * P:(k + 1) * P], block, v.ident[:])
        last.then_inc(turned, 1)


def tile_moments_dve(dve, v, rows, t, u, norm_step):
    dve.bn_stats(v.stats[:, t, :], rows).then_inc(norm_step, 1)
    dve.wait_ge(norm_step, 3 * u + 1)
    dve.bn_aggr(v.moments[:, t, :], v.stats[:, t, :]).then_inc(norm_step, 1)
    dve.wait_ge(norm_step, 3 * u + 2)
    dve.tensor_scalar(v.rstd[:, t:t + 1], v.moments[:, t, 1:2], EPS, None, ALU.add).then_inc(norm_step, 1)


def tile_roots_pool(pool, v, tiles, norm_step, rooted):
    for u in range(tiles):
        t = u % v.BINS
        pool.wait_ge(norm_step, 3 * u + 3)
        pool.tensor_tensor(v.rstd[:, t:t + 1], v.rstd[:, t:t + 1], v.minus_half[:, 0:1], ALU.pow).then_inc(rooted, 1)


def tile_shift_dve(dve, v, t, roots, rooted, norm_ready):
    dve.wait_ge(rooted, roots)
    dve.scalar_tensor_tensor(v.shift[:, t:t + 1], v.moments[:, t, 0:1], -1.0, v.rstd[:, t:t + 1], ALU.mult, ALU.mult).then_inc(norm_ready, 1)


def tile_relu_act(act, v, to, t, norm_ready, h_ready):
    act.wait_ge(norm_ready, t + 1)
    act.activation(to, v.x[:, t, :], ACT.Relu, bias=v.shift[:, t:t + 1], scale=v.rstd[:, t:t + 1]).then_inc(h_ready, 1)


def tile_turn_pe(pe, v, blocks, bank, u, ready, turned):
    pe.wait_ge(ready, u + 1)
    for k, block in enumerate(blocks):
        last = pe.transpose(v.ps[:, bank, k * P:(k + 1) * P], block, v.ident[:])
    last.then_inc(turned, 1)


def tile_keep_act(act, v, bank, t, u, turned, kept):
    act.wait_ge(turned, u + 1)
    act.activation(v.hT[:, :, t * P:(t + 1) * P], v.ps[:, bank, :].rearrange("p (k n) -> p k n", n=P), ACT.Copy).then_inc(kept, 1)


def gcn_block(nc, a, v):
    z, BINS, KT, N = v.z, v.BINS, v.KT, v.N
    with nc.cleanup_on_exit(), ExitStack() as c:
        def sem(name):
            return nc.alloc_semaphore(name="gcn_" + name)

        def sb(name, shape, dt=F32):
            return c.enter_context(nc.sbuf_tensor(name, shape, dt))
        ps, x, h, hT, by_src, by_dst = v.ps, v.x, v.h, v.hT, v.by_src, v.by_dst
        out_degree = sb("out_degree", [P, 8])
        has_out = sb("has_out", [P, 8])
        diagonal = sb("diagonal", [P, 2 * BINS - 1, P])
        adj = sb("adj", [P, BINS, N], F32R)
        rows_high = sb("rows_high", [P, BINS, z.D], F32R)
        rows_low = sb("rows_low", [P, BINS, z.D], F32R)
        (rooted, projected, h_kept, counts_turned, counts_kept, adj_step, diagonal_set, high_set, scaled, summed, row_step, degree_step) = (
            sem(n) for n in ("rooted", "projected", "h_kept", "counts_turned", "counts_kept", "adj_step", "diagonal_set", "high_set",
                             "scaled", "summed", "row_step", "degree_step"))
        x_done, norm_step, norm_rooted, norm_ready, h_ready, turned, kept = (
            sem(n) for n in ("x_done", "norm_step", "norm_rooted", "norm_ready", "h_ready", "turned", "kept"))
        blk = c.enter_context(nc.Block())

        @blk.sync
        def _(sp):
            sp.dma_start(v.up[:, 0, :], a["L1_gnn_W_up0"]).then_inc(v.tp_weights, 16)
            sp.dma_start(v.up[:, 1, :], a["L1_gnn_W_up1"]).then_inc(v.tp_weights, 16)
            sp.dma_start(v.w4[0:z.HID, :], a["L1_gnn_W_mlp4"]).then_inc(v.tp_weights, 16)
            sp.dma_start(v.w4[z.HID:P, :], a["L1_gnn_W_mlp4"]).then_inc(v.tp_weights, 16)
            sp.dma_start(v.wo[:, 0], a["L1_gnn_W_out0"].rearrange("(q u) n -> u q n", u=P)).then_inc(v.tp_weights, 16)
            sp.dma_start(v.wo[:, 1], a["L1_gnn_W_out1"].rearrange("(q u) n -> u q n", u=P)).then_inc(v.tp_weights, 16)

        @blk.gpsimd
        def _(pool):
            pool.memset(diagonal[:], 0.0).then_inc(diagonal_set, 1)
            pool.wait_ge(diagonal_set, 1)
            pool.tensor_copy(diagonal[:, BINS - 1, :], v.ident[:]).then_inc(diagonal_set, 1)
            root_pool(pool, v, v.dinv_gcn[:], adj_step, 2 * BINS, rooted)
            root_pool(pool, v, v.dinv_cheb[:], degree_step, 1, rooted)
            tile_roots_pool(pool, v, BINS, norm_step, norm_rooted)

        @blk.vector
        def _(dve):
            dve.wait_ge(diagonal_set, 2)
            dve.wait_ge(counts_turned, BINS)
            for t in range(BINS):
                dve.wait_ge(counts_kept, t + 1)
                dve.tensor_tensor(by_dst[:, t, :], by_dst[:, t, :], by_src[:, t, :], ALU.add).then_inc(adj_step, 1)
                dve.wait_ge(adj_step, 2 * t + 1)
                dve.scalar_tensor_tensor(adj[:, t, :], by_dst[:, t, :], 1.0,
                                         diagonal[:, BINS - 1 - t:2 * BINS - 1 - t, :].rearrange("p a n -> p (a n)"),
                                         ALU.min, ALU.add, accum_out=v.dinv_gcn[:, t:t + 1]).then_inc(adj_step, 1)
            dve.tensor_scalar(v.dinv_cheb[:], out_degree[:], 1.0, None, ALU.max).then_inc(degree_step, 1)
            dve.tensor_scalar(has_out[:], out_degree[:], 0.0, None, ALU.is_gt).then_inc(degree_step, 1)
            for t in range(BINS):
                dve.wait_ge(high_set, t + 1)
                dve.scalar_tensor_tensor(rows_low[:, t, :], h[:, t, :], v.dinv_gcn[:, t:t + 1], rows_high[:, t, :].bitcast(F32),
                                         ALU.mult, ALU.subtract).then_inc(scaled, 1)
            dve.wait_ge(rooted, 2)
            dve.wait_ge(degree_step, 2)
            dve.tensor_tensor(v.dinv_cheb[:], v.dinv_cheb[:], has_out[:], ALU.mult).then_inc(degree_step, 1)
            dve.wait_ge(degree_step, 3)
            dve.tensor_scalar(v.ndinv_cheb[:], v.dinv_cheb[:], -1.0, None, ALU.mult).then_inc(degree_step, 1)
            for t in range(BINS):
                dve.tensor_tensor(x[:, t, :], x[:, t, :], v.b_gcn[:], ALU.add).then_inc(row_step, 1)
            for t in range(BINS):
                dve.wait_ge(summed, t + 1)
                dve.wait_ge(row_step, t + 1)
                dve.scalar_tensor_tensor(x[:, t, :], ps[:, t % 4, :], v.dinv_gcn[:, t:t + 1], x[:, t, :], ALU.mult, ALU.add).then_inc(x_done, 1)
                dve.wait_ge(x_done, t + 1)
                tile_moments_dve(dve, v, x[:, t, :], t, t, norm_step)
                if t >= 1:
                    tile_shift_dve(dve, v, t - 1, t, norm_rooted, norm_ready)
            tile_shift_dve(dve, v, BINS - 1, BINS, norm_rooted, norm_ready)

        @blk.scalar
        def _(act):
            for t in range(BINS):
                act.wait_ge(counts_turned, t + 1)
                g = 2 * (t % 4)
                act.activation(by_src[:, t, :], ps[:, g:g + 2, :].rearrange("p a n -> p (a n)"), ACT.Copy,
                               accum_out=out_degree[:, t:t + 1]).then_inc(counts_kept, 1)
            for t in range(BINS):
                act.wait_ge(projected, t + 1)
                act.activation(h[:, t, :], ps[:, 4 + t % 4, :], ACT.Copy).then_inc(h_kept, 1)
            act.wait_ge(rooted, 1)
            for t in range(BINS):
                act.wait_ge(h_kept, t + 1)
                act.activation(rows_high[:, t, :], h[:, t, :], ACT.Copy, scale=v.dinv_gcn[:, t:t + 1]).then_inc(high_set, 1)
            act.wait_ge(scaled, BINS)
            for t in range(BINS + 2):
                if t < BINS:
                    tile_relu_act(act, v, h[:, t, :], t, norm_ready, h_ready)
                if t >= 2:
                    tile_keep_act(act, v, 4 + (t - 2) % 4, t - 2, t - 2, turned, kept)

        @blk.tensor
        def _(pe):
            for t in range(BINS):
                if t >= 4:
                    pe.wait_ge(counts_kept, t - 3)
                for b in range(BINS):
                    last = pe.transpose(ps[:, 2 * (t % 4) + b // 4, (b % 4) * P:(b % 4 + 1) * P], by_dst[:, b, t * P:(t + 1) * P], v.ident[:])
                last.then_inc(counts_turned, 1)
            pe.wait_ge(counts_kept, BINS)
            pe.wait_ge(v.weights_in[0], 32)
            for t in range(BINS):
                if t >= 4:
                    pe.wait_ge(h_kept, t - 3)
                for k in range(KT):
                    last = pe.matmul(ps[:, 4 + t % 4, :], hT[:, k, t * P:(t + 1) * P], v.w_gcn[:, k, :], start=(k == 0), stop=(k == KT - 1))
                last.then_inc(projected, 1)
            pe.wait_ge(adj_step, 2 * BINS)
            pe.wait_ge(h_kept, BINS)
            for t in range(BINS + 2):
                if t < BINS:
                    if t >= 4:
                        pe.wait_ge(x_done, t - 3)
                    for m in range(BINS):
                        if t == 0:
                            pe.wait_ge(scaled, m + 1)
                        pe.matmul(ps[:, t % 4, :], adj[:, m, t * P:(t + 1) * P], rows_high[:, m, :], start=(m == 0), stop=False)
                        last = pe.matmul(ps[:, t % 4, :], adj[:, m, t * P:(t + 1) * P], rows_low[:, m, :], start=False, stop=(m == BINS - 1))
                    last.then_inc(summed, 1)
                if t >= 2:
                    n = t - 2
                    if n >= 4:
                        pe.wait_ge(kept, n - 3)
                    tile_turn_pe(pe, v, [h[:, n, 0:P]] + [h[:, n, P + m:z.D:3] for m in range(3)], 4 + n % 4, n, h_ready, turned)


def tensor_product_block(nc, a, v):
    z, BINS, KT, N, D, PAIRS, ROW, HID = v.z, v.BINS, v.KT, v.N, v.D, v.PAIRS, v.ROW, v.HID
    RING = 4
    Y = range(4)
    acc = v.by_dst
    x, h, hT, ps = v.x, v.h, v.hT, v.ps
    with nc.cleanup_on_exit(), ExitStack() as c0:
        def sb0(name, shape, dt=F32):
            return c0.enter_context(nc.sbuf_tensor(name, shape, dt))

        def sem0(name):
            return nc.alloc_semaphore(name="sum_" + name)
        up, w4, wo = v.up, v.w4, v.wo
        w4_parts = sb0("w_mlp4_parts", [P, 2, D], F32R)
        w_step, w_scaled = sem0("w_step"), sem0("w_scaled")

        with nc.cleanup_on_exit(), ExitStack() as c:
            def sem(name):
                return nc.alloc_semaphore(name="sum_" + name)
            projected, staged, table_out = (sem(n) for n in ("tp_projected", "tp_staged", "table_out"))
            blk = c.enter_context(nc.Block())

            @blk.sync
            def _(sp):
                for t in range(BINS):
                    sp.wait_ge(staged, t + 1)
                    sp.dma_start(v.up_table[t * P:(t + 1) * P, :], h[:, t, :]).then_inc(table_out, 16)
                sp.wait_ge(table_out, 16 * BINS)

            @blk.vector
            def _(dve):
                for t in range(BINS):
                    dve.wait_ge(projected, t + 1)
                    dve.tensor_scalar(h[:, t, :], ps[:, t, :], P ** -0.5, None, ALU.mult).then_inc(staged, 1)

            @blk.gpsimd
            def _(pool):
                pool.memset(acc[:], 0.0).then_inc(w_step, 1)
                pool.wait_ge(w_scaled, 2)
                pool.tensor_copy(w4_parts[:, 0, :], w4[:]).then_inc(w_scaled, 1)
                pool.wait_ge(w_scaled, 3)
                pool.tensor_tensor(w4_parts[:, 1, :], w4[:], w4_parts[:, 0, :].bitcast(F32), ALU.subtract).then_inc(w_step, 1)

            @blk.scalar
            def _(act):
                act.wait_ge(v.tp_weights, 96)
                c4 = SILU_2MOM * HID ** -0.5
                co = (2 * P) ** -0.5 / AVG_NEIGHBORS
                act.activation(w4[:, 0:3 * P], w4[:, 0:3 * P], ACT.Copy, scale=c4).then_inc(w_scaled, 1)
                act.activation(w4[:, 3 * P:], w4[:, 3 * P:], ACT.Copy, scale=c4 * 3.0 ** -0.5).then_inc(w_scaled, 1)
                act.activation(wo[:].rearrange("p a q n -> p (a q n)"), wo[:].rearrange("p a q n -> p (a q n)"), ACT.Copy, scale=co).then_inc(w_step, 1)

            @blk.tensor
            def _(pe):
                pe.wait_ge(v.tp_weights, 96)
                for t in range(BINS):
                    for k in range(4):
                        last = pe.matmul(ps[:, t, k * P:(k + 1) * P], hT[:, k, t * P:(t + 1) * P], up[:, min(k, 1), :], start=True, stop=True)
                    last.then_inc(projected, 1)

        with nc.cleanup_on_exit(), ExitStack() as c:
            def sb(name, shape, dt=F32):
                return c.enter_context(nc.sbuf_tensor(name, shape, dt))

            def sem(name):
                return nc.alloc_semaphore(name="sum_" + name)
            G = hT[:].rearrange("p k n -> p (k n)").rearrange("p (r q d) -> p r q d", r=RING, q=2)
            slot = [sb(f"slot{r}", [P, 2, ROW]) for r in range(RING)]
            nodes = [sb(f"nodes{r}", [P, 2], I32) for r in range(RING)]
            zero2 = sb("zero2", [P, 2], I32)
            hidT = [sb(f"hidT{b}", [P, 2, P], F32R) for b in range(2)]
            hot = [sb(f"hot{r}", [P, 2, P]) for r in range(RING)]
            hot_y = [sb(f"hot_y{b}", [P, 2, 4, P]) for b in range(2)]
            vector_y = [sb(f"vector_y{b}", [P, 2, 3, P]) for b in range(2)]
            dots = [sb(f"dots{b}", [P, 2, P]) for b in range(2)]
            msg = [sb(f"msg{b}", [P, 2, 6, P]) for b in range(2)]
            slot_in = [sem(f"slot_in{r}") for r in range(RING)]
            rows_in = [sem(f"rows_in{r}") for r in range(RING)]
            (index_set, pool_set, hid_turned, hid_kept, weighted, hot_set, hot_scaled, dot_step, vector_scaled, msg_done, summed, added,
             mixed, x_step) = (sem(n) for n in (
                 "index_set", "pool_set", "hid_turned", "hid_kept", "weighted", "hot_set", "hot_scaled", "dot_step", "vector_scaled",
                 "msg_done", "summed", "added", "mixed", "x_step"))
            norm_step, norm_rooted, norm_ready, h_ready, turned, kept = (
                sem(n) for n in ("norm_step", "norm_rooted", "norm_ready", "h_ready", "turned", "kept"))
            STEPS = PAIRS // RING
            LAST = STEPS - 1
            AHEAD = 2
            blk = c.enter_context(nc.Block())
            path_banks = lambda b: ps[:, 2 * b:2 * b + 2, :]
            acc_banks = lambda b: ps[:, 4 + 2 * b:6 + 2 * b, :]

            def over_pairs(engine, pair):
                with engine.Fori(0, LAST) as i:
                    for r in range(RING):
                        pair(i, r, True)
                for r in range(RING):
                    pair(LAST, r, r + AHEAD < RING)

            def lap(i, r, ahead):
                return (r + ahead) % RING, i + (r + ahead) // RING

            @blk.sync
            def _(sp):
                view = v.slots.rearrange("(s q p) r -> s p q r", q=2, p=P)

                def load(r, pair):
                    sp.dma_start(slot[r][:], pair).then_inc(slot_in[r], 16)

                for r in range(RING):
                    load(r, view[r])
                with sp.Fori(0, LAST) as i:
                    for r in range(RING):
                        sp.wait_ge(msg_done, RING * i + r + 1 + AHEAD)
                        sp.wait_ge(hot_scaled, RING * i + r + 1 + AHEAD)
                        load(r, view[bass.ds((i + 1) * RING + r, 1)].rearrange("a p q r -> p (a q) r"))
                for n, name in enumerate(("L2_gnn_W1_0", "L2_gnn_W1_1", "L2_gnn_W2_0", "L2_gnn_W2_1")):
                    sp.dma_start(v.weights[:, n], a[name].rearrange("(k p) n -> p k n", p=P)).then_inc(v.weights_in[n], 16)

            @blk.gpsimd
            def _(pool):
                pool.memset(zero2[:], 0).then_inc(pool_set, 1)
                pool.wait_ge(pool_set, 1)

                def gather(r, laps):
                    pool.wait_ge(slot_in[r], 16 * laps + 16)
                    pool.tensor_tensor(nodes[r][:], slot[r][:, :, 0].bitcast(I32), zero2[:], ALU.add).then_inc(index_set, 1)
                    pool.wait_ge(index_set, 1)
                    for q in range(2):
                        pool.indirect_dma_start(out=G[:, r, q, :], out_offset=None, in_=v.up_table,
                                                in_offset=bass.IndirectOffsetOnAxis(ap=nodes[r][:, q:q + 1], axis=0)).then_inc(rows_in[r], 16)

                def pair(i, r, ahead):
                    pool.sem_clear(index_set)
                    pool.wait_ge(msg_done, RING * i + r + 1)
                    if ahead:
                        gather(*lap(i, r, AHEAD))
                    pool.wait_ge(rows_in[r], 32 * i + 32)
                    pool.tensor_tensor(vector_y[r % 2][:], G[:, r, :, P:4 * P].rearrange("p q (m n) -> p q m n", n=P),
                                       slot[r][:, :, 5:8].unsqueeze(3).to_broadcast([P, 2, 3, P]), ALU.mult).then_inc(vector_scaled, 1)

                for n in range(AHEAD):
                    pool.sem_clear(index_set)
                    gather(n, 0)
                over_pairs(pool, pair)
                tile_roots_pool(pool, v, BINS, norm_step, norm_rooted)

            @blk.vector
            def _(dve):
                bins = [dve.alloc_register(f"sum_bin{k}") for k in range(RING)]

                def one_hots(r):
                    for q in range(2):
                        last = dve.tensor_scalar(hot[r][:, q, :], v.iota1[:], slot[r][:, q, 1:2], None, ALU.is_equal)
                    last.then_inc(hot_set, 1)

                def load_bins(i):
                    dve.load(bins, v.tile_bin[0:1, bass.ds(i * RING, RING)])
                    return [dve.snap(reg, min_val=0, max_val=BINS - 1) for reg in bins]

                def pair(i, r, last_bin, more):
                    b, n = r % 2, RING * i + r
                    m, rows, w = msg[b], G[:, r, :, :], path_banks(b)
                    dve.wait_ge(vector_scaled, n + 1)
                    if more:
                        one_hots((r + 1) % RING)
                    dve.tensor_tensor(dots[b][:], vector_y[b][:, :, 0, :], vector_y[b][:, :, 1, :], ALU.add).then_inc(dot_step, 1)
                    dve.wait_ge(weighted, n + 1)
                    dve.tensor_tensor(m[:, :, 0:6:5, :], w[:, :, 0:2 * P].rearrange("p q (a n) -> p q a n", n=P),
                                      rows[:, :, 0:P].unsqueeze(2).to_broadcast([P, 2, 2, P]), ALU.mult)
                    dve.wait_ge(dot_step, 2 * n + 1)
                    dve.tensor_tensor(dots[b][:], dots[b][:], vector_y[b][:, :, 2, :], ALU.add).then_inc(dot_step, 1)
                    dve.tensor_tensor(m[:, :, 1:4, :], w[:, :, 2 * P:3 * P].unsqueeze(2).to_broadcast([P, 2, 3, P]),
                                      rows[:, :, P:4 * P].rearrange("p q (a n) -> p q a n", n=P), ALU.mult)
                    dve.wait_ge(dot_step, 2 * n + 2)
                    dve.tensor_tensor(m[:, :, 4, :], w[:, :, 3 * P:4 * P], dots[b][:], ALU.mult).then_inc(msg_done, 1)
                    add_sums(n, last_bin, 1 - b)

                def add_sums(n, last_bin, b):
                    dve.wait_ge(summed, n + 2)
                    dve.wait_ge(added, n + 1)
                    dst = acc[:, bass.ds(last_bin, 1), :]
                    dve.tensor_tensor(dst, dst, acc_banks(b).rearrange("p a n -> p (a n)").unsqueeze(1), ALU.add).then_inc(added, 1)

                dve.sem_inc(msg_done, AHEAD)
                dve.sem_inc(added, 1)
                dve.wait_ge(slot_in[0], 16)
                one_hots(0)
                with dve.Fori(0, LAST) as i:
                    at = load_bins(i)
                    for r in range(RING):
                        pair(i, r, at[r], True)
                at = load_bins(LAST)
                for r in range(RING):
                    pair(LAST, r, at[r], r < RING - 1)
                last_bin = dve.value_load(v.tile_bin[0:1, PAIRS:PAIRS + 1], min_val=0, max_val=BINS - 1)
                add_sums(PAIRS, last_bin, 1)
                for t in range(BINS):
                    xr = x[:, t, :]
                    dve.wait_ge(mixed, t + 1)
                    dve.tensor_tensor(xr[:, 0:P], xr[:, 0:P], ps[:, 4 + t % 4, 0:P], ALU.add).then_inc(x_step, 1)
                    xm = xr[:, P:D].rearrange("p (n m) -> p m n", m=3)
                    dve.tensor_tensor(xm, xm, ps[:, 4 + t % 4, P:D].rearrange("p (m n) -> p m n", m=3), ALU.add).then_inc(x_step, 1)
                    dve.wait_ge(x_step, 2 * t + 2)
                    tile_moments_dve(dve, v, xr, t, t, norm_step)
                    if t >= 1:
                        tile_shift_dve(dve, v, t - 1, t, norm_rooted, norm_ready)
                tile_shift_dve(dve, v, BINS - 1, BINS, norm_rooted, norm_ready)

            @blk.scalar
            def _(act):
                def keep_hidden(b, n):
                    act.wait_ge(hid_turned, n + 1)
                    act.activation(hidT[b][:].rearrange("p q e -> p (q e)"), path_banks(b)[:, 0, 0:2 * P], ACT.Copy).then_inc(hid_kept, 1)

                def pair(i, r, ahead):
                    b, n = r % 2, RING * i + r
                    act.wait_ge(hot_set, n + 1)
                    act.wait_ge(summed, n + 1)
                    for q in range(2):
                        for m in Y:
                            last = act.activation(hot_y[b][:, q, m, :], hot[r][:, q, :], ACT.Copy, scale=slot[r][:, q, 4 + m:5 + m])
                    last.then_inc(hot_scaled, 1)
                    if ahead:
                        keep_hidden(b, n + AHEAD)

                for n in range(AHEAD):
                    keep_hidden(n, n)
                act.sem_inc(hot_scaled, AHEAD)
                over_pairs(act, pair)
                for t in range(BINS + 2):
                    if t < BINS:
                        tile_relu_act(act, v, h[:, t, :], t, norm_ready, h_ready)
                    if t >= 2:
                        tile_keep_act(act, v, (t - 2) % 4, t - 2, t - 2, turned, kept)

            def mix(pe, t):
                f = acc[:, t, :].rearrange("p (k n) -> p k n", n=P)
                if t >= 4:
                    pe.wait_ge(x_step, 2 * (t - 3))
                o = ps[:, 4 + t % 4, :]
                pe.matmul(o[:, 0:P], f[:, 0, :], wo[:, 0, 0, :], start=True, stop=False, skip_group_check=True)
                last = pe.matmul(o[:, 0:P], f[:, 4, :], wo[:, 0, 1, :], start=False, stop=True, skip_group_check=True)
                for m in range(3):
                    pe.matmul(o[:, (m + 1) * P:(m + 2) * P], f[:, 5 + m, :], wo[:, 1, 0, :], start=False, stop=False, skip_group_check=True)
                    last = pe.matmul(o[:, (m + 1) * P:(m + 2) * P], f[:, 1 + m, :], wo[:, 1, 1, :], start=False, stop=True, skip_group_check=True)
                last.then_inc(mixed, 1)

            @blk.tensor
            def _(pe):
                def turn_hidden(r, laps):
                    pe.wait_ge(slot_in[r], 16 * laps + 16)
                    for q in range(2):
                        last = pe.transpose(path_banks(r % 2)[:, 0, q * P:(q + 1) * P], slot[r][:, q, 8:ROW], v.ident[:])
                    last.then_inc(hid_turned, 1)

                def path_weights(b, n):
                    pe.wait_ge(hid_kept, n + 1)
                    for q in range(2):
                        pe.matmul(path_banks(b)[:, q, :], hidT[b][:, q, :], w4_parts[:, 0, :], start=True, stop=False)
                        last = pe.matmul(path_banks(b)[:, q, :], hidT[b][:, q, :], w4_parts[:, 1, :], start=False, stop=True)
                    last.then_inc(weighted, 1)

                def pair(i, r, ahead):
                    b, n = r % 2, RING * i + r
                    pe.wait_ge(msg_done, n + 1 + AHEAD)
                    if ahead:
                        turn_hidden(*lap(i, r, AHEAD))
                    pe.wait_ge(hot_scaled, n + 1 + AHEAD)
                    A, B = acc_banks(b)[:, 0, :], acc_banks(b)[:, 1, :]
                    for q in range(2):
                        m, hy, first, lastq = msg[b][:, q], hot_y[b][:, q], q == 0, q == 1
                        for k in range(4):
                            pe.matmul(A[:, k * P:(k + 1) * P], m[:, k, :], hy[:, 0, :], start=first and k == 0, stop=lastq, skip_group_check=True)
                        pe.matmul(B[:, 0:P], m[:, 4, :], hot[r][:, q, :], start=first, stop=lastq, skip_group_check=True)
                        last = pe.matmul(B[:, P:4 * P], m[:, 5, :], hy[:, 1:4, :], start=False, stop=lastq, skip_group_check=True)
                    last.then_inc(summed, 1)
                    if ahead:
                        path_weights(b, n + AHEAD)

                pe.wait_ge(w_step, 3)
                pe.sem_inc(summed, 1)
                for j in range(2):
                    last = pe.matmul(ps[:, 6 + j, :], acc[:, 0, 0:P], acc[:, 0, 0:D], start=True, stop=True)
                last.then_inc(summed, 1)
                for n in range(AHEAD):
                    turn_hidden(n, 0)
                for n in range(AHEAD):
                    path_weights(n, n)
                over_pairs(pe, pair)
                pe.wait_ge(added, PAIRS + 2)
                for t in range(BINS + 2):
                    if t < BINS:
                        mix(pe, t)
                    if t >= 2:
                        n = t - 2
                        if n >= 4:
                            pe.wait_ge(kept, n - 3)
                        tile_turn_pe(pe, v, [h[:, n, k * P:(k + 1) * P] for k in range(KT)], n % 4, n, h_ready, turned)


def cheb_block(nc, a, v):
    z, BINS, KT, N, D = v.z, v.BINS, v.KT, v.N, v.D
    x, h, hT, ps, by_src = v.x, v.h, v.hT, v.ps, v.by_src
    r = v.by_dst[:, :, 0:D]
    with nc.cleanup_on_exit(), ExitStack() as c:
        def sem(name):
            return nc.alloc_semaphore(name="cheb_" + name)
        affine = c.enter_context(nc.sbuf_tensor("affine", [P, 4, D], F32))
        (norm_step, rooted, norm_ready, rows_ready, turned, kept, projected, scaled, summed, row_step, affine_in, affine_step, bias_added) = (
            sem(n) for n in ("norm_step", "rooted", "norm_ready", "rows_ready", "turned", "kept", "projected", "scaled", "summed",
                             "row_step", "affine_in", "affine_step", "bias_added"))
        blk = c.enter_context(nc.Block())

        @blk.sync
        def _(sp):
            for k, name in enumerate(("L2_gnn_b1", "L2_gnn_b2", "L2_gnn_gamma", "L2_gnn_beta")):
                sp.dma_start(affine[:, k, :], broadcast_rows(a[name], D)).then_inc(affine_in, 16)
            sp.wait_ge(affine_in, 64)
            load_relational(sp, a, v, 0)
            load_loop(sp, a, v, 0)

        @blk.gpsimd
        def _(pool):
            tile_roots_pool(pool, v, 2 * BINS, norm_step, rooted)

        @blk.vector
        def _(dve):
            dve.wait_ge(affine_in, 64)
            for t in range(BINS):
                dve.tensor_tensor(x[:, t, :], x[:, t, :], affine[:, 1, :], ALU.add).then_inc(bias_added, 1)
            for conv in range(2):
                for t in range(BINS):
                    u = conv * BINS + t
                    dve.wait_ge(summed, u + 1)
                    own, far = ps[:, 2 * (t % 2), :], ps[:, 2 * (t % 2) + 1, :]
                    row = r[:, t, :] if conv == 0 else x[:, t, :]
                    if conv == 1:
                        dve.wait_ge(bias_added, t + 1)
                    dve.scalar_tensor_tensor(row, far, v.ndinv_cheb[:, t:t + 1], affine[:, 0, :] if conv == 0 else row, ALU.mult, ALU.add).then_inc(row_step, 1)
                    dve.wait_ge(row_step, 2 * u + 1)
                    dve.tensor_tensor(row, row, own, ALU.add).then_inc(row_step, 1)
                    dve.wait_ge(row_step, 2 * u + 2)
                    tile_moments_dve(dve, v, row, t, u, norm_step)
                    if conv == 1:
                        tile_shift_dve(dve, v, t, u + 1, rooted, norm_ready)
                    else:
                        dve.wait_ge(rooted, u + 1)
                        dve.tensor_scalar(row, row, v.moments[:, t, 0:1], v.rstd[:, t:t + 1], ALU.subtract, ALU.mult).then_inc(affine_step, 1)
                        dve.wait_ge(affine_step, 3 * t + 1)
                        dve.tensor_tensor(row, row, affine[:, 2, :], ALU.mult).then_inc(affine_step, 1)
                        dve.wait_ge(affine_step, 3 * t + 2)
                        dve.tensor_tensor(row, row, affine[:, 3, :], ALU.add).then_inc(affine_step, 1)
                        dve.wait_ge(affine_step, 3 * t + 3)
                        dve.scalar_tensor_tensor(row, row, LEAK, row, ALU.mult, ALU.max).then_inc(rows_ready, 1)

        @blk.scalar
        def _(act):
            for conv in range(2):
                for t in range(BINS):
                    act.wait_ge(projected, conv * BINS + t + 1)
                    act.activation(h[:, t, :], ps[:, t % 4, :], ACT.Copy, scale=v.dinv_cheb[:, t:t + 1]).then_inc(scaled, 1)
                for t in range(BINS + 1):
                    if conv == 1 and t < BINS:
                        tile_relu_act(act, v, r[:, t, :], t, norm_ready, rows_ready)
                    if t >= 1:
                        tile_keep_act(act, v, 4 + (t - 1) % 4, t - 1, conv * BINS + t - 1, turned, kept)

        @blk.tensor
        def _(pe):
            for conv in range(2):
                base = conv * BINS
                if conv == 1:
                    pe.wait_ge(row_step, 2 * BINS)
                pe.wait_ge(v.weights_in[2 * conv + 1], 16)
                for t in range(BINS):
                    if conv == 1:
                        pe.wait_ge(kept, t + 1)
                    if t >= 4:
                        pe.wait_ge(scaled, base + t - 3)
                    for k in range(KT):
                        last = pe.matmul(ps[:, t % 4, :], hT[:, k, t * P:(t + 1) * P], v.weights[:, 2 * conv + 1, k, :], start=(k == 0), stop=(k == KT - 1))
                    last.then_inc(projected, 1)
                pe.wait_ge(v.weights_in[2 * conv], 32 if conv == 0 else 16)
                pe.wait_ge(scaled, base + BINS)
                for t in range(BINS + 1):
                    if t < BINS:
                        if t >= 2:
                            pe.wait_ge(row_step, 2 * (base + t - 1))
                        g = 2 * (t % 2)
                        for k in range(KT):
                            pe.matmul(ps[:, g, :], hT[:, k, t * P:(t + 1) * P], v.weights[:, 2 * conv, k, :], start=(k == 0), stop=(k == KT - 1))
                        for m in range(BINS):
                            last = pe.matmul(ps[:, g + 1, :], by_src[:, m, t * P:(t + 1) * P], h[:, m, :], start=(m == 0), stop=(m == BINS - 1))
                        last.then_inc(summed, 1)
                    if t >= 1:
                        n = base + t - 1
                        if n >= 4:
                            pe.wait_ge(kept, n - 3)
                        tile_turn_pe(pe, v, [r[:, t - 1, k * P:(k + 1) * P] for k in range(KT)], 4 + (t - 1) % 4, n, rows_ready, turned)


def relational_block(nc, a, v, out):
    row_no = v.meta[:].bitcast(I32)[:, :, 3]
    with nc.cleanup_on_exit(), ExitStack() as c0:
        ones_row = c0.enter_context(nc.sbuf_tensor("ones_row", [1, P], F32))
        for layer in range(2):
            with nc.cleanup_on_exit(), ExitStack() as c:
                relational_layer(nc, a, v, out, layer, c, row_no, ones_row)


def relational_layer(nc, a, v, out, layer, c, row_no, ones_row):
    z, BINS, KT, N, D, TILES = v.z, v.BINS, v.KT, v.N, v.D, v.TILES
    RELS, BASES = z.RELS, z.BASES
    x, h, hT, ps = v.x, v.h, v.hT, v.ps
    basis, loop_w, comp, bias = v.basis[layer], v.loop_w, v.comp, v.rel_bias
    SET = 4
    RING = 2 * SET
    STEPS = TILES // RING
    DVE_RELS = 6
    POOL_RELS = RELS - DVE_RELS
    PART = DVE_RELS // 2
    DVE_TERMS = DVE_RELS * (BASES - 1)
    POOL_TERMS = POOL_RELS * (BASES - 1)
    ACT_TERMS = DVE_RELS + POOL_RELS * BASES

    def sb(name, shape, dt=F32):
        return c.enter_context(nc.sbuf_tensor(f"{name}_{layer}", shape, dt))

    def sem(name):
        return nc.alloc_semaphore(name=f"rel{layer}_{name}")
    stage = v.by_dst[:].rearrange("p a n -> p (a n)").rearrange("p (b r d) -> p b r d", b=2, r=RELS)
    rows_room = v.by_src[:].rearrange("p a n -> p (a n)").rearrange("p (g d) -> p g d", d=D)
    terms = rows_room[:, 0:2 * POOL_TERMS, :].rearrange("p (b r k) d -> p b r k d", b=2, r=POOL_RELS)
    G = rows_room[:, 0:RING, :]
    table = v.rel_table[layer]
    table_rows = table.rearrange("(r t p) d -> t p r d", r=RELS, p=P)
    nodes = [sb(f"nodes{b}", [P, SET], I32) for b in range(2)]
    hot = [sb(f"hot{r}", [P, P]) for r in range(RING)]
    rows_in = [sem(f"rows_in{r}") for r in range(RING)]
    table_out = [sem(f"table_out{b}") for b in range(2)]
    (turned, kept, based, act_term, dve_mix, pool_mix, index_set, hot_set, tile_summed,
     row_step, out_done, bias_added, ones_set) = (sem(n) for n in (
         "turned", "kept", "based", "act_term", "dve_mix", "pool_mix", "index_set",
         "hot_set", "tile_summed", "row_step", "out_done", "bias_added", "ones_set"))
    blk = c.enter_context(nc.Block())

    @blk.sync
    def _(sp):
        if layer == 0:
            load_relational(sp, a, v, 1)
        else:
            load_loop(sp, a, v, 1)
        for t in range(BINS):
            sp.wait_ge(dve_mix, DVE_TERMS * t + (DVE_TERMS if t < BINS - 1 else DVE_TERMS // 2))
            sp.dma_start(table_rows[t][:, 0:PART], stage[:, t % 2, 0:PART]).then_inc(table_out[t % 2], 16)
            sp.wait_ge(dve_mix, DVE_TERMS * (t + 1))
            sp.wait_ge(pool_mix, POOL_TERMS * (t + 1))
            sp.dma_start(table_rows[t][:, PART:], stage[:, t % 2, PART:]).then_inc(table_out[t % 2], 16)
        if layer == 1:
            for t in range(BINS):
                sp.wait_ge(row_step, t + 1)
                sp.dma_start(out[t * P:(t + 1) * P, :], x[:, t, :]).then_inc(out_done, 16)
            sp.wait_ge(out_done, 16 * BINS)

    @blk.gpsimd
    def _(pool):
        if layer == 0:
            pool.memset(ones_row[:], 1.0).then_inc(ones_set, 1)
        for t in range(BINS):
            for b in range(1, BASES):
                for rel in range(POOL_RELS):
                    if b == 1:
                        pool.wait_ge(act_term, ACT_TERMS * t + POOL_TERMS + DVE_RELS + rel + 1)
                    else:
                        pool.wait_ge(pool_mix, POOL_TERMS * t + POOL_RELS * (b - 2) + rel + 1)
                    row = stage[:, t % 2, DVE_RELS + rel, :]
                    pool.tensor_tensor(row, row, terms[:, t % 2, rel, b - 1, :], ALU.add).then_inc(pool_mix, 1)
        for b in range(2):
            pool.wait_ge(table_out[b], 32 * BINS // 2)
        pool.wait_ge(pool_mix, POOL_TERMS * BINS)
        with pool.Fori(0, STEPS) as i:
            for b in range(2):
                pool.sem_clear(index_set)
                pool.wait_ge(tile_summed, i * RING + (b + 1) * SET)
                pool.tensor_copy(nodes[b][:], row_no[:, bass.ds(i * RING + b * SET, SET)]).then_inc(index_set, 1)
                pool.wait_ge(index_set, 1)
                for k in range(SET):
                    pool.indirect_dma_start(out=G[:, b * SET + k, :], out_offset=None, in_=table,
                                            in_offset=bass.IndirectOffsetOnAxis(ap=nodes[b][:, k:k + 1], axis=0)).then_inc(rows_in[b * SET + k], 16)

    @blk.vector
    def _(dve):
        for t in range(BINS if layer == 1 else 0):
            dve.wait_ge(turned, t + 1)
            dve.tensor_copy(hT[:, :, t * P:(t + 1) * P], ps[:, t % 4, :].rearrange("p (k n) -> p k n", n=P)).then_inc(kept, 1)
        for t in range(BINS):
            parts = 1 if t < BINS - 1 else 2
            size = DVE_RELS // parts
            for part in range(parts):
                before = DVE_TERMS * t + part * DVE_TERMS // parts
                for b in range(1, BASES):
                    for n in range(size):
                        rel = size * part + n
                        if b == 1:
                            dve.wait_ge(act_term, ACT_TERMS * t + POOL_TERMS + rel + 1)
                        else:
                            dve.wait_ge(dve_mix, before + size * (b - 2) + n + 1)
                        row = stage[:, t % 2, rel, :]
                        k = rel * BASES + b
                        dve.scalar_tensor_tensor(row, ps[:, 4 * (t % 2) + b, :], comp[:, layer, k:k + 1], row, ALU.mult, ALU.add).then_inc(dve_mix, 1)
        if layer == 1:
            for t in range(BINS):
                dve.tensor_tensor(x[:, t, :], x[:, t, :], bias[:, layer, :], ALU.add).then_inc(bias_added, 1)
        with dve.Fori(0, STEPS) as i:
            for r in range(RING):
                dve.wait_ge(tile_summed, i * RING + r + 1)
                t = bass.ds(i * RING + r, 1)
                dve.tensor_scalar(hot[r][:], v.iota1[:], v.meta[:, t, 1:2].rearrange("p a b -> p (a b)"),
                                  v.meta[:, t, 2:3].rearrange("p a b -> p (a b)"), ALU.is_equal, ALU.mult).then_inc(hot_set, 1)
        dve.wait_ge(tile_summed, TILES + RING)
        if layer == 0:
            for t in range(0, BINS, 2):
                dve.tensor_scalar(h[:, t, :], ps[:, t, :], 0.0, None, ALU.max).then_inc(row_step, 1)
        else:
            dve.wait_ge(bias_added, BINS)
            for t in range(BINS):
                dve.tensor_tensor(x[:, t, :], ps[:, t, :], x[:, t, :], ALU.add).then_inc(row_step, 1)

    @blk.scalar
    def _(act):
        act.wait_ge(v.relational_in[layer], 16 * (BASES + 2))
        for t in range(BINS):
            act.wait_ge(based, t + 1)
            if t >= 2:
                act.wait_ge(pool_mix, POOL_TERMS * (t - 1))
            for b in range(1, BASES):
                for rel in range(DVE_RELS, RELS):
                    k = rel * BASES + b
                    act.activation(terms[:, t % 2, rel - DVE_RELS, b - 1, :], ps[:, 4 * (t % 2) + b, :], ACT.Copy,
                                   scale=comp[:, layer, k:k + 1]).then_inc(act_term, 1)
            if t >= 2:
                act.wait_ge(table_out[t % 2], 32 * (t // 2))
            for rel in range(RELS):
                k = rel * BASES
                act.activation(stage[:, t % 2, rel, :], ps[:, 4 * (t % 2), :], ACT.Copy, scale=comp[:, layer, k:k + 1]).then_inc(act_term, 1)
        if layer == 0:
            act.wait_ge(tile_summed, TILES + RING)
            for t in range(1, BINS, 2):
                act.activation(h[:, t, :], ps[:, t, :], ACT.Relu).then_inc(row_step, 1)

    @blk.tensor
    def _(pe):
        bins = [pe.alloc_register(f"rel{layer}_bin{k}") for k in range(RING // 2)]
        for t in range(BINS if layer == 1 else 0):
            if t >= 4:
                pe.wait_ge(kept, t - 3)
            for k in range(KT):
                last = pe.transpose(ps[:, t % 4, k * P:(k + 1) * P], h[:, t, k * P:(k + 1) * P], v.ident[:])
            last.then_inc(turned, 1)
        pe.wait_ge(v.relational_in[layer], 16 * (BASES + 2))
        if layer == 1:
            pe.wait_ge(kept, BINS)
        for t in range(BINS):
            for b in range(BASES):
                if t >= 2 and b == 0:
                    pe.wait_ge(act_term, ACT_TERMS * (t - 1))
                elif t >= 2:
                    pe.wait_ge(dve_mix, DVE_TERMS * (t - 2) + DVE_RELS * b)
                for k in range(KT):
                    last = pe.matmul(ps[:, 4 * (t % 2) + b, :], hT[:, k, t * P:(t + 1) * P], basis[:, b, k, :], start=(k == 0), stop=(k == KT - 1))
            last.then_inc(based, 1)
        pe.sem_inc(tile_summed, RING)
        if layer == 0:
            pe.wait_ge(ones_set, 1)
        pe.wait_ge(v.loop_in, 16 * (layer + 1))
        EARLY = BINS // 2

        def own_row(t, ks):
            for k in ks:
                pe.matmul(ps[:, t, :], hT[:, k, t * P:(t + 1) * P], loop_w[:, k, :], start=(k == 0), stop=False, skip_group_check=True)

        for t in range(BINS):
            if t in (0, EARLY):
                last_tile = BINS - 2 + t // EARLY
                pe.wait_ge(dve_mix, DVE_TERMS * (last_tile + 1))
                pe.wait_ge(act_term, ACT_TERMS * (last_tile + 1))
            own_row(t, range(KT if t < EARLY else 1))
            if layer == 0:
                pe.matmul(ps[:, t, :], ones_row[:], bias[0:1, layer, :], start=False, stop=False, skip_group_check=True)

        def sum_gathered(first, end):
            with pe.Fori(first, end) as i:
                pe.load(bins, v.tile_bin[0:1, bass.ds(i * (RING // 2) + 1, RING // 2)])
                at = [pe.snap(reg, min_val=0, max_val=BINS - 1) for reg in bins]
                for r in range(RING):
                    pe.wait_ge(hot_set, i * RING + r + 1)
                    pe.wait_ge(rows_in[r], 16 * i + 16)
                    pe.matmul(ps[:, bass.ds(at[r // 2], 1), :], hot[r][:], G[:, r, :], start=False, stop=False, skip_group_check=True).then_inc(tile_summed, 1)

        for t in range(EARLY, BINS):
            own_row(t, range(1, KT))
            sum_gathered(2 * (t - EARLY), 2 * (t - EARLY + 1))
        sum_gathered(2 * (BINS - EARLY), STEPS)


def kernel(**inputs):
    import numpy as np
    import concourse.bacc as bacc
    from concourse.bass_utils import run_bass_kernel_spmd as run

    nc = bacc.Bacc("TRN2", target_bir_lowering=False, num_devices=1)
    arrays, aps = {}, {}
    for name, value in inputs.items():
        arr = np.ascontiguousarray(value)
        arrays[f"in_{name}"] = arr
        aps[name] = nc.dram_tensor(f"in_{name}", arr.shape, mybir.dt.from_np(arr.dtype), kind="ExternalInput").ap()
    out = nc.dram_tensor("out", inputs["x"].shape, F32, kind="ExternalOutput").ap()
    build_program(nc, aps, out)
    return run(nc, [arrays], core_ids=[0]).results[0]["out"]
```
